# Optimizing a Trainium2 kernel written in Bass

```python
import numpy as np
import jax
import jax.numpy as jnp

def _softmax(x, axis=-1):
    return jax.nn.softmax(x, axis=axis)

def _gelu(x):
    return jax.nn.gelu(x, approximate=True)

def _silu(x):
    return jax.nn.silu(x)

def _sigmoid(x):
    return jax.nn.sigmoid(x)

def _layernorm(x, axis=-1, eps=1e-05):
    m = jnp.mean(x, axis=axis, keepdims=True)
    v = jnp.var(x, axis=axis, keepdims=True)
    return (x - m) / jnp.sqrt(v + eps)

def _scatter_add(tgt, idx, src, axis=0):
    return tgt.at[idx].add(src)

def _segment_sum(src, seg, n):
    return jax.ops.segment_sum(src, seg, n)
kernel_name = 'mk_xattn_seq_d4_seqx_r8_d3ba6f'

def setup_inputs(seed: int=0):
    np.random.seed(seed)
    _w = jnp.asarray

    def _rec_inputs():
        import jax
        import jax.numpy as jnp
        _rk = jax.random.key(seed)
        x = -0.0002928 + 1 * jax.random.normal(jax.random.fold_in(_rk, 1), (32, 64, 256), jnp.float32)
        _lenS = 64 - jax.random.randint(jax.random.fold_in(_rk, 7), (32,), 0, max(1, 64 // 4) + 1, jnp.int32)
        _lenS2 = 64 - jax.random.randint(jax.random.fold_in(_rk, 8), (32,), 0, max(1, 64 // 4) + 1, jnp.int32)
        _ctx_2048P = jax.random.normal(jax.random.fold_in(_rk, 11), (32, 16, 256), jnp.float32)
        _ctx_2048c = jax.random.dirichlet(jax.random.fold_in(_rk, 511), 0.3 * jnp.ones((16,), jnp.float32), (32, 64))
        _ctx_2048t = jnp.einsum('bsk,bkd->bsd', _ctx_2048c, _ctx_2048P)
        _ctx_2048t = _ctx_2048t * jax.lax.rsqrt(jnp.mean(jnp.square(_ctx_2048t)) + 1e-12) * 0.953939
        ctx_2048 = -1.39393e-06 + 0.999914 * (_ctx_2048t + 0.3 * jax.random.normal(jax.random.fold_in(_rk, 611), (32, 64, 256), jnp.float32))
        _validS = jnp.arange(64)[None, :] < _lenS[:, None]
        _validS2 = jnp.arange(64)[None, :] < _lenS2[:, None]
        _causal = jnp.tril(jnp.ones((64, 64), dtype=bool))
        mask_1x1xSxS2_fc1 = jnp.where(jnp.broadcast_to(_validS2[0:1, None, None, :], (1, 1, 64, 64)), 1.0, 0.0).astype(jnp.float32)
        mask_Bx1xSxS2_ff1 = jnp.where(jnp.ones((32, 1, 64, 64), dtype=bool), 1.0, 0.0).astype(jnp.float32)
        mask_BxS2_bf1 = jnp.ones((32, 64), dtype=bool)
        return (x, ctx_2048, mask_1x1xSxS2_fc1, mask_Bx1xSxS2_ff1, mask_BxS2_bf1)
    x, ctx_2048, mask_1x1xSxS2_fc1, mask_Bx1xSxS2_ff1, mask_BxS2_bf1 = _rec_inputs()

    def _L0_xattn_setup():
        import jax, jax.numpy as jnp
        import numpy as np
        H = 256
        NH = 16
        HD = H // NH
        EPS = 1e-05

        def gelu(x):
            return 0.5 * x * (1.0 + jnp.tanh(0.7978845608028654 * x * (1.0 + 0.044715 * x * x)))

        def layernorm(x, scale, bias):
            m = jnp.mean(x, axis=-1, keepdims=True)
            v = jnp.mean(jnp.square(x - m), axis=-1, keepdims=True)
            return (x - m) * jax.lax.rsqrt(v + EPS) * scale + bias

        def split_heads(x):
            b, s, _ = x.shape
            return x.reshape(b, s, NH, HD).transpose(0, 2, 1, 3)

        def merge_heads(x):
            b, nh, s, hd = x.shape
            return x.transpose(0, 2, 1, 3).reshape(b, s, nh * hd)

        def attention(q, k, v, mask):
            scores = jnp.einsum('bhqd,bhkd->bhqk', q, k) / jnp.sqrt(jnp.float32(HD))
            scores = scores * mask - 10000.0 * (1.0 - mask)
            probs = jax.nn.softmax(scores, axis=-1)
            return jnp.einsum('bhqk,bhkd->bhqd', probs, v)
        key = jax.random.key(seed)
        ks = jax.random.split(key, 16)
        b, s, t = (2, 128, 128)
        w = lambda k, i, o: jax.random.normal(k, (i, o), jnp.float32) * 0.02
        inp = {'hidden_states': jax.random.normal(ks[0], (b, s, H), jnp.float32), 'encoder_states': jax.random.normal(ks[1], (b, t, H), jnp.float32), 'ltor_mask': jnp.tril(jnp.ones((1, 1, s, s), jnp.float32)), 'cross_mask': jnp.ones((b, 1, s, t), jnp.float32), 'ln1_s': jnp.ones((H,), jnp.float32), 'ln1_b': jnp.zeros((H,), jnp.float32), 'w_qkv': w(ks[2], H, 3 * H), 'b_qkv': jnp.zeros((3 * H,), jnp.float32), 'w_ao': w(ks[3], H, H), 'b_ao': jnp.zeros((H,), jnp.float32), 'ln2_s': jnp.ones((H,), jnp.float32), 'ln2_b': jnp.zeros((H,), jnp.float32), 'w_q': w(ks[4], H, H), 'b_q': jnp.zeros((H,), jnp.float32), 'w_kv': w(ks[5], H, 2 * H), 'b_kv': jnp.zeros((2 * H,), jnp.float32), 'w_co': w(ks[6], H, H), 'b_co': jnp.zeros((H,), jnp.float32), 'ln3_s': jnp.ones((H,), jnp.float32), 'ln3_b': jnp.zeros((H,), jnp.float32), 'w1': w(ks[7], H, 4 * H), 'b1': jnp.zeros((4 * H,), jnp.float32), 'w2': w(ks[8], 4 * H, H), 'b2': jnp.zeros((H,), jnp.float32)}
        return inp
    _L0_xattn_all = _L0_xattn_setup()
    _L0_xattn_in = {k: v for k, v in _L0_xattn_all.items() if k in ('ln1_s', 'ln1_b', 'w_qkv', 'b_qkv', 'w_ao', 'b_ao', 'ln2_s', 'ln2_b', 'w_q', 'b_q', 'w_kv', 'b_kv', 'w_co', 'b_co', 'ln3_s', 'ln3_b', 'w1', 'b1', 'w2', 'b2')}
    del _L0_xattn_all

    def _L1_xattn_setup():
        import jax, jax.numpy as jnp
        import numpy as np
        E, H, L, B = (256, 32, 128, 4)
        S = E // H
        DM, DD = (32, 64)

        def _ln(x, w, b, eps=1e-05):
            m = x.mean(-1, keepdims=True)
            v = ((x - m) ** 2).mean(-1, keepdims=True)
            return (x - m) / jnp.sqrt(v + eps) * w + b

        def _block(x, state, ln1_w, ln1_b, ln2_w, ln2_b, maa_x, maa_w1, maa_w2, maa_stack, time_decay, td_w1, td_w2, u, Wr, Wk, Wv, Wg, Wo, gn_w, gn_b, ffn_maa_k, ffn_maa_r, Wfk, Wfr, Wfv):
            b, l, e = x.shape
            h = u.shape[0]
            s_ = e // h
            xa = _ln(x, ln1_w, ln1_b)
            sx = jnp.concatenate([state[:, 1:2] - xa[:, :1], xa[:, :-1] - xa[:, 1:]], axis=1)
            xxx = jnp.tanh((xa + sx * maa_x) @ maa_w1).reshape(b, l, 5, DM)
            xxx = jnp.einsum('blfd,fde->blfe', xxx, maa_w2)
            xm = xa[:, :, None] + sx[:, :, None] * (maa_stack + xxx)
            xk, xw, xv, xr, xg = (xm[:, :, j] for j in range(5))
            w = jnp.exp(-jnp.exp(time_decay + jnp.tanh(xw @ td_w1) @ td_w2)).reshape(b, l, h, s_)
            r = (xr @ Wr.T).reshape(b, l, h, s_)
            k = (xk @ Wk.T).reshape(b, l, h, s_)
            v = (xv @ Wv.T).reshape(b, l, h, s_)
            g = jax.nn.silu(xg @ Wg.T)
            s0 = state[:, 2:2 + s_].reshape(b, h, s_, s_)

            def step(s, rkvw):
                r_t, k_t, v_t, w_t = rkvw
                a = k_t[..., :, None] * v_t[..., None, :]
                out = jnp.einsum('bhi,bhij->bhj', r_t, u * a + s)
                s = a + w_t[..., :, None] * s
                return (s, out)
            rkvw = tuple((jnp.moveaxis(t, 1, 0) for t in (r, k, v, w)))
            _, out = jax.lax.scan(step, s0, rkvw)
            out = jnp.moveaxis(out, 0, 1).reshape(b, l, e)
            og = out.reshape(b, l, h, s_)
            m = og.mean(-1, keepdims=True)
            va = ((og - m) ** 2).mean(-1, keepdims=True)
            og = ((og - m) / jnp.sqrt(va + 1e-05)).reshape(b, l, e) * gn_w + gn_b
            x1 = x + og * g @ Wo.T
            xc = _ln(x1, ln2_w, ln2_b)
            sx2 = jnp.concatenate([state[:, 0:1] - xc[:, :1], xc[:, :-1] - xc[:, 1:]], axis=1)
            xk2 = xc + sx2 * ffn_maa_k
            xr2 = xc + sx2 * ffn_maa_r
            rr = jax.nn.sigmoid(xr2 @ Wfr.T)
            kk = jnp.square(jax.nn.relu(xk2 @ Wfk.T))
            return x1 + rr * (kk @ Wfv.T)
        key = jax.random.key(seed)
        ks = jax.random.split(key, 24)
        sc = 0.02
        d = {'x': jax.random.normal(ks[0], (B, L, E), jnp.float32), 'state': jax.random.normal(ks[1], (B, 2 + S, E), jnp.float32) * 0.1, 'ln1_w': jnp.ones((E,), jnp.float32), 'ln1_b': jnp.zeros((E,), jnp.float32), 'ln2_w': jnp.ones((E,), jnp.float32), 'ln2_b': jnp.zeros((E,), jnp.float32), 'maa_x': jax.random.normal(ks[2], (E,), jnp.float32) * 0.1, 'maa_w1': jax.random.normal(ks[3], (E, 5 * DM), jnp.float32) * sc, 'maa_w2': jax.random.normal(ks[4], (5, DM, E), jnp.float32) * sc, 'maa_stack': jax.random.normal(ks[5], (1, 5, E), jnp.float32) * 0.1, 'time_decay': jax.random.normal(ks[6], (E,), jnp.float32) * 0.5, 'td_w1': jax.random.normal(ks[7], (E, DD), jnp.float32) * sc, 'td_w2': jax.random.normal(ks[8], (DD, E), jnp.float32) * sc, 'u': jax.random.normal(ks[9], (H, S, 1), jnp.float32) * 0.1, 'Wr': jax.random.normal(ks[10], (E, E), jnp.float32) * sc, 'Wk': jax.random.normal(ks[11], (E, E), jnp.float32) * sc, 'Wv': jax.random.normal(ks[12], (E, E), jnp.float32) * sc, 'Wg': jax.random.normal(ks[13], (E, E), jnp.float32) * sc, 'Wo': jax.random.normal(ks[14], (E, E), jnp.float32) * sc, 'gn_w': jnp.ones((E,), jnp.float32), 'gn_b': jnp.zeros((E,), jnp.float32), 'ffn_maa_k': jax.random.normal(ks[15], (E,), jnp.float32) * 0.1, 'ffn_maa_r': jax.random.normal(ks[16], (E,), jnp.float32) * 0.1, 'Wfk': jax.random.normal(ks[17], (E, E), jnp.float32) * sc, 'Wfr': jax.random.normal(ks[18], (E, E), jnp.float32) * sc, 'Wfv': jax.random.normal(ks[19], (E, E), jnp.float32) * sc}
        return d
    _L1_xattn_all = _L1_xattn_setup()
    _L1_xattn_in = {k: v for k, v in _L1_xattn_all.items() if k in ('ln1_w', 'ln1_b', 'ln2_w', 'ln2_b', 'maa_x', 'maa_w1', 'maa_w2', 'maa_stack', 'time_decay', 'td_w1', 'td_w2', 'u', 'Wr', 'Wk', 'Wv', 'Wg', 'Wo', 'gn_w', 'gn_b', 'ffn_maa_k', 'ffn_maa_r', 'Wfk', 'Wfr', 'Wfv')}
    del _L1_xattn_all

    def _L2_xattn_setup():
        import jax, jax.numpy as jnp
        import numpy as np
        B, Q, S1, S2 = (4, 32, 256, 256)
        D, H, K, F = (256, 16, 128, 1024)
        LN_EPS = 1e-05

        def _layer_norm(x, scale, offset):
            mu = jnp.mean(x, axis=-1, keepdims=True)
            var = jnp.var(x, axis=-1, keepdims=True)
            return (x - mu) * jax.lax.rsqrt(var + LN_EPS) * scale + offset

        def _cross_attention(q_in, kv_in, wq, bq, wk, bk, wv, bv, wo, bo, bias_k, bias_v):
            b, q_len, _ = q_in.shape
            t = kv_in.shape[1]
            qh = (q_in @ wq + bq).reshape(b, q_len, H, K)
            kh = (kv_in @ wk + bk).reshape(b, t, H, K)
            vh = (kv_in @ wv + bv).reshape(b, t, H, K)
            kh = jnp.concatenate([kh, jnp.broadcast_to(bias_k, (b, 1, H, K))], axis=1)
            vh = jnp.concatenate([vh, jnp.broadcast_to(bias_v, (b, 1, H, K))], axis=1)
            scale = jnp.sqrt(jnp.asarray(K, q_in.dtype))
            logits = jnp.einsum('bqhk,bthk->bhqt', qh, kh) / scale
            weights = jax.nn.softmax(logits, axis=-1)
            ctx = jnp.einsum('bhqt,bthk->bqhk', weights, vh).reshape(b, q_len, H * K)
            return ctx @ wo + bo

        def _forward(x, xf_1, xf_2, ln1_scale, ln1_offset, wq1, bq1, wk1, bk1, wv1, bv1, wo1, bo1, bias_k1, bias_v1, ln2_scale, ln2_offset, wq2, bq2, wk2, bk2, wv2, bv2, wo2, bo2, bias_k2, bias_v2, ln_mlp_scale, ln_mlp_offset, w_fc1, b_fc1, w_fc2, b_fc2):
            res = x
            h = _layer_norm(x, ln1_scale, ln1_offset)
            x = res + _cross_attention(h, xf_1, wq1, bq1, wk1, bk1, wv1, bv1, wo1, bo1, bias_k1, bias_v1)
            res = x
            h = _layer_norm(x, ln2_scale, ln2_offset)
            x = res + _cross_attention(h, xf_2, wq2, bq2, wk2, bk2, wv2, bv2, wo2, bo2, bias_k2, bias_v2)
            h = _layer_norm(x, ln_mlp_scale, ln_mlp_offset)
            h = jax.nn.gelu(h @ w_fc1 + b_fc1, approximate=False) @ w_fc2 + b_fc2
            return x + h
        key = jax.random.key(seed)
        ks = iter(jax.random.split(key, 64))

        def rn(shape, s=0.02):
            return jax.random.normal(next(ks), shape, jnp.float32) * s
        inp = {'x': rn((B, Q, D), 1.0), 'xf_1': rn((B, S1, D), 1.0), 'xf_2': rn((B, S2, D), 1.0)}
        for i in (1, 2):
            inp[f'ln{i}_scale'] = jnp.ones((D,), jnp.float32)
            inp[f'ln{i}_offset'] = jnp.zeros((D,), jnp.float32)
            inp[f'wq{i}'] = rn((D, H * K))
            inp[f'bq{i}'] = jnp.zeros((H * K,), jnp.float32)
            inp[f'wk{i}'] = rn((D, H * K))
            inp[f'bk{i}'] = jnp.zeros((H * K,), jnp.float32)
            inp[f'wv{i}'] = rn((D, H * K))
            inp[f'bv{i}'] = jnp.zeros((H * K,), jnp.float32)
            inp[f'wo{i}'] = rn((H * K, D))
            inp[f'bo{i}'] = jnp.zeros((D,), jnp.float32)
            inp[f'bias_k{i}'] = rn((1, 1, H, K))
            inp[f'bias_v{i}'] = rn((1, 1, H, K))
        inp['ln_mlp_scale'] = jnp.ones((D,), jnp.float32)
        inp['ln_mlp_offset'] = jnp.zeros((D,), jnp.float32)
        inp['w_fc1'] = rn((D, F))
        inp['b_fc1'] = jnp.zeros((F,), jnp.float32)
        inp['w_fc2'] = rn((F, D))
        inp['b_fc2'] = jnp.zeros((D,), jnp.float32)
        return inp
    _L2_xattn_all = _L2_xattn_setup()
    _L2_xattn_in = {k: v for k, v in _L2_xattn_all.items() if k in ('ln1_scale', 'ln1_offset', 'wq1', 'bq1', 'wk1', 'bk1', 'wv1', 'bv1', 'wo1', 'bo1', 'bias_k1', 'bias_v1', 'ln2_scale', 'ln2_offset', 'wq2', 'bq2', 'wk2', 'bk2', 'wv2', 'bv2', 'wo2', 'bo2', 'bias_k2', 'bias_v2', 'ln_mlp_scale', 'ln_mlp_offset', 'w_fc1', 'b_fc1', 'w_fc2', 'b_fc2')}
    del _L2_xattn_all

    def _L3_xattn_setup():
        import jax, jax.numpy as jnp
        import numpy as np
        D = 256
        H = 16
        HD = D // H
        INNER = 4 * D
        EPS = 1e-05

        def layer_norm(x, w, b):
            mu = jnp.mean(x, axis=-1, keepdims=True)
            var = jnp.mean(jnp.square(x - mu), axis=-1, keepdims=True)
            return (x - mu) * jax.lax.rsqrt(var + EPS) * w + b
        key = jax.random.key(seed)
        ks = jax.random.split(key, 12)
        B, LQ, LK = (4, 128, 256)
        std = 0.02
        inp = {'hidden_states': jax.random.normal(ks[0], (B, LQ, D), jnp.float32), 'encoder_hidden_states': jax.random.normal(ks[1], (B, LK, D), jnp.float32), 'encoder_attention_mask': jnp.ones((B, LK), dtype=bool), 'ln1_w': jnp.ones((D,), jnp.float32), 'ln1_b': jnp.zeros((D,), jnp.float32), 'q_w': jax.random.normal(ks[2], (D, D), jnp.float32) * std, 'q_b': jnp.zeros((D,), jnp.float32), 'k_w': jax.random.normal(ks[3], (D, D), jnp.float32) * std, 'k_b': jnp.zeros((D,), jnp.float32), 'v_w': jax.random.normal(ks[4], (D, D), jnp.float32) * std, 'v_b': jnp.zeros((D,), jnp.float32), 'cproj_w': jax.random.normal(ks[5], (D, D), jnp.float32) * std, 'cproj_b': jnp.zeros((D,), jnp.float32), 'ln2_w': jnp.ones((D,), jnp.float32), 'ln2_b': jnp.zeros((D,), jnp.float32), 'fc_w': jax.random.normal(ks[6], (D, INNER), jnp.float32) * std, 'fc_b': jnp.zeros((INNER,), jnp.float32), 'proj_w': jax.random.normal(ks[7], (INNER, D), jnp.float32) * std, 'proj_b': jnp.zeros((D,), jnp.float32)}
        return inp
    _L3_xattn_all = _L3_xattn_setup()
    _L3_xattn_in = {k: v for k, v in _L3_xattn_all.items() if k in ('ln1_w', 'ln1_b', 'q_w', 'q_b', 'k_w', 'k_b', 'v_w', 'v_b', 'cproj_w', 'cproj_b', 'ln2_w', 'ln2_b', 'fc_w', 'fc_b', 'proj_w', 'proj_b')}
    del _L3_xattn_all
    return {'x': x, 'ctx_2048': ctx_2048, 'mask_1x1xSxS2_fc1': mask_1x1xSxS2_fc1, 'mask_Bx1xSxS2_ff1': mask_Bx1xSxS2_ff1, 'mask_BxS2_bf1': mask_BxS2_bf1, 'L0_xattn_ln1_s': _L0_xattn_in['ln1_s'], 'L0_xattn_ln1_b': _L0_xattn_in['ln1_b'], 'L0_xattn_w_qkv': _L0_xattn_in['w_qkv'], 'L0_xattn_b_qkv': _L0_xattn_in['b_qkv'], 'L0_xattn_w_ao': _L0_xattn_in['w_ao'], 'L0_xattn_b_ao': _L0_xattn_in['b_ao'], 'L0_xattn_ln2_s': _L0_xattn_in['ln2_s'], 'L0_xattn_ln2_b': _L0_xattn_in['ln2_b'], 'L0_xattn_w_q': _L0_xattn_in['w_q'], 'L0_xattn_b_q': _L0_xattn_in['b_q'], 'L0_xattn_w_kv': _L0_xattn_in['w_kv'], 'L0_xattn_b_kv': _L0_xattn_in['b_kv'], 'L0_xattn_w_co': _L0_xattn_in['w_co'], 'L0_xattn_b_co': _L0_xattn_in['b_co'], 'L0_xattn_ln3_s': _L0_xattn_in['ln3_s'], 'L0_xattn_ln3_b': _L0_xattn_in['ln3_b'], 'L0_xattn_w1': _L0_xattn_in['w1'], 'L0_xattn_b1': _L0_xattn_in['b1'], 'L0_xattn_w2': _L0_xattn_in['w2'], 'L0_xattn_b2': _L0_xattn_in['b2'], 'L1_xattn_ln1_w': _L1_xattn_in['ln1_w'], 'L1_xattn_ln1_b': _L1_xattn_in['ln1_b'], 'L1_xattn_ln2_w': _L1_xattn_in['ln2_w'], 'L1_xattn_ln2_b': _L1_xattn_in['ln2_b'], 'L1_xattn_maa_x': _L1_xattn_in['maa_x'], 'L1_xattn_maa_w1': _L1_xattn_in['maa_w1'], 'L1_xattn_maa_w2': _L1_xattn_in['maa_w2'], 'L1_xattn_maa_stack': _L1_xattn_in['maa_stack'], 'L1_xattn_time_decay': _L1_xattn_in['time_decay'], 'L1_xattn_td_w1': _L1_xattn_in['td_w1'], 'L1_xattn_td_w2': _L1_xattn_in['td_w2'], 'L1_xattn_u': _L1_xattn_in['u'], 'L1_xattn_Wr': _L1_xattn_in['Wr'], 'L1_xattn_Wk': _L1_xattn_in['Wk'], 'L1_xattn_Wv': _L1_xattn_in['Wv'], 'L1_xattn_Wg': _L1_xattn_in['Wg'], 'L1_xattn_Wo': _L1_xattn_in['Wo'], 'L1_xattn_gn_w': _L1_xattn_in['gn_w'], 'L1_xattn_gn_b': _L1_xattn_in['gn_b'], 'L1_xattn_ffn_maa_k': _L1_xattn_in['ffn_maa_k'], 'L1_xattn_ffn_maa_r': _L1_xattn_in['ffn_maa_r'], 'L1_xattn_Wfk': _L1_xattn_in['Wfk'], 'L1_xattn_Wfr': _L1_xattn_in['Wfr'], 'L1_xattn_Wfv': _L1_xattn_in['Wfv'], 'L2_xattn_ln1_scale': _L2_xattn_in['ln1_scale'], 'L2_xattn_ln1_offset': _L2_xattn_in['ln1_offset'], 'L2_xattn_wq1': _L2_xattn_in['wq1'], 'L2_xattn_bq1': _L2_xattn_in['bq1'], 'L2_xattn_wk1': _L2_xattn_in['wk1'], 'L2_xattn_bk1': _L2_xattn_in['bk1'], 'L2_xattn_wv1': _L2_xattn_in['wv1'], 'L2_xattn_bv1': _L2_xattn_in['bv1'], 'L2_xattn_wo1': _L2_xattn_in['wo1'], 'L2_xattn_bo1': _L2_xattn_in['bo1'], 'L2_xattn_bias_k1': _L2_xattn_in['bias_k1'], 'L2_xattn_bias_v1': _L2_xattn_in['bias_v1'], 'L2_xattn_ln2_scale': _L2_xattn_in['ln2_scale'], 'L2_xattn_ln2_offset': _L2_xattn_in['ln2_offset'], 'L2_xattn_wq2': _L2_xattn_in['wq2'], 'L2_xattn_bq2': _L2_xattn_in['bq2'], 'L2_xattn_wk2': _L2_xattn_in['wk2'], 'L2_xattn_bk2': _L2_xattn_in['bk2'], 'L2_xattn_wv2': _L2_xattn_in['wv2'], 'L2_xattn_bv2': _L2_xattn_in['bv2'], 'L2_xattn_wo2': _L2_xattn_in['wo2'], 'L2_xattn_bo2': _L2_xattn_in['bo2'], 'L2_xattn_bias_k2': _L2_xattn_in['bias_k2'], 'L2_xattn_bias_v2': _L2_xattn_in['bias_v2'], 'L2_xattn_ln_mlp_scale': _L2_xattn_in['ln_mlp_scale'], 'L2_xattn_ln_mlp_offset': _L2_xattn_in['ln_mlp_offset'], 'L2_xattn_w_fc1': _L2_xattn_in['w_fc1'], 'L2_xattn_b_fc1': _L2_xattn_in['b_fc1'], 'L2_xattn_w_fc2': _L2_xattn_in['w_fc2'], 'L2_xattn_b_fc2': _L2_xattn_in['b_fc2'], 'L3_xattn_ln1_w': _L3_xattn_in['ln1_w'], 'L3_xattn_ln1_b': _L3_xattn_in['ln1_b'], 'L3_xattn_q_w': _L3_xattn_in['q_w'], 'L3_xattn_q_b': _L3_xattn_in['q_b'], 'L3_xattn_k_w': _L3_xattn_in['k_w'], 'L3_xattn_k_b': _L3_xattn_in['k_b'], 'L3_xattn_v_w': _L3_xattn_in['v_w'], 'L3_xattn_v_b': _L3_xattn_in['v_b'], 'L3_xattn_cproj_w': _L3_xattn_in['cproj_w'], 'L3_xattn_cproj_b': _L3_xattn_in['cproj_b'], 'L3_xattn_ln2_w': _L3_xattn_in['ln2_w'], 'L3_xattn_ln2_b': _L3_xattn_in['ln2_b'], 'L3_xattn_fc_w': _L3_xattn_in['fc_w'], 'L3_xattn_fc_b': _L3_xattn_in['fc_b'], 'L3_xattn_proj_w': _L3_xattn_in['proj_w'], 'L3_xattn_proj_b': _L3_xattn_in['proj_b']}

def reference(x, ctx_2048, mask_1x1xSxS2_fc1, mask_Bx1xSxS2_ff1, mask_BxS2_bf1, L0_xattn_ln1_s, L0_xattn_ln1_b, L0_xattn_w_qkv, L0_xattn_b_qkv, L0_xattn_w_ao, L0_xattn_b_ao, L0_xattn_ln2_s, L0_xattn_ln2_b, L0_xattn_w_q, L0_xattn_b_q, L0_xattn_w_kv, L0_xattn_b_kv, L0_xattn_w_co, L0_xattn_b_co, L0_xattn_ln3_s, L0_xattn_ln3_b, L0_xattn_w1, L0_xattn_b1, L0_xattn_w2, L0_xattn_b2, L1_xattn_ln1_w, L1_xattn_ln1_b, L1_xattn_ln2_w, L1_xattn_ln2_b, L1_xattn_maa_x, L1_xattn_maa_w1, L1_xattn_maa_w2, L1_xattn_maa_stack, L1_xattn_time_decay, L1_xattn_td_w1, L1_xattn_td_w2, L1_xattn_u, L1_xattn_Wr, L1_xattn_Wk, L1_xattn_Wv, L1_xattn_Wg, L1_xattn_Wo, L1_xattn_gn_w, L1_xattn_gn_b, L1_xattn_ffn_maa_k, L1_xattn_ffn_maa_r, L1_xattn_Wfk, L1_xattn_Wfr, L1_xattn_Wfv, L2_xattn_ln1_scale, L2_xattn_ln1_offset, L2_xattn_wq1, L2_xattn_bq1, L2_xattn_wk1, L2_xattn_bk1, L2_xattn_wv1, L2_xattn_bv1, L2_xattn_wo1, L2_xattn_bo1, L2_xattn_bias_k1, L2_xattn_bias_v1, L2_xattn_ln2_scale, L2_xattn_ln2_offset, L2_xattn_wq2, L2_xattn_bq2, L2_xattn_wk2, L2_xattn_bk2, L2_xattn_wv2, L2_xattn_bv2, L2_xattn_wo2, L2_xattn_bo2, L2_xattn_bias_k2, L2_xattn_bias_v2, L2_xattn_ln_mlp_scale, L2_xattn_ln_mlp_offset, L2_xattn_w_fc1, L2_xattn_b_fc1, L2_xattn_w_fc2, L2_xattn_b_fc2, L3_xattn_ln1_w, L3_xattn_ln1_b, L3_xattn_q_w, L3_xattn_q_b, L3_xattn_k_w, L3_xattn_k_b, L3_xattn_v_w, L3_xattn_v_b, L3_xattn_cproj_w, L3_xattn_cproj_b, L3_xattn_ln2_w, L3_xattn_ln2_b, L3_xattn_fc_w, L3_xattn_fc_b, L3_xattn_proj_w, L3_xattn_proj_b):
    import jax
    import jax.numpy as jnp

    def _L0_xattn_ref(hidden_states, encoder_states, ltor_mask, cross_mask, ln1_s, ln1_b, w_qkv, b_qkv, w_ao, b_ao, ln2_s, ln2_b, w_q, b_q, w_kv, b_kv, w_co, b_co, ln3_s, ln3_b, w1, b1, w2, b2):
        import jax, jax.numpy as jnp
        import numpy as np
        H = 256
        NH = 16
        HD = H // NH
        EPS = 1e-05

        def gelu(x):
            return 0.5 * x * (1.0 + jnp.tanh(0.7978845608028654 * x * (1.0 + 0.044715 * x * x)))

        def layernorm(x, scale, bias):
            m = jnp.mean(x, axis=-1, keepdims=True)
            v = jnp.mean(jnp.square(x - m), axis=-1, keepdims=True)
            return (x - m) * jax.lax.rsqrt(v + EPS) * scale + bias

        def split_heads(x):
            b, s, _ = x.shape
            return x.reshape(b, s, NH, HD).transpose(0, 2, 1, 3)

        def merge_heads(x):
            b, nh, s, hd = x.shape
            return x.transpose(0, 2, 1, 3).reshape(b, s, nh * hd)

        def attention(q, k, v, mask):
            scores = jnp.einsum('bhqd,bhkd->bhqk', q, k) / jnp.sqrt(jnp.float32(HD))
            scores = scores * mask - 10000.0 * (1.0 - mask)
            probs = jax.nn.softmax(scores, axis=-1)
            return jnp.einsum('bhqk,bhkd->bhqd', probs, v)
        ln_out = layernorm(hidden_states, ln1_s, ln1_b)
        qkv = ln_out @ w_qkv + b_qkv
        q, k, v = jnp.split(qkv, 3, axis=-1)
        ctx = merge_heads(attention(split_heads(q), split_heads(k), split_heads(v), ltor_mask))
        attn_out = ctx @ w_ao + b_ao
        x = hidden_states + attn_out
        ln_out = layernorm(x, ln2_s, ln2_b)
        q = ln_out @ w_q + b_q
        kv = encoder_states @ w_kv + b_kv
        k, v = jnp.split(kv, 2, axis=-1)
        ctx = merge_heads(attention(split_heads(q), split_heads(k), split_heads(v), cross_mask))
        cross_out = ctx @ w_co + b_co
        x = x + cross_out
        ln_out = layernorm(x, ln3_s, ln3_b)
        mlp_out = gelu(ln_out @ w1 + b1) @ w2 + b2
        return x + mlp_out

    def _L1_xattn_ref(x, state, ln1_w, ln1_b, ln2_w, ln2_b, maa_x, maa_w1, maa_w2, maa_stack, time_decay, td_w1, td_w2, u, Wr, Wk, Wv, Wg, Wo, gn_w, gn_b, ffn_maa_k, ffn_maa_r, Wfk, Wfr, Wfv):
        import jax, jax.numpy as jnp
        import numpy as np
        E, H, L, B = (256, 32, 128, 4)
        S = E // H
        DM, DD = (32, 64)

        def _ln(x, w, b, eps=1e-05):
            m = x.mean(-1, keepdims=True)
            v = ((x - m) ** 2).mean(-1, keepdims=True)
            return (x - m) / jnp.sqrt(v + eps) * w + b

        def _block(x, state, ln1_w, ln1_b, ln2_w, ln2_b, maa_x, maa_w1, maa_w2, maa_stack, time_decay, td_w1, td_w2, u, Wr, Wk, Wv, Wg, Wo, gn_w, gn_b, ffn_maa_k, ffn_maa_r, Wfk, Wfr, Wfv):
            b, l, e = x.shape
            h = u.shape[0]
            s_ = e // h
            xa = _ln(x, ln1_w, ln1_b)
            sx = jnp.concatenate([state[:, 1:2] - xa[:, :1], xa[:, :-1] - xa[:, 1:]], axis=1)
            xxx = jnp.tanh((xa + sx * maa_x) @ maa_w1).reshape(b, l, 5, DM)
            xxx = jnp.einsum('blfd,fde->blfe', xxx, maa_w2)
            xm = xa[:, :, None] + sx[:, :, None] * (maa_stack + xxx)
            xk, xw, xv, xr, xg = (xm[:, :, j] for j in range(5))
            w = jnp.exp(-jnp.exp(time_decay + jnp.tanh(xw @ td_w1) @ td_w2)).reshape(b, l, h, s_)
            r = (xr @ Wr.T).reshape(b, l, h, s_)
            k = (xk @ Wk.T).reshape(b, l, h, s_)
            v = (xv @ Wv.T).reshape(b, l, h, s_)
            g = jax.nn.silu(xg @ Wg.T)
            s0 = state[:, 2:2 + s_].reshape(b, h, s_, s_)

            def step(s, rkvw):
                r_t, k_t, v_t, w_t = rkvw
                a = k_t[..., :, None] * v_t[..., None, :]
                out = jnp.einsum('bhi,bhij->bhj', r_t, u * a + s)
                s = a + w_t[..., :, None] * s
                return (s, out)
            rkvw = tuple((jnp.moveaxis(t, 1, 0) for t in (r, k, v, w)))
            _, out = jax.lax.scan(step, s0, rkvw)
            out = jnp.moveaxis(out, 0, 1).reshape(b, l, e)
            og = out.reshape(b, l, h, s_)
            m = og.mean(-1, keepdims=True)
            va = ((og - m) ** 2).mean(-1, keepdims=True)
            og = ((og - m) / jnp.sqrt(va + 1e-05)).reshape(b, l, e) * gn_w + gn_b
            x1 = x + og * g @ Wo.T
            xc = _ln(x1, ln2_w, ln2_b)
            sx2 = jnp.concatenate([state[:, 0:1] - xc[:, :1], xc[:, :-1] - xc[:, 1:]], axis=1)
            xk2 = xc + sx2 * ffn_maa_k
            xr2 = xc + sx2 * ffn_maa_r
            rr = jax.nn.sigmoid(xr2 @ Wfr.T)
            kk = jnp.square(jax.nn.relu(xk2 @ Wfk.T))
            return x1 + rr * (kk @ Wfv.T)
        return _block(x, state, ln1_w, ln1_b, ln2_w, ln2_b, maa_x, maa_w1, maa_w2, maa_stack, time_decay, td_w1, td_w2, u, Wr, Wk, Wv, Wg, Wo, gn_w, gn_b, ffn_maa_k, ffn_maa_r, Wfk, Wfr, Wfv)

    def _L2_xattn_ref(x, xf_1, xf_2, ln1_scale, ln1_offset, wq1, bq1, wk1, bk1, wv1, bv1, wo1, bo1, bias_k1, bias_v1, ln2_scale, ln2_offset, wq2, bq2, wk2, bk2, wv2, bv2, wo2, bo2, bias_k2, bias_v2, ln_mlp_scale, ln_mlp_offset, w_fc1, b_fc1, w_fc2, b_fc2):
        import jax, jax.numpy as jnp
        import numpy as np
        B, Q, S1, S2 = (4, 32, 256, 256)
        D, H, K, F = (256, 16, 128, 1024)
        LN_EPS = 1e-05

        def _layer_norm(x, scale, offset):
            mu = jnp.mean(x, axis=-1, keepdims=True)
            var = jnp.var(x, axis=-1, keepdims=True)
            return (x - mu) * jax.lax.rsqrt(var + LN_EPS) * scale + offset

        def _cross_attention(q_in, kv_in, wq, bq, wk, bk, wv, bv, wo, bo, bias_k, bias_v):
            b, q_len, _ = q_in.shape
            t = kv_in.shape[1]
            qh = (q_in @ wq + bq).reshape(b, q_len, H, K)
            kh = (kv_in @ wk + bk).reshape(b, t, H, K)
            vh = (kv_in @ wv + bv).reshape(b, t, H, K)
            kh = jnp.concatenate([kh, jnp.broadcast_to(bias_k, (b, 1, H, K))], axis=1)
            vh = jnp.concatenate([vh, jnp.broadcast_to(bias_v, (b, 1, H, K))], axis=1)
            scale = jnp.sqrt(jnp.asarray(K, q_in.dtype))
            logits = jnp.einsum('bqhk,bthk->bhqt', qh, kh) / scale
            weights = jax.nn.softmax(logits, axis=-1)
            ctx = jnp.einsum('bhqt,bthk->bqhk', weights, vh).reshape(b, q_len, H * K)
            return ctx @ wo + bo

        def _forward(x, xf_1, xf_2, ln1_scale, ln1_offset, wq1, bq1, wk1, bk1, wv1, bv1, wo1, bo1, bias_k1, bias_v1, ln2_scale, ln2_offset, wq2, bq2, wk2, bk2, wv2, bv2, wo2, bo2, bias_k2, bias_v2, ln_mlp_scale, ln_mlp_offset, w_fc1, b_fc1, w_fc2, b_fc2):
            res = x
            h = _layer_norm(x, ln1_scale, ln1_offset)
            x = res + _cross_attention(h, xf_1, wq1, bq1, wk1, bk1, wv1, bv1, wo1, bo1, bias_k1, bias_v1)
            res = x
            h = _layer_norm(x, ln2_scale, ln2_offset)
            x = res + _cross_attention(h, xf_2, wq2, bq2, wk2, bk2, wv2, bv2, wo2, bo2, bias_k2, bias_v2)
            h = _layer_norm(x, ln_mlp_scale, ln_mlp_offset)
            h = jax.nn.gelu(h @ w_fc1 + b_fc1, approximate=False) @ w_fc2 + b_fc2
            return x + h
        return _forward(x, xf_1, xf_2, ln1_scale, ln1_offset, wq1, bq1, wk1, bk1, wv1, bv1, wo1, bo1, bias_k1, bias_v1, ln2_scale, ln2_offset, wq2, bq2, wk2, bk2, wv2, bv2, wo2, bo2, bias_k2, bias_v2, ln_mlp_scale, ln_mlp_offset, w_fc1, b_fc1, w_fc2, b_fc2)

    def _L3_xattn_ref(hidden_states, encoder_hidden_states, encoder_attention_mask, ln1_w, ln1_b, q_w, q_b, k_w, k_b, v_w, v_b, cproj_w, cproj_b, ln2_w, ln2_b, fc_w, fc_b, proj_w, proj_b):
        import jax, jax.numpy as jnp
        import numpy as np
        D = 256
        H = 16
        HD = D // H
        INNER = 4 * D
        EPS = 1e-05

        def layer_norm(x, w, b):
            mu = jnp.mean(x, axis=-1, keepdims=True)
            var = jnp.mean(jnp.square(x - mu), axis=-1, keepdims=True)
            return (x - mu) * jax.lax.rsqrt(var + EPS) * w + b
        B, LQ, _ = hidden_states.shape
        LK = encoder_hidden_states.shape[1]
        residual = hidden_states
        x = layer_norm(hidden_states, ln1_w, ln1_b)
        q = (x @ q_w + q_b).reshape(B, LQ, H, HD).transpose(0, 2, 1, 3)
        k = (encoder_hidden_states @ k_w + k_b).reshape(B, LK, H, HD).transpose(0, 2, 1, 3)
        v = (encoder_hidden_states @ v_w + v_b).reshape(B, LK, H, HD).transpose(0, 2, 1, 3)
        scale = 1.0 / np.sqrt(HD).astype(np.float32)
        scores = jnp.einsum('bhqd,bhkd->bhqk', q, k) * scale
        mask = encoder_attention_mask[:, None, None, :]
        mask_value = jnp.finfo(scores.dtype).min
        scores = jnp.where(mask, scores, mask_value)
        attn = jax.nn.softmax(scores, axis=-1)
        out = jnp.einsum('bhqk,bhkd->bhqd', attn, v)
        out = out.transpose(0, 2, 1, 3).reshape(B, LQ, D)
        out = out @ cproj_w + cproj_b
        hidden = out + residual
        residual = hidden
        y = layer_norm(hidden, ln2_w, ln2_b)
        y = jax.nn.gelu(y @ fc_w + fc_b, approximate=True)
        y = y @ proj_w + proj_b
        return residual + y
    x = _L0_xattn_ref(x, ctx_2048, mask_1x1xSxS2_fc1, mask_Bx1xSxS2_ff1, L0_xattn_ln1_s, L0_xattn_ln1_b, L0_xattn_w_qkv, L0_xattn_b_qkv, L0_xattn_w_ao, L0_xattn_b_ao, L0_xattn_ln2_s, L0_xattn_ln2_b, L0_xattn_w_q, L0_xattn_b_q, L0_xattn_w_kv, L0_xattn_b_kv, L0_xattn_w_co, L0_xattn_b_co, L0_xattn_ln3_s, L0_xattn_ln3_b, L0_xattn_w1, L0_xattn_b1, L0_xattn_w2, L0_xattn_b2)
    x = _L1_xattn_ref(x, ctx_2048, L1_xattn_ln1_w, L1_xattn_ln1_b, L1_xattn_ln2_w, L1_xattn_ln2_b, L1_xattn_maa_x, L1_xattn_maa_w1, L1_xattn_maa_w2, L1_xattn_maa_stack, L1_xattn_time_decay, L1_xattn_td_w1, L1_xattn_td_w2, L1_xattn_u, L1_xattn_Wr, L1_xattn_Wk, L1_xattn_Wv, L1_xattn_Wg, L1_xattn_Wo, L1_xattn_gn_w, L1_xattn_gn_b, L1_xattn_ffn_maa_k, L1_xattn_ffn_maa_r, L1_xattn_Wfk, L1_xattn_Wfr, L1_xattn_Wfv)
    x = _L2_xattn_ref(x, ctx_2048, ctx_2048, L2_xattn_ln1_scale, L2_xattn_ln1_offset, L2_xattn_wq1, L2_xattn_bq1, L2_xattn_wk1, L2_xattn_bk1, L2_xattn_wv1, L2_xattn_bv1, L2_xattn_wo1, L2_xattn_bo1, L2_xattn_bias_k1, L2_xattn_bias_v1, L2_xattn_ln2_scale, L2_xattn_ln2_offset, L2_xattn_wq2, L2_xattn_bq2, L2_xattn_wk2, L2_xattn_bk2, L2_xattn_wv2, L2_xattn_bv2, L2_xattn_wo2, L2_xattn_bo2, L2_xattn_bias_k2, L2_xattn_bias_v2, L2_xattn_ln_mlp_scale, L2_xattn_ln_mlp_offset, L2_xattn_w_fc1, L2_xattn_b_fc1, L2_xattn_w_fc2, L2_xattn_b_fc2)
    x = _L3_xattn_ref(x, ctx_2048, mask_BxS2_bf1, L3_xattn_ln1_w, L3_xattn_ln1_b, L3_xattn_q_w, L3_xattn_q_b, L3_xattn_k_w, L3_xattn_k_b, L3_xattn_v_w, L3_xattn_v_b, L3_xattn_cproj_w, L3_xattn_cproj_b, L3_xattn_ln2_w, L3_xattn_ln2_b, L3_xattn_fc_w, L3_xattn_fc_b, L3_xattn_proj_w, L3_xattn_proj_b)
    return x

_drawn_inputs = setup_inputs


def setup_inputs(seed=0):
    import zlib

    import numpy as np

    out = dict(_drawn_inputs(seed))
    spreads = {'L0_xattn_ln1_s': (1.0, 0.6),
     'L0_xattn_ln1_b': (0.0, 0.8),
     'L0_xattn_b_qkv': (0.0, 0.285),
     'L0_xattn_b_ao': (0.0, 0.1),
     'L0_xattn_ln2_s': (1.0, 0.6),
     'L0_xattn_ln2_b': (0.0, 2.0),
     'L0_xattn_b_q': (0.0, 2.0),
     'L0_xattn_b_kv': (0.0, 0.296),
     'L0_xattn_b_co': (0.0, 0.1),
     'L0_xattn_ln3_s': (1.0, 0.6),
     'L0_xattn_ln3_b': (0.0, 0.693),
     'L0_xattn_b1': (0.0, 0.1),
     'L0_xattn_b2': (0.0, 0.1),
     'L1_xattn_ln1_w': (1.0, 0.6),
     'L1_xattn_ln1_b': (0.0, 0.595),
     'L1_xattn_ln2_w': (1.0, 0.6),
     'L1_xattn_ln2_b': (0.0, 0.8),
     'L1_xattn_gn_w': (1.0, 0.6),
     'L1_xattn_gn_b': (0.0, 0.8),
     'L2_xattn_ln1_scale': (1.0, 0.6),
     'L2_xattn_ln1_offset': (0.0, 0.8),
     'L2_xattn_bq1': (0.0, 0.8),
     'L2_xattn_bk1': (0.0, 2.0),
     'L2_xattn_bv1': (0.0, 0.286),
     'L2_xattn_bo1': (0.0, 0.269),
     'L2_xattn_ln2_scale': (1.0, 0.6),
     'L2_xattn_ln2_offset': (0.0, 0.8),
     'L2_xattn_bq2': (0.0, 0.8),
     'L2_xattn_bk2': (0.0, 2.0),
     'L2_xattn_bv2': (0.0, 0.309),
     'L2_xattn_bo2': (0.0, 0.279),
     'L2_xattn_ln_mlp_scale': (1.0, 0.6),
     'L2_xattn_ln_mlp_offset': (0.0, 2.0),
     'L2_xattn_b_fc1': (0.0, 0.706),
     'L2_xattn_b_fc2': (0.0, 0.27),
     'L3_xattn_ln1_w': (1.0, 0.6),
     'L3_xattn_ln1_b': (0.0, 2.0),
     'L3_xattn_q_b': (0.0, 2.0),
     'L3_xattn_k_b': (0.0, 2.0),
     'L3_xattn_v_b': (0.0, 0.8),
     'L3_xattn_cproj_b': (0.0, 0.268),
     'L3_xattn_ln2_w': (1.0, 0.6),
     'L3_xattn_ln2_b': (0.0, 2.0),
     'L3_xattn_fc_b': (0.0, 0.765),
     'L3_xattn_proj_b': (0.0, 0.299)}
    factors = {'L0_xattn_w_qkv': 3.255,
     'L0_xattn_w_q': 200.0,
     'L1_xattn_maa_x': 8.0,
     'L1_xattn_maa_w1': 8.0,
     'L1_xattn_maa_w2': 8.0,
     'L1_xattn_maa_stack': 3.065,
     'L1_xattn_time_decay': 2.937,
     'L1_xattn_td_w1': 8.0,
     'L1_xattn_td_w2': 8.0,
     'L1_xattn_u': 6.228,
     'L1_xattn_ffn_maa_k': 8.0,
     'L1_xattn_ffn_maa_r': 8.0,
     'L1_xattn_Wfk': 3.024,
     'L1_xattn_Wfr': 8.0,
     'L1_xattn_Wfv': 2.83,
     'L2_xattn_wq1': 8.0,
     'L2_xattn_wk1': 8.0,
     'L2_xattn_bias_k1': 64.0,
     'L2_xattn_bias_v1': 64.0,
     'L2_xattn_wq2': 8.0,
     'L2_xattn_wk2': 8.0,
     'L2_xattn_bias_k2': 64.0,
     'L2_xattn_bias_v2': 64.0,
     'L3_xattn_q_w': 8.0,
     'L3_xattn_k_w': 8.0}
    for name, (base, spread) in spreads.items():
        noise = np.random.default_rng([zlib.crc32(name.encode()), seed]).standard_normal(out[name].shape)
        drawn = base * np.exp(spread * noise) if base else spread * noise
        out[name] = jnp.asarray(drawn.astype(out[name].dtype))
    for name, factor in factors.items():
        out[name] = (out[name] * factor).astype(out[name].dtype)
    return out
```

```python
import numpy as np
import concourse.bass as bass
from concourse import mybir
from contextlib import ExitStack

P = 128
D = 256
KT = D // P
NSEQ, SEQ = 32, 64
CHUNKS = 4
NB = NSEQ // CHUNKS
TOK = NB * SEQ
NT = TOK // P
HF = 4 * D
MT = HF // P
EPS = 1e-5
H0 = 16
HG = 8
H2 = 16
KX = SEQ + 1
SLOT = SEQ + 1
S8 = 8
HL1 = P // S8
FS = [1, 0, 2, 3, 4]
NEG_BIG = float(np.finfo(np.float32).max)

COL2 = ["L0_ln1_s", "L0_ln1_b", "L0_bq_s", "L0_bk_s", "L0_ln2_s", "L0_ln2_b", "L0_b_q", "L0_bk_c",
        "L0_ln3_s", "L0_ln3_b", "L1_ln1_w", "L1_ln1_b", "L1_ln2_w", "L1_ln2_b", "L1_maa_x",
        "L1_st0", "L1_st1", "L1_st2", "L1_st3", "L1_st4", "L1_time_decay", "L1_u", "L1_gn_w",
        "L1_gn_b", "L1_fmk", "L1_fmr", "L2_ln1_s", "L2_ln1_b", "L2_ln2_s", "L2_ln2_b",
        "L2_lnm_s", "L2_lnm_b", "L3_ln1_w", "L3_ln1_b", "L3_q_b", "L3_k_b", "L3_ln2_w", "L3_ln2_b"]
COL8 = ["L0_b1", "L2_bf1", "L3_fcb"]
COL16 = ["L2_bq1", "L2_bk1", "L2_bik1", "L2_biv1", "L2_bq2", "L2_bk2", "L2_bik2", "L2_biv2"]
COL = {}
_at = 0
for _names, _w in ((COL2, KT), (COL8, MT), (COL16, H2)):
    for _n in _names:
        COL[_n] = _at
        _at += _w
NCOL = _at
ROWS = ["L0_bv_s", "L0_b_ao", "L0_bv_c", "L0_b_co", "L0_b2", "L2_bo1", "L2_bo2", "L2_bf2",
        "L3_v_b", "L3_cb", "L3_pb"]
CONSTS = [("ident", P), ("sel", S8 * P), ("headmask", HG), ("ones2", 32), ("heads8", HL1), ("block8", P)]
CAT = {}
_at = 0
for _n, _w in CONSTS:
    CAT[_n] = (_at, _w)
    _at += _w
NCONST = _at
WRES = [("L0_qkv", KT * 3 * D), ("L0_ao", KT * D), ("L0_q", KT * D), ("L0_kv", KT * 2 * D), ("L0_co", KT * D),
        ("L1_m1", KT * 160), ("L1_m2a", D), ("L1_m2b", D), ("L1_td1", KT * 64), ("L1_td2", D),
        ("L1_W", 8 * KT * D), ("L3_qkv", 3 * KT * D), ("L3_c", KT * D)]
WAT = {}
_at = 0
for _n, _w in WRES:
    WAT[_n] = (_at, _w)
    _at += _w
NWRES = _at


def build(nc, t_x, t_ctx, t_state, t_ltor, t_cross, t_bmask, t_cols, t_rows, t_consts, t_wres, t_mlp,
          t_w2, t_b2, t_wo2, t_out):
    f32 = mybir.dt.float32
    ALU = mybir.AluOpType
    ACT = mybir.ActivationFunctionType
    AX = mybir.AxisListType.X
    ctx = ExitStack()
    with ctx:
        def sb(name, cols, dt=f32):
            return ctx.enter_context(nc.sbuf_tensor(name, [P, cols], dt))[:, :]

        def view(ap, pat, **kw):
            return ap.rearrange(pat, **kw)

        cols = sb("cols", NCOL)
        rows = view(sb("rows", len(ROWS) * D), "p (r d) -> p r d", d=D)
        consts = sb("consts", NCONST)
        wres = sb("wres", NWRES)
        mlp_w = sb("mlp_w", KT * HF + MT * D)
        X = view(sb("X", NT * D), "p (t d) -> p t d", d=D)
        xn = view(sb("xn", NT * D), "p (t d) -> p t d", d=D)
        ctxT = view(sb("ctxT", KT * TOK), "p (k n) -> p k n", k=KT)
        hT = view(sb("hT", KT * TOK), "p (k n) -> p k n", k=KT)
        qT = view(sb("qT", KT * TOK), "p (k n) -> p k n", k=KT)
        kT = view(sb("kT", KT * TOK), "p (k n) -> p k n", k=KT)
        aT = view(sb("aT", KT * TOK), "p (k n) -> p k n", k=KT)
        vbd = view(sb("vbd", NB * 8 * 32), "p (b h c) -> p b h c", b=NB, h=8)
        pbd = view(sb("pbd", 2 * NT * P), "p (s t k) -> p s t k", s=2, t=NT)
        w2ring = view(sb("w2ring", 3 * 3 * KT * P), "p (s w) -> p s w", s=3)
        b2ring = view(sb("b2ring", 3 * 2 * P), "p (s w d) -> p s w d", s=3, w=2)
        dbv = view(sb("dbv", 2 * P), "p (s d) -> p s d", s=2)
        m_self = sb("m_self", SEQ)
        m_cross = view(sb("m_cross", NT * SEQ), "p (t k) -> p t k", t=NT)
        m_key8 = view(sb("m_key8", NT * SEQ, mybir.dt.uint8), "p (t k) -> p t k", t=NT)
        m_key = view(sb("m_key", NT * SEQ), "p (t k) -> p t k", t=NT)
        a_self = sb("a_self", SEQ)
        a_cross = view(sb("a_cross", NT * SEQ), "p (t k) -> p t k", t=NT)
        a_key = view(sb("a_key", NT * SEQ), "p (t k) -> p t k", t=NT)
        s0 = view(sb("s0", KT * NB * S8), "p (k b j) -> p k b j", k=KT, b=NB)
        bst = view(sb("bst", NT * 6), "p (t s) -> p t s", t=NT)
        mv = view(sb("mv", NT * 2), "p (t s) -> p t s", t=NT)
        rstd = sb("rstd", NT)
        neghalf = sb("neghalf", 1)
        nmax = view(sb("nmax", 4 * HG), "p (s h) -> p s h", s=4)
        small = sb("small", 4 * 64)
        ARENA = 17000
        arena = sb("arena", ARENA)
        used = {}

        def carve(layer, n):
            at = used.get(layer, 0)
            used[layer] = at + n
            assert used[layer] <= ARENA, (layer, used[layer])
            return arena[:, at:at + n]

        kbd = view(carve("att", KT * HG * TOK), "p (g h n) -> p g h n", g=KT, h=HG)
        T = view(carve("att", 4 * TOK), "p (s h k) -> p s h k", s=4, h=HG)
        PTs = view(carve("att", 2 * TOK), "p (s h q) -> p s h q", s=2, h=4)
        rden = view(carve("att", 2 * P), "p (s q) -> p s q", s=2)
        ctx_tok = view(carve("att", NT * D), "p (t d) -> p t d", t=NT)
        gT = view(carve("mlp", MT * TOK), "p (m n) -> p m n", m=MT)
        sxT = view(carve("l1", KT * TOK), "p (k n) -> p k n", k=KT)
        xm = view(carve("l1", 2 * KT * TOK), "p (s k n) -> p s k n", s=2, k=KT)
        zA = carve("l1", TOK)
        zB = carve("l1", TOK)
        tw = carve("l1", TOK)
        dtmp = view(carve("l1", KT * TOK), "p (k n) -> p k n", k=KT)
        wdec = view(carve("l1", KT * NB * SLOT), "p (k n) -> p k n", k=KT)
        vT = view(carve("l1", KT * TOK), "p (k n) -> p k n", k=KT)
        gateT = view(carve("l1", KT * TOK), "p (k n) -> p k n", k=KT)
        rku = view(carve("l1", KT * TOK), "p (k n) -> p k n", k=KT)
        kvA = view(carve("l1", 3 * NB * SLOT), "p (s n) -> p s n", s=3)
        stS = view(carve("l1", 3 * NB * SLOT), "p (s n) -> p s n", s=3)
        rsZ = view(carve("l1", 3 * TOK), "p (s n) -> p s n", s=3)
        q2 = view(carve("l2", 2 * TOK), "p (s n) -> p s n", s=2)
        k2 = view(carve("l2", 2 * NB * KX), "p (s b k) -> p s b k", s=2, b=NB)
        v2 = view(carve("l2", 2 * TOK), "p (s t d) -> p s t d", s=2, t=NT)
        E2 = view(carve("l2", 2 * NT * KX), "p (s t k) -> p s t k", s=2, t=NT)
        PT2 = view(carve("l2", 2 * TOK), "p (s t q) -> p s t q", s=2, t=NT)
        c2T = view(carve("l2", H2 * TOK), "p (h n) -> p h n", h=H2)
        wo2 = view(carve("l2", H2 * D), "p (h d) -> p h d", h=H2)

        bank = [ctx.enter_context(nc.psum_tensor(f"bank{i}", [P, 512], f32)) for i in range(8)]
        RING = 6

        def col(name, k=0):
            return cols[:, COL[name] + k:COL[name] + k + 1]

        def row(name):
            return rows[:, ROWS.index(name), :]

        def const(name):
            a, w = CAT[name]
            return consts[:, a:a + w]

        def weight(name, k=KT):
            a, w = WAT[name]
            return view(wres[:, a:a + w], "p (k n) -> p k n", k=k)

        ident = const("ident")
        sel = view(const("sel"), "p (j c) -> p j c", j=S8)
        hmask = const("headmask")
        w1 = view(mlp_w[:, 0:KT * HF], "p (k n) -> p k n", k=KT)
        w2 = view(mlp_w[:, KT * HF:], "p (m n) -> p m n", m=MT)
        l1w = view(weight("L1_W", 1)[:, 0, :], "p (w k n) -> p w k n", w=8, k=KT)

        def sem(name):
            return ctx.enter_context(nc.semaphore(name))

        s_small, s_wl0, s_wl1, s_wl3, s_once = map(sem, ("vectors_in", "w_l0_in", "w_l1_in", "w_l3_in", "preset"))
        names = """x_in ctx_in state_in mask_in mlp_in wo_in w2_in0 w2_in1 w2_in2 out_done
            masks_ready slots_zero ctx_tp ctxT_ready
            dve_step pool_step act_step
            ln_mv ln_rstd ln_xn ln_tp ln_hT x_biased x_updated
            qk_mm qk_T kbd_dve kbd_pool v_mm v_bd att_scores att_scaled att_masked att_max att_sub att_exp
            att_tp att_PT att_pv att_out proj_mm
            mlp_up_mm mlp_act
            l1_sx l1_xm0 l1_z_mm l1_z l1_y_mm l1_y l1_xm l1_td_mm l1_td l1_dec_mm l1_dec l1_rkvg_mm l1_rkvg
            l1_rku l1_rku_mm l1_uv l1_vb l1_kv l1_slot l1_state l1_rs l1_rs_used l1_og l1_cent l1_sq l1_var l1_rs_gn
            l1_gn l1_gn_tp l1_gn_T l1_gated l1_sx2 l1_x2 l1_ffk_mm l1_relu l1_kk l1_rr_mm l1_rr
            l2_dbv l2_q_mm l2_q l2_k_mm l2_k l2_kb l2_v_mm l2_v l2_scores l2_max l2_sub l2_exp l2_prob_a
            l2_prob_b l2_rden l2_tp l2_PT l2_pv l2_c""".split()
        loop_sems = [sem(n) for n in names]
        S = dict(zip(names, loop_sems))
        nums = [s.num for s in loop_sems]
        assert nums == list(range(nums[0], nums[0] + len(nums)))

        with nc.Block() as block:
            @block.sync
            def _(sp):
                sp.dma_start(consts, t_consts).then_inc(s_small, 16)
                sp.dma_start(cols, t_cols).then_inc(s_small, 16)
                sp.dma_start(m_self[0:SEQ, :], t_ltor).then_inc(s_small, 16)
                sp.dma_start(m_self[SEQ:P, :], t_ltor).then_inc(s_small, 16)
                sp.dma_start(rows.rearrange("p r d -> p (r d)"), t_rows.partition_broadcast(P)).then_inc(s_small, 16)
                for s, first, last in ((s_wl0, "L0_qkv", "L0_co"), (s_wl1, "L1_m1", "L1_W"), (s_wl3, "L3_qkv", "L3_c")):
                    a, b = WAT[first][0], WAT[last][0] + WAT[last][1]
                    sp.dma_start(wres[:, a:b], t_wres[:, a:b]).then_inc(s, 16)

            @block.gpsimd
            def _(pool):
                nc.gpsimd.memset(neghalf, -0.5).then_inc(s_once, 1)
                nc.gpsimd.memset(vbd, 0.0).then_inc(s_once, 1)
                nc.gpsimd.memset(pbd, 0.0).then_inc(s_once, 1)
        SMALL, ONCE = 5 * 16, 3

        with nc.Fori(0, CHUNKS) as chunk:
            with nc.Block() as block:

                ring = {"n": 0, "freed": [None] * RING, "at": {}}

                def take(pe, tag, stage, n):
                    i = ring["n"] % RING
                    ring["n"] += 1
                    if ring["freed"][i]:
                        pe.wait_ge(S[ring["freed"][i][0]], ring["freed"][i][1])
                    ring["freed"][i] = (stage, n)
                    ring["at"][tag] = i
                    return bank[i]

                def held(tag):
                    return bank[ring["at"][tag]]

                @block.tensor
                def _(pe):
                    mm = nc.tensor.matmul

                    def transposes(tag, src, need, tp, used_by, n_used):
                        for k in range(KT):
                            b = take(pe, (tag, k), used_by, n_used + k + 1)
                            for t in range(NT):
                                need(t)
                                last = nc.tensor.transpose(b[:, t * P:(t + 1) * P], src[:, t, k * P:(k + 1) * P], ident)
                            last.then_inc(S[tp], 1)

                    def norm(L):
                        transposes(("ln", L), xn, lambda t: pe.wait_ge(S["ln_xn"], NT * L + t + 1), "ln_tp", "ln_hT", KT * L)

                    def linear(tag, w, src, m0, signal, used_by, n, rows_out=P):
                        b = take(pe, tag, used_by, n)
                        for k in range(w.shape[1]):
                            last = mm(b[0:rows_out, :], w[:, k, m0:m0 + rows_out], src[:, k, :],
                                      start=(k == 0), stop=(k == w.shape[1] - 1))
                        last.then_inc(S[signal], 1)

                    def out_proj(site, w, src, nk, before):
                        for t in range(NT):
                            before(t)
                            b = take(pe, ("proj", site, t), "x_updated", NT * site + t + 1)
                            for k in range(nk):
                                last = mm(b[:, 0:D], src[:, k, t * P:(t + 1) * P], w[:, k, :],
                                          start=(k == 0), stop=(k == nk - 1))
                            last.then_inc(S["proj_mm"], 1)

                    def attention(a, site, wq, wk, wv, kv_src, w_out):
                        for i, (w, src) in enumerate(((wq, hT), (wq, hT), (wk, kv_src), (wk, kv_src))):
                            linear(("qk", a, i), w, src, (i % KT) * P, "qk_mm", "qk_T", 4 * a + i + 1)
                        for g in range(NT // 2):
                            b = take(pe, ("v", a, g), "v_bd", 8 * a + 4 * (g + 1))
                            for i in range(2):
                                t = 2 * g + i
                                for k in range(KT):
                                    last = mm(b[:, i * D:(i + 1) * D], kv_src[:, k, t * P:(t + 1) * P], wv[:, k, :],
                                              start=(k == 0), stop=(k == KT - 1))
                            last.then_inc(S["v_mm"], 1)
                        U = KT * NT
                        for s in range(U + 3):
                            if s < U:
                                g, t, n = s // NT, s % NT, U * a + s
                                if t == 0:
                                    pe.wait_ge(S["qk_T"], 4 * a + 4)
                                    pe.wait_ge(S[("kbd_dve", "kbd_pool")[g]], HG * (a + 1))
                                b = take(pe, ("s", n), "att_scaled", n + 1)
                                for h in range(2):
                                    q0 = t * P + h * SEQ
                                    last = mm(b[h * SEQ:(h + 1) * SEQ, :], qT[:, g, q0:q0 + SEQ], kbd[:, g, :, q0:q0 + SEQ],
                                              start=True, stop=True)
                                last.then_inc(S["att_scores"], 1)
                            if 2 <= s < U + 2:
                                n = U * a + s - 2
                                pe.wait_ge(S["att_exp"], n + 1)
                                b = take(pe, ("tp", n), "att_PT", n + 1)
                                for h in range(4):
                                    last = nc.tensor.transpose(b[:, h * P:(h + 1) * P],
                                                               T[:, n % 4, 2 * h:2 * h + 2, :].rearrange("p h k -> p (h k)"), ident)
                                last.then_inc(S["att_tp"], 1)
                            if s >= 3:
                                u = s - 3
                                g, t, n = u // NT, u % NT, U * a + u
                                pe.wait_ge(S["att_PT"], n + 1)
                                if u == 0:
                                    pe.wait_ge(S["v_bd"], 8 * (a + 1))
                                b = take(pe, ("pv", n), "att_out", n + 1)
                                for h in range(4):
                                    o = slice(32 * h, 32 * h + 32)
                                    for half in range(2):
                                        mm(b[o, half * SEQ:(half + 1) * SEQ], vbd[:, 2 * t + half, 4 * g + h, :],
                                           PTs[:, n % 2, h, half * SEQ:(half + 1) * SEQ], start=True, stop=True,
                                           tile_position=(0, 32 * h))
                                    last = mm(b[o, P:2 * P], const("ones2"), PTs[:, n % 2, h, :], start=True, stop=True,
                                              tile_position=(0, 32 * h))
                                last.then_inc(S["att_pv"], 1)
                        out_proj(site, w_out, aT, KT, lambda t: pe.wait_ge(S["att_out"], U * a + NT + t + 1))

                    def mlp(m, L, site):
                        pe.wait_ge(S["mlp_in"], 16 * (m + 1))
                        pe.wait_ge(S["ln_hT"], KT * (L + 1))
                        for i in range(MT):
                            linear(("mlp", m, i), w1, hT, i * P, "mlp_up_mm", "mlp_act", MT * m + i + 1)
                        pe.wait_ge(S["mlp_act"], MT * (m + 1))
                        out_proj(site, w2, gT, MT, lambda t: None)

                    pe.wait_ge(s_small, SMALL)
                    pe.wait_ge(S["ctx_in"], 16)
                    transposes("ctx", ctx_tok, lambda t: None, "ctx_tp", "ctxT_ready", 0)
                    norm(0)
                    pe.wait_ge(s_wl0, 16)
                    pe.wait_ge(S["ln_hT"], KT)
                    pe.wait_ge(s_once, ONCE)
                    qkv = weight("L0_qkv")
                    attention(0, 0, qkv[:, :, 0:D], qkv[:, :, D:2 * D], qkv[:, :, 2 * D:3 * D], hT, weight("L0_ao"))
                    norm(1)
                    pe.wait_ge(S["ln_hT"], 2 * KT)
                    pe.wait_ge(S["ctxT_ready"], KT)
                    kv = weight("L0_kv")
                    attention(1, 1, weight("L0_q"), kv[:, :, 0:D], kv[:, :, D:2 * D], ctxT, weight("L0_co"))
                    norm(2)
                    mlp(0, 2, 2)
                    norm(3)
                    pe.wait_ge(s_wl1, 16)
                    m1 = weight("L1_m1")
                    pe.wait_ge(S["l1_xm0"], KT)
                    linear("z0", m1, xm[:, 1], 0, "l1_z_mm", "l1_z", 1)
                    linear("z1", m1, xm[:, 1], P, "l1_z_mm", "l1_z", 2, rows_out=32)
                    pe.wait_ge(S["l1_z"], 2)

                    def l1_y(f):
                        i = FS.index(f)
                        for c in range(KT):
                            b = take(pe, ("y", i, c), "l1_y", KT * i + c + 1)
                            if f < 4:
                                w, z = weight("L1_m2a", 1)[32 * f:32 * f + 32, 0], zA[32 * f:32 * f + 32, :]
                            else:
                                w, z = weight("L1_m2b", 1)[0:32, 0], zB[0:32, :]
                            mm(b[:, :], w[:, c * P:(c + 1) * P], z, start=True, stop=True,
                               tile_position=(32 * (f % 4), 0)).then_inc(S["l1_y_mm"], 1)

                    def l1_use(i):
                        f, x = FS[i], xm[:, i % 2]
                        pe.wait_ge(S["l1_xm"], KT * (i + 1))
                        if f == 1:
                            linear("td", weight("L1_td1"), x, 0, "l1_td_mm", "l1_td", 1, rows_out=64)
                        else:
                            for c in range(KT):
                                n = KT * (i - 1) + c
                                linear(("rkvg", n), l1w[:, {3: 0, 0: 1, 2: 2, 4: 3}[f]], x, c * P, "l1_rkvg_mm", "l1_rkvg", n + 1)

                    l1_y(FS[0])
                    for i in range(5):
                        if i < 4:
                            l1_y(FS[i + 1])
                        l1_use(i)
                        if i == 1:
                            pe.wait_ge(S["l1_td"], 1)
                            for c in range(KT):
                                b = take(pe, ("dec", c), "l1_dec", 2 * c + 1)
                                mm(b[:, :], weight("L1_td2", 1)[0:64, 0, c * P:(c + 1) * P], tw[0:64, :],
                                   start=True, stop=True).then_inc(S["l1_dec_mm"], 1)
                    for c in range(KT):
                        pe.wait_ge(S["l1_rku"], c + 1)
                        b = take(pe, ("rku", c), "l1_uv", c + 1)
                        mm(b[:, :], const("block8"), rku[:, c, :], start=True, stop=True).then_inc(S["l1_rku_mm"], 1)

                    def l1_sum(n):
                        c, j = n // S8, n % S8
                        pe.wait_ge(S["l1_rs"], n + 1)
                        for t in range(NT):
                            last = mm(bank[6 + t // 2][:, (t % 2) * D + c * P + j:(t % 2) * D + (c + 1) * P:S8],
                                      rsZ[:, n % 3, t * P:(t + 1) * P], const("heads8"), start=False,
                                      stop=(n == KT * S8 - 1 and t % 2 == 1), skip_group_check=True)
                        last.then_inc(S["l1_rs_used"], 1)

                    for n in range(KT * S8 + 3):
                        if n < KT * S8:
                            c, j = n // S8, n % S8
                            if n == 0:
                                pe.wait_ge(S["l1_rkvg"], 2 * KT)
                            b = take(pe, ("vb", n), "l1_kv", n + 1)
                            mm(b[:, :], sel[:, j, :], vT[:, c, :], start=True, stop=True).then_inc(S["l1_vb"], 1)
                        if n == 2:
                            pe.wait_ge(S["l1_uv"], KT)
                            for t in range(NT):
                                for c in range(KT):
                                    mm(bank[6 + t // 2][:, (t % 2) * D + c * P:(t % 2) * D + (c + 1) * P],
                                       rku[:, c, t * P:(t + 1) * P], ident, start=(t % 2 == 0 and c == 0), stop=False,
                                       skip_group_check=True)
                        if n >= 3:
                            l1_sum(n - 3)
                    transposes("gn", xn, lambda t: pe.wait_ge(S["l1_gn"], t // 2 + 1), "l1_gn_tp", "l1_gn_T", 0)
                    pe.wait_ge(S["l1_gated"], KT)
                    out_proj(3, l1w[:, 4], aT, KT, lambda t: None)
                    norm(4)
                    pe.wait_ge(S["l1_x2"], KT)
                    for c in range(KT):
                        linear(("ffk", c), l1w[:, 5], xm[:, 0], c * P, "l1_ffk_mm", "l1_relu", c + 1)
                    pe.wait_ge(S["l1_x2"], 2 * KT)
                    for t in range(NT):
                        b = take(pe, ("rr", t), "l1_rr", t + 1)
                        for k in range(KT):
                            last = mm(b[:, 0:D], xm[:, 1, k, t * P:(t + 1) * P], l1w[:, 6, k, :], start=(k == 0), stop=(k == KT - 1))
                        last.then_inc(S["l1_rr_mm"], 1)
                    pe.wait_ge(S["l1_kk"], KT)
                    out_proj(4, l1w[:, 7], aT, KT, lambda t: None)

                    def cross2(z, L, site):
                        def project(h):
                            n = H2 * z + h
                            w = w2ring[:, n % 3, :].rearrange("p (w k d) -> p w k d", w=3, k=KT)
                            pe.wait_ge(S[f"w2_in{n % 3}"], 32 * (n // 3 + 1))
                            if h == 0:
                                pe.wait_ge(S["ln_hT"], KT * (L + 1))
                            linear(("q2", n), w[:, 0], hT, 0, "l2_q_mm", "l2_q", n + 1)
                            linear(("k2", n), w[:, 1], ctxT, 0, "l2_k_mm", "l2_k", n + 1)
                            b = take(pe, ("v2", n), "l2_v", n + 1)
                            for t in range(NT):
                                for k in range(KT):
                                    last = mm(b[:, t * P:(t + 1) * P], ctxT[:, k, t * P:(t + 1) * P], w[:, 2, k, :],
                                              start=(k == 0), stop=(k == KT - 1))
                            last.then_inc(S["l2_v_mm"], 1)

                        def scores(h):
                            n = H2 * z + h
                            pe.wait_ge(S["l2_q"], n + 1)
                            pe.wait_ge(S["l2_k"], n + 1)
                            pe.wait_ge(S["l2_kb"], n + 1)
                            b = take(pe, ("s2", n), "l2_sub", n + 1)
                            for t in range(NT):
                                for half in range(2):
                                    q0 = t * P + half * SEQ
                                    last = mm(b[half * SEQ:(half + 1) * SEQ, t * KX:(t + 1) * KX], q2[:, n % 2, q0:q0 + SEQ],
                                              k2[:, n % 2, 2 * t + half, :], start=True, stop=True)
                            last.then_inc(S["l2_scores"], 1)

                        def turn(h):
                            n = H2 * z + h
                            pe.wait_ge(S["l2_prob_a"], n + 1)
                            pe.wait_ge(S["l2_prob_b"], n + 1)
                            b = take(pe, ("tp2", n), "l2_PT", n + 1)
                            for t in range(NT):
                                last = nc.tensor.transpose(b[:, t * P:(t + 1) * P], pbd[:, n % 2, t, :], ident)
                            last.then_inc(S["l2_tp"], 1)

                        def weigh(h):
                            n = H2 * z + h
                            pe.wait_ge(S["l2_PT"], n + 1)
                            pe.wait_ge(S["l2_v"], n + 1)
                            b = take(pe, ("pv2", n), "l2_c", n + 1)
                            for t in range(NT):
                                last = mm(b[:, t * P:(t + 1) * P], v2[:, n % 2, t, :], PT2[:, n % 2, t, :], start=True, stop=True)
                            last.then_inc(S["l2_pv"], 1)

                        project(0)
                        for h in range(H2):
                            scores(h)
                            if h >= 1:
                                weigh(h - 1)
                            if h + 1 < H2:
                                project(h + 1)
                            turn(h)
                        weigh(H2 - 1)
                        pe.wait_ge(S["wo_in"], 16 * (z + 1))
                        pe.wait_ge(S["l2_c"], H2 * (z + 1))
                        out_proj(site, wo2, c2T, H2, lambda t: None)

                    norm(5)
                    cross2(0, 5, 5)
                    norm(6)
                    cross2(1, 6, 6)
                    norm(7)
                    mlp(1, 7, 7)
                    norm(8)
                    pe.wait_ge(s_wl3, 16)
                    pe.wait_ge(S["ln_hT"], 9 * KT)
                    w3 = weight("L3_qkv", 1)[:, 0, :].rearrange("p (w k n) -> p w k n", w=3, k=KT)
                    attention(2, 8, w3[:, 0], w3[:, 1], w3[:, 2], ctxT, weight("L3_c"))
                    norm(9)
                    mlp(2, 9, 9)

                @block.scalar
                def _(act):
                    A = nc.scalar.activation

                    def norm(L, s, b):
                        for k in range(KT):
                            act.wait_ge(S["ln_tp"], KT * L + k + 1)
                            A(hT[:, k, :], held((("ln", L), k))[:, :], ACT.Identity, bias=col(b, k), scale=col(s, k)).then_inc(S["ln_hT"], 1)

                    def attention(a, bq, bk):
                        for i in range(4):
                            act.wait_ge(S["qk_mm"], 4 * a + i + 1)
                            out, b = (qT, bq) if i < KT else (kT, bk)
                            A(out[:, i % KT, :], held(("qk", a, i))[:, :], ACT.Identity, bias=col(b, i % KT)).then_inc(S["qk_T"], 1)
                        U = KT * NT
                        for s in range(1, U + 2):
                            if s - 1 < U:
                                n = U * a + s - 1
                                act.wait_ge(S["att_sub"], n + 1)
                                A(T[:, n % 4], T[:, n % 4], ACT.Exp).then_inc(S["att_exp"], 1)
                            if s >= 2:
                                n = U * a + s - 2
                                act.wait_ge(S["att_tp"], n + 1)
                                if n % U >= 2:
                                    act.wait_ge(S["att_pv"], n - 1)
                                A(PTs[:, n % 2].rearrange("p h q -> p (h q)"), held(("tp", n))[:, :], ACT.Copy).then_inc(S["att_PT"], 1)

                    def mlp(m, bias, func):
                        for i in range(MT):
                            act.wait_ge(S["mlp_up_mm"], MT * m + i + 1)
                            A(gT[:, i, :], held(("mlp", m, i))[:, :], func, bias=col(bias, i)).then_inc(S["mlp_act"], 1)

                    act.wait_ge(s_small, SMALL)
                    for k in range(KT):
                        act.wait_ge(S["ctx_tp"], k + 1)
                        A(ctxT[:, k, :], held(("ctx", k))[:, :], ACT.Copy).then_inc(S["ctxT_ready"], 1)
                    norm(0, "L0_ln1_s", "L0_ln1_b")
                    attention(0, "L0_bq_s", "L0_bk_s")
                    norm(1, "L0_ln2_s", "L0_ln2_b")
                    attention(1, "L0_b_q", "L0_bk_c")
                    norm(2, "L0_ln3_s", "L0_ln3_b")
                    mlp(0, "L0_b1", ACT.Gelu_apprx_tanh)
                    norm(3, "L1_ln1_w", "L1_ln1_b")
                    for i, z in enumerate((zA, zB)):
                        act.wait_ge(S["l1_z_mm"], i + 1)
                        r = P if i == 0 else 32
                        A(z[0:r, :], held(f"z{i}")[0:r, :], ACT.Tanh).then_inc(S["l1_z"], 1)
                    act.wait_ge(S["l1_td_mm"], 1)
                    A(tw[0:64, :], held("td")[0:64, :], ACT.Tanh).then_inc(S["l1_td"], 1)

                    def rkvg(i, out, func):
                        for c in range(KT):
                            n = KT * (i - 1) + c
                            act.wait_ge(S["l1_rkvg_mm"], n + 1)
                            A(out[:, c, :], held(("rkvg", n))[:, :], func).then_inc(S["l1_rkvg"], 1)

                    rkvg(1, kT, ACT.Copy)
                    for c in range(KT):
                        act.wait_ge(S["l1_dec_mm"], c + 1)
                        A(dtmp[:, c, :], held(("dec", c))[:, :], ACT.Exp, bias=col("L1_time_decay", c)).then_inc(S["l1_dec"], 1)
                        act.wait_ge(S["l1_dec"], 2 * c + 1)
                        A(wdec[:, c, :].rearrange("p (b s) -> p b s", s=SLOT)[:, :, 1:SLOT],
                          dtmp[:, c, :].rearrange("p (b s) -> p b s", s=SEQ), ACT.Exp, scale=-1.0).then_inc(S["l1_dec"], 1)
                    rkvg(2, vT, ACT.Copy)
                    rkvg(3, qT, ACT.Copy)
                    rkvg(4, gateT, ACT.Silu)
                    for g in range(2):
                        act.wait_ge(S["l1_cent"], g + 1)
                        A(rsZ[:, g, :], xn[:, 2 * g:2 * g + 2, :].rearrange("p t d -> p (t d)"), ACT.Square).then_inc(S["l1_sq"], 1)
                    for c in range(KT):
                        act.wait_ge(S["l1_gn_tp"], c + 1)
                        A(dtmp[:, c, :], held(("gn", c))[:, :], ACT.Identity, bias=col("L1_gn_b", c), scale=col("L1_gn_w", c)).then_inc(S["l1_gn_T"], 1)
                    norm(4, "L1_ln2_w", "L1_ln2_b")
                    for c in range(KT):
                        act.wait_ge(S["l1_ffk_mm"], c + 1)
                        A(dtmp[:, c, :], held(("ffk", c))[:, :], ACT.Relu).then_inc(S["l1_relu"], 1)
                    for t in range(NT):
                        act.wait_ge(S["l1_rr_mm"], t + 1)
                        A(gateT[:, t // 2, (t % 2) * D:(t % 2 + 1) * D], held(("rr", t))[:, 0:D], ACT.Sigmoid).then_inc(S["l1_rr"], 1)

                    def cross2(z, bq, bk):
                        def qk(h):
                            n = H2 * z + h
                            act.wait_ge(S["l2_q_mm"], n + 1)
                            if n >= 2:
                                act.wait_ge(S["l2_scores"], n - 1)
                            A(q2[:, n % 2, :], held(("q2", n))[:, :], ACT.Identity, bias=col(bq, h)).then_inc(S["l2_q"], 1)
                            act.wait_ge(S["l2_k_mm"], n + 1)
                            A(k2[:, n % 2, :, 0:SEQ], held(("k2", n))[:, :].rearrange("p (b k) -> p b k", b=NB), ACT.Identity,
                              bias=col(bk, h)).then_inc(S["l2_k"], 1)

                        qk(0)
                        for h in range(H2):
                            n = H2 * z + h
                            act.wait_ge(S["l2_sub"], n + 1)
                            A(E2[:, n % 2], E2[:, n % 2], ACT.Exp, scale=float(P) ** -0.5).then_inc(S["l2_exp"], 1)
                            if h + 1 < H2:
                                qk(h + 1)
                            act.wait_ge(S["l2_tp"], n + 1)
                            if n >= 2:
                                act.wait_ge(S["l2_pv"], n - 1)
                            A(PT2[:, n % 2].rearrange("p t q -> p (t q)"), held(("tp2", n))[:, :], ACT.Copy).then_inc(S["l2_PT"], 1)

                    norm(5, "L2_ln1_s", "L2_ln1_b")
                    cross2(0, "L2_bq1", "L2_bk1")
                    norm(6, "L2_ln2_s", "L2_ln2_b")
                    cross2(1, "L2_bq2", "L2_bk2")
                    norm(7, "L2_lnm_s", "L2_lnm_b")
                    mlp(1, "L2_bf1", ACT.Gelu)
                    norm(8, "L3_ln1_w", "L3_ln1_b")
                    attention(2, "L3_q_b", "L3_k_b")
                    norm(9, "L3_ln2_w", "L3_ln2_b")
                    mlp(2, "L3_fcb", ACT.Gelu_apprx_tanh)

                @block.vector
                def _(dve):
                    V = nc.vector
                    steps = [0]

                    def settle(ins):
                        steps[0] += 1
                        ins.then_inc(S["dve_step"], 1)
                        dve.wait_ge(S["dve_step"], steps[0])

                    def norm(L):
                        if L:
                            dve.wait_ge(S["x_updated"], NT * L)
                        for t in range(NT):
                            last = V.bn_stats(bst[:, t, :], X[:, t, :])
                        settle(last)
                        for t in range(NT):
                            last = V.bn_aggr(mv[:, t, :], bst[:, t, :])
                        last.then_inc(S["ln_mv"], 1)
                        dve.wait_ge(S["ln_mv"], L + 1)
                        dve.wait_ge(S["ln_rstd"], L + 1)
                        for t in range(NT):
                            V.tensor_scalar(xn[:, t, :], X[:, t, :], mv[:, t, 0:1], rstd[:, t:t + 1], ALU.subtract, ALU.mult)\
                                .then_inc(S["ln_xn"], 1)

                    def residual(site, biased):
                        for t in range(NT):
                            dve.wait_ge(S["proj_mm"], NT * site + t + 1)
                            if biased is not None:
                                dve.wait_ge(S["x_biased"], biased + 1)
                            V.tensor_tensor(X[:, t, :], X[:, t, :], held(("proj", site, t))[:, 0:D], ALU.add).then_inc(S["x_updated"], 1)

                    def attention(a, site, biased, bv, mult):
                        dve.wait_ge(S["qk_T"], 4 * a + 3)
                        for h in range(HG):
                            V.tensor_scalar(kbd[:, 0, h, :], kT[:, 0, :], hmask[:, h:h + 1], None, ALU.mult).then_inc(S["kbd_dve"], 1)
                        for g in range(NT // 2):
                            dve.wait_ge(S["v_mm"], 2 * a + g + 1)
                            for half in range(2):
                                for par in range(2):
                                    src = held(("v", a, g))[half * SEQ:(half + 1) * SEQ, :].rearrange(
                                        "p (t h r d) -> p t h r d", t=2, h=8, r=2)[:, :, :, par, :]
                                    brow = row(bv)[half * SEQ:(half + 1) * SEQ, :].rearrange(
                                        "p (h r d) -> p h r d", h=8, r=2)[:, :, par, :].unsqueeze(1).to_broadcast([SEQ, 2, 8, 16])
                                    dst = vbd[par * SEQ:(par + 1) * SEQ, 4 * g + half:4 * g + half + 3:2, :, par * 16:(par + 1) * 16]
                                    V.tensor_tensor(dst, src, brow, ALU.add).then_inc(S["v_bd"], 1)
                        U = KT * NT
                        for s in range(U + 3):
                            if s < U:
                                n, t = U * a + s, s % NT
                                dve.wait_ge(S["att_scores"], n + 1)
                                if s >= 4:
                                    dve.wait_ge(S["att_tp"], n - 3)
                                if s == 0:
                                    dve.wait_ge(S["masks_ready"], 3)
                                m = mult(t).unsqueeze(1).to_broadcast([P, HG, SEQ])
                                V.scalar_tensor_tensor(T[:, n % 4], held(("s", n))[:, :].rearrange("p (h k) -> p h k", h=HG),
                                                       (D // H0) ** -0.5, m, ALU.mult, ALU.mult).then_inc(S["att_scaled"], 1)
                            if 1 <= s <= U:
                                n = U * a + s - 1
                                dve.wait_ge(S["att_masked"], n + 1)
                                V.tensor_reduce(nmax[:, n % 4, :], T[:, n % 4], AX, ALU.max, negate=True).then_inc(S["att_max"], 1)
                            if s >= 3:
                                u = s - 3
                                n, g, t = U * a + u, u // NT, u % NT
                                dve.wait_ge(S["att_pv"], n + 1)
                                b = held(("pv", n))
                                settle(V.reciprocal(rden[:, n % 2, :], b[:, P:2 * P]))
                                V.tensor_tensor(aT[:, g, t * P:(t + 1) * P], b[:, 0:P], rden[:, n % 2, :], ALU.mult).then_inc(S["att_out"], 1)
                        residual(site, biased)

                    norm_no = iter(range(10))
                    dve.wait_ge(s_small, SMALL)
                    dve.wait_ge(s_once, ONCE)
                    dve.wait_ge(S["x_in"], 16)
                    norm(0)
                    attention(0, 0, 0, "L0_bv_s", lambda t: m_self)
                    norm(1)
                    attention(1, 1, 1, "L0_bv_c", lambda t: m_cross[:, t, :])
                    norm(2)
                    residual(2, 2)
                    norm(3)
                    for c in range(KT):
                        dve.wait_ge(S["l1_sx"], 2 * c + 2)
                        dve.wait_ge(S["ln_hT"], 3 * KT + c + 1)
                        V.scalar_tensor_tensor(xm[:, 1, c, :], sxT[:, c, :], col("L1_maa_x", c), hT[:, c, :], ALU.mult, ALU.add)\
                            .then_inc(S["l1_xm0"], 1)
                    for i, f in enumerate(FS):
                        for c in range(KT):
                            dve.wait_ge(S["l1_y_mm"], KT * i + c + 1)
                            if i == 1:
                                dve.wait_ge(S["l1_z_mm"], 2)
                            if i == 2:
                                dve.wait_ge(S["l1_td_mm"], 1)
                            if i > 2:
                                dve.wait_ge(S["l1_rkvg_mm"], KT * (i - 2))
                            V.scalar_tensor_tensor(xm[:, i % 2, c, :], held(("y", i, c))[:, :], col(f"L1_st{f}", c), sxT[:, c, :],
                                                   ALU.add, ALU.mult).then_inc(S["l1_y"], 1)
                    dve.wait_ge(S["l1_rkvg"], 3 * KT)
                    for c in range(KT):
                        V.scalar_tensor_tensor(rku[:, c, :], kT[:, c, :], col("L1_u", c), qT[:, c, :], ALU.mult, ALU.mult)\
                            .then_inc(S["l1_rku"], 1)
                    for c in range(KT):
                        dve.wait_ge(S["l1_rku_mm"], c + 1)
                        V.tensor_tensor(rku[:, c, :], held(("rku", c))[:, :], vT[:, c, :], ALU.mult).then_inc(S["l1_uv"], 1)
                    for n in range(KT * S8 + 1):
                        if n < KT * S8:
                            c = n // S8
                            dve.wait_ge(S["l1_vb"], n + 1)
                            if n >= 3:
                                dve.wait_ge(S["l1_state"], n - 2)
                            V.tensor_tensor(kvA[:, n % 3, :].rearrange("p (b s) -> p b s", s=SLOT)[:, :, 1:SLOT],
                                            held(("vb", n))[:, :].rearrange("p (b s) -> p b s", s=SEQ),
                                            kT[:, c, :].rearrange("p (b s) -> p b s", s=SEQ), ALU.mult).then_inc(S["l1_kv"], 1)
                        if n >= 1:
                            m = n - 1
                            dve.wait_ge(S["l1_slot"], m + 1)
                            dve.wait_ge(S["l1_kv"], m + 1)
                            dve.wait_ge(S["l1_dec"], 4)
                            dve.wait_ge(S["slots_zero"], 1)
                            if m >= 3:
                                dve.wait_ge(S["l1_rs"], m - 2)
                            V.tensor_tensor_scan(stS[:, m % 3, :], wdec[:, m // S8, :], kvA[:, m % 3, :], 0.0, ALU.mult, ALU.add)\
                                .then_inc(S["l1_state"], 1)
                    G = small[:, 0:64]
                    dve.wait_ge(S["l1_rs_used"], KT * S8)
                    for g in range(2):
                        og = bank[6 + g][:, :].rearrange("p (h j) -> p h j", j=S8)
                        xg = xn[:, 2 * g:2 * g + 2, :].rearrange("p t (h j) -> p (t h) j", j=S8)
                        settle(V.tensor_reduce(G, og, AX, ALU.add))
                        V.scalar_tensor_tensor(xg, G.unsqueeze(2).to_broadcast([P, 64, S8]), -1.0 / S8, og, ALU.mult, ALU.add)\
                            .then_inc(S["l1_cent"], 1)
                        dve.wait_ge(S["l1_sq"], g + 1)
                        V.tensor_reduce(small[:, 64 + 64 * g:128 + 64 * g], rsZ[:, g, :].rearrange("p (h j) -> p h j", j=S8), AX, ALU.add)\
                            .then_inc(S["l1_var"], 1)
                    for g in range(2):
                        dve.wait_ge(S["l1_rs_gn"], g + 1)
                        dve.wait_ge(S["l1_cent"], g + 1)
                        xg = xn[:, 2 * g:2 * g + 2, :].rearrange("p t (h j) -> p (t h) j", j=S8)
                        V.tensor_tensor(xg, xg, small[:, 64 + 64 * g:128 + 64 * g].unsqueeze(2).to_broadcast([P, 64, S8]), ALU.mult)\
                            .then_inc(S["l1_gn"], 1)
                    residual(3, None)
                    norm(4)
                    for k, name in enumerate(("L1_fmk", "L1_fmr")):
                        for c in range(KT):
                            dve.wait_ge(S["l1_sx2"], 2 * c + 2)
                            dve.wait_ge(S["ln_hT"], 4 * KT + c + 1)
                            V.scalar_tensor_tensor(xm[:, k, c, :], sxT[:, c, :], col(name, c), hT[:, c, :], ALU.mult, ALU.add)\
                                .then_inc(S["l1_x2"], 1)
                    for t in range(NT):
                        dve.wait_ge(S["proj_mm"], NT * 4 + t + 1)
                        dve.wait_ge(S["l1_rr"], t + 1)
                        tmp = rsZ[:, t // 2, (t % 2) * D:(t % 2 + 1) * D]
                        settle(V.tensor_tensor(tmp, held(("proj", 4, t))[:, 0:D], gateT[:, t // 2, (t % 2) * D:(t % 2 + 1) * D], ALU.mult))
                        V.tensor_tensor(X[:, t, :], X[:, t, :], tmp, ALU.add).then_inc(S["x_updated"], 1)

                    def cross2(z, site, biased, biv):
                        def value(h):
                            n = H2 * z + h
                            dve.wait_ge(S["l2_v_mm"], n + 1)
                            dve.wait_ge(S["l2_dbv"], n + 1)
                            if n >= 2:
                                dve.wait_ge(S["l2_pv"], n - 1)
                            V.tensor_tensor(v2[:, n % 2], held(("v2", n))[:, :].rearrange("p (t d) -> p t d", t=NT),
                                            dbv[:, n % 2, :].unsqueeze(1).to_broadcast([P, NT, P]), ALU.add).then_inc(S["l2_v"], 1)

                        def context(h):
                            n = H2 * z + h
                            dve.wait_ge(S["l2_pv"], n + 1)
                            V.tensor_scalar(c2T[:, h, :], held(("pv2", n))[:, :], col(biv, h), None, ALU.add).then_inc(S["l2_c"], 1)

                        value(0)
                        for h in range(H2):
                            n = H2 * z + h
                            dve.wait_ge(S["l2_scores"], n + 1)
                            s = held(("s2", n))[:, 0:NT * KX].rearrange("p (t k) -> p t k", t=NT)
                            V.tensor_reduce(nmax[:, n % 2, 0:NT], s, AX, ALU.max, negate=True).then_inc(S["l2_max"], 1)
                            dve.wait_ge(S["l2_max"], n + 1)
                            if n >= 2:
                                dve.wait_ge(S["l2_prob_a"], n - 1)
                                dve.wait_ge(S["l2_prob_b"], n - 1)
                            V.tensor_tensor(E2[:, n % 2], s, nmax[:, n % 2, 0:NT].unsqueeze(2).to_broadcast([P, NT, KX]), ALU.add)\
                                .then_inc(S["l2_sub"], 1)
                            if h >= 1:
                                context(h - 1)
                            dve.wait_ge(S["l2_exp"], n + 1)
                            den = small[:, 8 * (n % 2):8 * (n % 2) + 4]
                            rec = small[:, 8 * (n % 2) + 4:8 * (n % 2) + 8]
                            settle(V.tensor_reduce(den, E2[:, n % 2], AX, ALU.add))
                            V.reciprocal(rec, den).then_inc(S["l2_rden"], 1)
                            dve.wait_ge(S["l2_rden"], n + 1)
                            if n >= 2:
                                dve.wait_ge(S["l2_tp"], n - 1)
                            V.tensor_tensor(pbd[0:SEQ, n % 2, :, 0:SEQ], E2[0:SEQ, n % 2, :, 0:SEQ],
                                            rec[0:SEQ, :].unsqueeze(2).to_broadcast([SEQ, NT, SEQ]), ALU.mult).then_inc(S["l2_prob_a"], 1)
                            if h + 1 < H2:
                                value(h + 1)
                        context(H2 - 1)
                        residual(site, biased)

                    norm(5)
                    cross2(0, 5, 3, "L2_biv1")
                    norm(6)
                    cross2(1, 6, 4, "L2_biv2")
                    norm(7)
                    residual(7, 5)
                    norm(8)
                    attention(2, 8, 6, "L3_v_b", lambda t: m_key[:, t, :])
                    norm(9)
                    residual(9, 7)

                @block.gpsimd
                def _(pool):
                    G = nc.gpsimd
                    steps = [0]

                    def settle(ins):
                        steps[0] += 1
                        ins.then_inc(S["pool_step"], 1)
                        pool.wait_ge(S["pool_step"], steps[0])

                    def power(out, var, n, signal):
                        settle(G.tensor_scalar(out, var, 1.0, EPS, ALU.mult, ALU.add))
                        G.tensor_tensor(out, out, neghalf.to_broadcast([P, n]), ALU.pow).then_inc(S[signal], 1)

                    def norm(L):
                        pool.wait_ge(S["ln_mv"], L + 1)
                        if L:
                            pool.wait_ge(S["ln_xn"], NT * L)
                        power(rstd, mv[:, :, 1], NT, "ln_rstd")

                    def bias(L, name):
                        pool.wait_ge(S["ln_xn"], NT * (L + 1))
                        G.tensor_tensor(X, X, row(name).unsqueeze(1).to_broadcast([P, NT, D]), ALU.add).then_inc(S["x_biased"], 1)

                    def attention(a, add):
                        pool.wait_ge(S["qk_T"], 4 * a + 4)
                        for h in range(HG):
                            G.tensor_scalar(kbd[:, 1, h, :], kT[:, 1, :], hmask[:, h:h + 1], 1.0, ALU.mult, ALU.mult).then_inc(S["kbd_pool"], 1)
                        U = KT * NT
                        for s in range(U + 1):
                            if s < U:
                                n = U * a + s
                                pool.wait_ge(S["att_scaled"], n + 1)
                                G.tensor_tensor(T[:, n % 4], T[:, n % 4], add(s % NT).unsqueeze(1).to_broadcast([P, HG, SEQ]), ALU.add)\
                                    .then_inc(S["att_masked"], 1)
                            if s >= 1:
                                n = U * a + s - 1
                                pool.wait_ge(S["att_max"], n + 1)
                                G.tensor_tensor(T[:, n % 4], T[:, n % 4], nmax[:, n % 4, :].unsqueeze(2).to_broadcast([P, HG, SEQ]), ALU.add)\
                                    .then_inc(S["att_sub"], 1)

                    pool.wait_ge(s_small, SMALL)
                    pool.wait_ge(s_once, ONCE)
                    norm(0)
                    bias(0, "L0_b_ao")
                    pool.wait_ge(S["mask_in"], 3 * 16)
                    G.tensor_scalar(a_self, m_self, 10000.0, -10000.0, ALU.mult, ALU.add).then_inc(S["masks_ready"], 1)
                    G.tensor_scalar(a_cross, m_cross, 10000.0, -10000.0, ALU.mult, ALU.add).then_inc(S["masks_ready"], 1)
                    settle(G.tensor_copy(m_key, m_key8))
                    G.tensor_scalar(a_key, m_key, -1.0, NEG_BIG, ALU.add, ALU.mult).then_inc(S["masks_ready"], 1)
                    pool.wait_ge(S["masks_ready"], 3)
                    attention(0, lambda t: a_self)
                    norm(1)
                    bias(1, "L0_b_co")
                    attention(1, lambda t: a_cross[:, t, :])
                    norm(2)
                    bias(2, "L0_b2")
                    norm(3)

                    def shift(L, state_row, signal):
                        for c in range(KT):
                            pool.wait_ge(S["ln_hT"], KT * L + c + 1)
                            h = hT[:, c, :].rearrange("p (b s) -> p b s", s=SEQ)
                            o = sxT[:, c, :].rearrange("p (b s) -> p b s", s=SEQ)
                            st = ctxT[:, c, :].rearrange("p (b s) -> p b s", s=SEQ)[:, :, state_row:state_row + 1]
                            G.tensor_tensor(o[:, :, 1:SEQ], h[:, :, 0:SEQ - 1], h[:, :, 1:SEQ], ALU.subtract).then_inc(S[signal], 1)
                            G.tensor_tensor(o[:, :, 0:1], st, h[:, :, 0:1], ALU.subtract).then_inc(S[signal], 1)

                    pool.wait_ge(S["ctxT_ready"], KT)
                    pool.wait_ge(S["x_updated"], 3 * NT)
                    G.memset(wdec.rearrange("p k (b s) -> p (k b) s", s=SLOT)[:, :, 0:1], 0.0).then_inc(S["slots_zero"], 1)
                    shift(3, 1, "l1_sx")
                    for i in range(5):
                        for c in range(KT):
                            pool.wait_ge(S["l1_y"], KT * i + c + 1)
                            G.tensor_tensor(xm[:, i % 2, c, :], xm[:, i % 2, c, :], hT[:, c, :], ALU.add).then_inc(S["l1_xm"], 1)
                    pool.wait_ge(S["state_in"], 16)
                    for n in range(KT * S8 + 2):
                        if n < KT * S8:
                            c, j = n // S8, n % S8
                            if n >= 3:
                                pool.wait_ge(S["l1_state"], n - 2)
                            G.tensor_copy(kvA[:, n % 3, :].rearrange("p (b s) -> p b s", s=SLOT)[:, :, 0], s0[:, c, :, j])\
                                .then_inc(S["l1_slot"], 1)
                        if n >= 2:
                            m = n - 2
                            pool.wait_ge(S["l1_state"], m + 1)
                            if m == 0:
                                pool.wait_ge(S["l1_rkvg"], 3 * KT)
                            if m >= 3:
                                pool.wait_ge(S["l1_rs_used"], m - 2)
                            G.tensor_tensor(rsZ[:, m % 3, :].rearrange("p (b s) -> p b s", s=SEQ),
                                            stS[:, m % 3, :].rearrange("p (b s) -> p b s", s=SLOT)[:, :, 0:SEQ],
                                            qT[:, m // S8, :].rearrange("p (b s) -> p b s", s=SEQ), ALU.mult).then_inc(S["l1_rs"], 1)
                    for g in range(2):
                        v = small[:, 64 + 64 * g:128 + 64 * g]
                        pool.wait_ge(S["l1_var"], g + 1)
                        settle(G.tensor_scalar(v, v, 1.0 / S8, EPS, ALU.mult, ALU.add))
                        G.tensor_tensor(v, v, neghalf.to_broadcast([P, 64]), ALU.pow).then_inc(S["l1_rs_gn"], 1)
                    for c in range(KT):
                        pool.wait_ge(S["l1_gn_T"], c + 1)
                        pool.wait_ge(S["l1_rkvg"], 4 * KT)
                        G.tensor_tensor(aT[:, c, :], dtmp[:, c, :], gateT[:, c, :], ALU.mult).then_inc(S["l1_gated"], 1)
                    norm(4)
                    shift(4, 0, "l1_sx2")
                    for c in range(KT):
                        pool.wait_ge(S["l1_relu"], c + 1)
                        G.tensor_tensor(aT[:, c, :], dtmp[:, c, :], dtmp[:, c, :], ALU.mult).then_inc(S["l1_kk"], 1)

                    def cross2(z, bik):
                        def head(h):
                            n = H2 * z + h
                            pool.wait_ge(S[f"w2_in{n % 3}"], 32 * (n // 3 + 1))
                            if n >= 2:
                                pool.wait_ge(S["l2_v"], n - 1)
                                pool.wait_ge(S["l2_scores"], n - 1)
                            G.tensor_tensor(dbv[:, n % 2, :], b2ring[:, n % 3, 0, :], b2ring[:, n % 3, 1, :], ALU.subtract).then_inc(S["l2_dbv"], 1)
                            G.tensor_copy(k2[:, n % 2, :, SEQ], col(bik, h).to_broadcast([P, NB])).then_inc(S["l2_kb"], 1)

                        head(0)
                        for h in range(H2):
                            if h + 1 < H2:
                                head(h + 1)
                            n = H2 * z + h
                            pool.wait_ge(S["l2_rden"], n + 1)
                            pool.wait_ge(S["l2_exp"], n + 1)
                            pool.wait_ge(S["l2_kb"], min(n + 2, H2 * (z + 1)))
                            if n >= 2:
                                pool.wait_ge(S["l2_tp"], n - 1)
                            rec = small[SEQ:P, 8 * (n % 2) + 4:8 * (n % 2) + 8]
                            G.tensor_tensor(pbd[SEQ:P, n % 2, :, SEQ:P], E2[SEQ:P, n % 2, :, 0:SEQ],
                                            rec.unsqueeze(2).to_broadcast([SEQ, NT, SEQ]), ALU.mult).then_inc(S["l2_prob_b"], 1)
                            pool.wait_ge(S["l2_prob_b"], n + 1)

                    norm(5)
                    bias(5, "L2_bo1")
                    cross2(0, "L2_bik1")
                    norm(6)
                    bias(6, "L2_bo2")
                    cross2(1, "L2_bik2")
                    norm(7)
                    bias(7, "L2_bf2")
                    norm(8)
                    bias(8, "L3_cb")
                    attention(2, lambda t: a_key[:, t, :])
                    norm(9)
                    bias(9, "L3_pb")

                @block.sync
                def _(sp):
                    def flat(ap):
                        return ap.rearrange("p a b -> p (a b)")

                    sp.dma_start(flat(X), t_x[chunk]).then_inc(S["x_in"], 16)
                    sp.dma_start(flat(ctx_tok), t_ctx[chunk]).then_inc(S["ctx_in"], 16)
                    sp.dma_start(flat(m_cross), t_cross[chunk]).then_inc(S["mask_in"], 16)
                    for half in range(2):
                        sp.dma_start(flat(m_key8[half * SEQ:(half + 1) * SEQ]),
                                     t_bmask[chunk, half, :].partition_broadcast(SEQ)).then_inc(S["mask_in"], 16)
                    sp.dma_start(s0.rearrange("p k b j -> p (k b j)"), t_state[chunk]).then_inc(S["state_in"], 16)
                    sp.dma_start(mlp_w, t_mlp[0]).then_inc(S["mlp_in"], 16)

                    def head_weights(n):
                        if n >= 3:
                            sp.wait_ge(S["l2_v_mm"], n - 2)
                            sp.wait_ge(S["l2_dbv"], n - 2)
                        sp.dma_start(w2ring[:, n % 3, :], t_w2[n]).then_inc(S[f"w2_in{n % 3}"], 16)
                        sp.dma_start(b2ring[:, n % 3].rearrange("p w d -> p (w d)"), t_b2[n].partition_broadcast(P))\
                            .then_inc(S[f"w2_in{n % 3}"], 16)

                    for n in range(3):
                        head_weights(n)
                    sp.wait_ge(S["x_updated"], 3 * NT)
                    sp.dma_start(mlp_w, t_mlp[1]).then_inc(S["mlp_in"], 16)
                    sp.wait_ge(S["x_updated"], 5 * NT)
                    sp.dma_start(flat(wo2), t_wo2[0]).then_inc(S["wo_in"], 16)
                    for n in range(3, 2 * H2):
                        if n == H2 + 3:
                            sp.wait_ge(S["x_updated"], 6 * NT)
                            sp.dma_start(flat(wo2), t_wo2[1]).then_inc(S["wo_in"], 16)
                        head_weights(n)
                    sp.wait_ge(S["x_updated"], 8 * NT)
                    sp.dma_start(mlp_w, t_mlp[2]).then_inc(S["mlp_in"], 16)
                    sp.wait_ge(S["x_updated"], 10 * NT)
                    sp.dma_start(t_out[chunk], flat(X)).then_inc(S["out_done"], 16)
                    sp.wait_ge(S["out_done"], 16)
            nc.gpsimd.sem_clear(range(nums[0], nums[0] + len(nums)))
            nc.all_engine_barrier()


def shape_constants():
    p = np.arange(P)
    sel = np.zeros((P, S8, P), np.float32)
    for j in range(S8):
        sel[:, j, :] = (p[:, None] // S8 == p[None, :] // S8) & (p[:, None] % S8 == j)
    parts = {
        "ident": np.eye(P),
        "sel": sel.reshape(P, -1),
        "headmask": p[:, None] // 16 == np.arange(HG)[None, :],
        "ones2": p[:, None] // SEQ == np.arange(32)[None, :] // 16,
        "heads8": p[:, None] // S8 == np.arange(HL1)[None, :],
        "block8": p[:, None] // S8 == p[None, :] // S8,
    }
    return np.concatenate([parts[n].astype(np.float32) for n, _ in CONSTS], axis=1)


def kernel(**inputs):
    import concourse.bacc as bacc
    from concourse.bass_utils import run_bass_kernel_spmd as run

    def g(name):
        return np.asarray(inputs[name])

    def L(i, name):
        return g(f"L{i}_xattn_{name}")

    def rows_on_partitions(w):
        k = w.shape[0] // P
        return w.reshape(k, P, w.shape[1]).transpose(1, 0, 2).reshape(P, -1)

    def pad_rows(w):
        out = np.zeros((P, w.shape[1]), w.dtype)
        out[:w.shape[0]] = w
        return out

    def tokens(a):
        n = a.shape[-1]
        return a.reshape(CHUNKS, NT, P, n).transpose(0, 2, 1, 3).reshape(CHUNKS, P, NT * n)

    x, enc = g("x"), g("ctx_2048")
    st = enc[:, 2:2 + S8, :].reshape(CHUNKS, NB, KT, P, S8).transpose(0, 3, 2, 1, 4).reshape(CHUNKS, P, -1)
    bqkv, bkv = L(0, "b_qkv"), L(0, "b_kv")
    stack = L(1, "maa_stack").reshape(5, D)
    vec = {
        "L0_ln1_s": L(0, "ln1_s"), "L0_ln1_b": L(0, "ln1_b"), "L0_bq_s": bqkv[:D], "L0_bk_s": bqkv[D:2 * D],
        "L0_ln2_s": L(0, "ln2_s"), "L0_ln2_b": L(0, "ln2_b"), "L0_b_q": L(0, "b_q"), "L0_bk_c": bkv[:D],
        "L0_ln3_s": L(0, "ln3_s"), "L0_ln3_b": L(0, "ln3_b"), "L1_ln1_w": L(1, "ln1_w"), "L1_ln1_b": L(1, "ln1_b"),
        "L1_ln2_w": L(1, "ln2_w"), "L1_ln2_b": L(1, "ln2_b"), "L1_maa_x": L(1, "maa_x"),
        "L1_time_decay": L(1, "time_decay"), "L1_u": L(1, "u"), "L1_gn_w": L(1, "gn_w"), "L1_gn_b": L(1, "gn_b"),
        "L1_fmk": L(1, "ffn_maa_k"), "L1_fmr": L(1, "ffn_maa_r"),
        "L2_ln1_s": L(2, "ln1_scale"), "L2_ln1_b": L(2, "ln1_offset"), "L2_ln2_s": L(2, "ln2_scale"),
        "L2_ln2_b": L(2, "ln2_offset"), "L2_lnm_s": L(2, "ln_mlp_scale"), "L2_lnm_b": L(2, "ln_mlp_offset"),
        "L3_ln1_w": L(3, "ln1_w"), "L3_ln1_b": L(3, "ln1_b"), "L3_q_b": L(3, "q_b"), "L3_k_b": L(3, "k_b"),
        "L3_ln2_w": L(3, "ln2_w"), "L3_ln2_b": L(3, "ln2_b"),
        "L0_b1": L(0, "b1"), "L2_bf1": L(2, "b_fc1"), "L3_fcb": L(3, "fc_b"),
        "L2_bq1": L(2, "bq1"), "L2_bk1": L(2, "bk1"), "L2_bik1": L(2, "bias_k1"), "L2_biv1": L(2, "bias_v1"),
        "L2_bq2": L(2, "bq2"), "L2_bk2": L(2, "bk2"), "L2_bik2": L(2, "bias_k2"), "L2_biv2": L(2, "bias_v2"),
        "L0_bv_s": bqkv[2 * D:], "L0_b_ao": L(0, "b_ao"), "L0_bv_c": bkv[D:], "L0_b_co": L(0, "b_co"), "L0_b2": L(0, "b2"),
        "L2_bo1": L(2, "bo1"), "L2_bo2": L(2, "bo2"), "L2_bf2": L(2, "b_fc2"),
        "L3_v_b": L(3, "v_b"), "L3_cb": L(3, "cproj_b"), "L3_pb": L(3, "proj_b"),
    }
    for i in range(5):
        vec[f"L1_st{i}"] = stack[i]
    cols = np.concatenate([vec[n].reshape(-1, P).T for n in COL2 + COL8 + COL16], axis=1)
    rows = np.concatenate([vec[n].reshape(-1) for n in ROWS])
    m2 = L(1, "maa_w2")
    wres = {
        "L0_qkv": rows_on_partitions(L(0, "w_qkv")), "L0_ao": rows_on_partitions(L(0, "w_ao")),
        "L0_q": rows_on_partitions(L(0, "w_q")), "L0_kv": rows_on_partitions(L(0, "w_kv")),
        "L0_co": rows_on_partitions(L(0, "w_co")),
        "L1_m1": rows_on_partitions(L(1, "maa_w1")), "L1_m2a": m2[:4].reshape(P, D), "L1_m2b": pad_rows(m2[4]),
        "L1_td1": rows_on_partitions(L(1, "td_w1")), "L1_td2": pad_rows(L(1, "td_w2")),
        "L1_W": np.concatenate([rows_on_partitions(L(1, n).T) for n in ("Wr", "Wk", "Wv", "Wg", "Wo", "Wfk", "Wfr", "Wfv")], axis=1),
        "L3_qkv": np.concatenate([rows_on_partitions(L(3, n)) for n in ("q_w", "k_w", "v_w")], axis=1),
        "L3_c": rows_on_partitions(L(3, "cproj_w")),
    }
    wres = np.concatenate([wres[n] for n, _ in WRES], axis=1)
    mlp = np.stack([np.concatenate([rows_on_partitions(a), rows_on_partitions(b)], axis=1) for a, b in
                    ((L(0, "w1"), L(0, "w2")), (L(2, "w_fc1"), L(2, "w_fc2")), (L(3, "fc_w"), L(3, "proj_w")))])
    w2, b2, wo2 = [], [], []
    for z in (1, 2):
        w = np.stack([L(2, f"w{n}{z}").reshape(KT, P, H2, P) for n in "qkv"])
        w2.append(w.transpose(3, 2, 0, 1, 4).reshape(H2, P, -1))
        b2.append(np.stack([L(2, f"bv{z}").reshape(H2, P), L(2, f"bias_v{z}").reshape(H2, P)], axis=1).reshape(H2, 2 * P))
        wo2.append(L(2, f"wo{z}").reshape(H2, P, D).transpose(1, 0, 2).reshape(P, -1))
    arrays = {
        "x_in": tokens(x), "ctx_in": tokens(enc), "state": st,
        "ltor": g("mask_1x1xSxS2_fc1").reshape(SEQ, SEQ), "cross": tokens(g("mask_Bx1xSxS2_ff1").reshape(NSEQ, SEQ, SEQ)),
        "bmask": g("mask_BxS2_bf1").view(np.uint8).reshape(CHUNKS, NT, 2, SEQ).transpose(0, 2, 1, 3).reshape(CHUNKS, 2, NT * SEQ),
        "cols": cols, "rows": rows, "consts": shape_constants(), "wres": wres, "mlp": mlp,
        "w2": np.concatenate(w2), "b2": np.concatenate(b2), "wo2": np.stack(wo2),
    }
    arrays = {k: np.ascontiguousarray(v) for k, v in arrays.items()}
    nc = bacc.Bacc("TRN2", target_bir_lowering=False, num_devices=1)
    args = [nc.dram_tensor(f"in_{k}", v.shape, mybir.dt.from_np(v.dtype), kind="ExternalInput").ap() for k, v in arrays.items()]
    out = nc.dram_tensor("out_0", (CHUNKS, P, NT * D), mybir.dt.float32, kind="ExternalOutput").ap()
    build(nc, *args, out)
    r = run(nc, [{f"in_{k}": v for k, v in arrays.items()}], core_ids=[0]).results[0]["out_0"]
    return r.reshape(CHUNKS, P, NT, D).transpose(0, 2, 1, 3).reshape(NSEQ, SEQ, D)
```

```python
import numpy as np
import concourse.bass as bass
from concourse import mybir
from contextlib import ExitStack

P = 128
D = 256
KT = D // P
NSEQ, SEQ = 32, 64
CHUNKS = 4
NB = NSEQ // CHUNKS
TOK = NB * SEQ
NT = TOK // P
HF = 4 * D
MT = HF // P
EPS = 1e-5
H0 = 16
HG = 8
H2 = 16
KX = SEQ + 1
SLOT = SEQ + 1
S8 = 8
HL1 = P // S8
FS = [1, 0, 2, 3, 4]
LAG = 3
TR = LAG + 3
QK_OWN = [(0, True), (0, False), (1, True), (1, False)]
QK_ENC = [(0, True), (1, True), (0, False), (1, False)]
SUMLAG = 5
GN_AT = S8 + SUMLAG + 1
NEG_BIG = float(np.finfo(np.float32).max)

COL2 = ["L0_ln1_s", "L0_ln1_b", "L0_bq_s", "L0_bk_s", "L0_ln2_s", "L0_ln2_b", "L0_b_q", "L0_bk_c",
        "L0_ln3_s", "L0_ln3_b", "L1_ln1_w", "L1_ln1_b", "L1_ln2_w", "L1_ln2_b", "L1_maa_x",
        "L1_st0", "L1_st1", "L1_st2", "L1_st3", "L1_st4", "L1_time_decay", "L1_u", "L1_gn_w",
        "L1_gn_b", "L1_fmk", "L1_fmr", "L2_ln1_s", "L2_ln1_b", "L2_ln2_s", "L2_ln2_b",
        "L2_lnm_s", "L2_lnm_b", "L3_ln1_w", "L3_ln1_b", "L3_q_b", "L3_k_b", "L3_ln2_w", "L3_ln2_b"]
COL8 = ["L0_b1", "L2_bf1", "L3_fcb"]
COL16 = ["L2_bq1", "L2_bk1", "L2_bik1", "L2_biv1", "L2_bq2", "L2_bk2", "L2_bik2", "L2_biv2"]
COL = {}
_at = 0
for _names, _w in ((COL2, KT), (COL8, MT), (COL16, H2)):
    for _n in _names:
        COL[_n] = _at
        _at += _w
NCOL = _at
ROWS = ["L0_bv_s", "L0_b_ao", "L0_bv_c", "L0_b_co", "L0_b2", "L2_bo1", "L2_bo2", "L2_bf2",
        "L3_v_b", "L3_cb", "L3_pb"]
CONSTS = [("ident", P), ("sel", S8 * P), ("headmask", HG), ("ones2", 32), ("heads8", HL1), ("block8", P)]
CAT = {}
_at = 0
for _n, _w in CONSTS:
    CAT[_n] = (_at, _w)
    _at += _w
NCONST = _at
WRES = [("L0_qkv", KT * 3 * D), ("L0_ao", KT * D), ("L0_q", KT * D), ("L0_kv", KT * 2 * D), ("L0_co", KT * D),
        ("L1_m1", KT * 160), ("L1_m2a", D), ("L1_m2b", D), ("L1_td1", KT * 64), ("L1_td2", D),
        ("L1_W", 8 * KT * D), ("L3_qkv", 3 * KT * D), ("L3_c", KT * D)]
WAT = {}
_at = 0
for _n, _w in WRES:
    WAT[_n] = (_at, _w)
    _at += _w
NWRES = _at


def build(nc, t_x, t_ctx, t_state, t_ltor, t_cross, t_bmask, t_cols, t_rows, t_consts, t_wres, t_mlp,
          t_w2, t_b2, t_wo2, t_out):
    f32 = mybir.dt.float32
    ALU = mybir.AluOpType
    ACT = mybir.ActivationFunctionType
    AX = mybir.AxisListType.X
    ctx = ExitStack()
    with ctx:
        def sb(name, cols, dt=f32):
            return ctx.enter_context(nc.sbuf_tensor(name, [P, cols], dt))[:, :]

        def view(ap, pat, **kw):
            return ap.rearrange(pat, **kw)

        cols = sb("cols", NCOL)
        rows = view(sb("rows", len(ROWS) * D), "p (r d) -> p r d", d=D)
        consts = sb("consts", NCONST)
        wres = sb("wres", NWRES)
        mlp_w = sb("mlp_w", KT * HF + MT * D)
        X = view(sb("X", NT * D), "p (t d) -> p t d", d=D)
        xn = view(sb("xn", NT * D), "p (t d) -> p t d", d=D)
        gn = xn.rearrange("p t d -> p (t d)").rearrange("p (c n) -> p c n", c=KT)
        ctxT = view(sb("ctxT", KT * TOK), "p (k n) -> p k n", k=KT)
        hT = view(sb("hT", KT * TOK), "p (k n) -> p k n", k=KT)
        qT = view(sb("qT", KT * TOK), "p (k n) -> p k n", k=KT)
        kT = view(sb("kT", KT * TOK), "p (k n) -> p k n", k=KT)
        aT = view(sb("aT", KT * TOK), "p (k n) -> p k n", k=KT)
        vbd = view(sb("vbd", NB * 8 * 32), "p (b h c) -> p b h c", b=NB, h=8)
        pbd = view(sb("pbd", 2 * NT * P), "p (s t k) -> p s t k", s=2, t=NT)
        w2ring = view(sb("w2ring", 3 * 3 * KT * P), "p (s w) -> p s w", s=3)
        b2ring = view(sb("b2ring", 3 * 2 * P), "p (s w d) -> p s w d", s=3, w=2)
        dbv = view(sb("dbv", 2 * P), "p (s d) -> p s d", s=2)
        m_self = sb("m_self", SEQ)
        m_cross = view(sb("m_cross", NT * SEQ), "p (t k) -> p t k", t=NT)
        m_key8 = view(sb("m_key8", NT * SEQ, mybir.dt.uint8), "p (t k) -> p t k", t=NT)
        m_key = view(sb("m_key", NT * SEQ), "p (t k) -> p t k", t=NT)
        a_self = sb("a_self", SEQ)
        a_cross = view(sb("a_cross", NT * SEQ), "p (t k) -> p t k", t=NT)
        a_key = view(sb("a_key", NT * SEQ), "p (t k) -> p t k", t=NT)
        s0 = view(sb("s0", KT * NB * S8), "p (k b j) -> p k b j", k=KT, b=NB)
        bst = view(sb("bst", NT * 6), "p (t s) -> p t s", t=NT)
        mv = view(sb("mv", NT * 2), "p (t s) -> p t s", t=NT)
        rstd = sb("rstd", NT)
        neghalf = sb("neghalf", 1)
        nmax = view(sb("nmax", TR * HG), "p (s h) -> p s h", s=TR)
        small = sb("small", 2 * 64)
        gn_var = sb("gn_var", 64)
        gn_sd = sb("gn_sd", 64)
        gn_r = sb("gn_r", 64)
        ARENA = 17000
        arena = sb("arena", ARENA)
        used = {}

        def carve(layer, n):
            at = used.get(layer, 0)
            used[layer] = at + n
            assert used[layer] <= ARENA, (layer, used[layer])
            return arena[:, at:at + n]

        kbd = view(carve("att", KT * HG * TOK), "p (g h n) -> p g h n", g=KT, h=HG)
        T = view(carve("att", TR * TOK), "p (s h k) -> p s h k", s=TR, h=HG)
        PTs = view(carve("att", 2 * TOK), "p (s h q) -> p s h q", s=2, h=4)
        rden = view(carve("att", 2 * P), "p (s q) -> p s q", s=2)
        ctx_tok = view(carve("att", NT * D), "p (t d) -> p t d", t=NT)
        x_first = view(carve("att", NT * D), "p (t d) -> p t d", t=NT)
        gT = view(carve("mlp", MT * TOK), "p (m n) -> p m n", m=MT)
        sxT = view(carve("l1", KT * TOK), "p (k n) -> p k n", k=KT)
        xm = view(carve("l1", 2 * KT * TOK), "p (s k n) -> p s k n", s=2, k=KT)
        zA = carve("l1", TOK)
        zB = carve("l1", TOK)
        tw = carve("l1", TOK)
        dtmp = view(carve("l1", KT * TOK), "p (k n) -> p k n", k=KT)
        wdec = view(carve("l1", KT * NB * SLOT), "p (k n) -> p k n", k=KT)
        vT = view(carve("l1", KT * TOK), "p (k n) -> p k n", k=KT)
        gateT = view(carve("l1", KT * TOK), "p (k n) -> p k n", k=KT)
        rku = view(carve("l1", KT * TOK), "p (k n) -> p k n", k=KT)
        kvA = view(carve("l1", 3 * NB * SLOT), "p (s n) -> p s n", s=3)
        stS = view(carve("l1", 3 * NB * SLOT), "p (s n) -> p s n", s=3)
        rsZ = view(carve("l1", 3 * TOK), "p (s n) -> p s n", s=3)
        gnsq = carve("l1", TOK)
        q2 = view(carve("l2", 2 * TOK), "p (s n) -> p s n", s=2)
        k2 = view(carve("l2", 2 * NB * KX), "p (s b k) -> p s b k", s=2, b=NB)
        v2 = view(carve("l2", 2 * TOK), "p (s t d) -> p s t d", s=2, t=NT)
        E2 = view(carve("l2", 2 * NT * KX), "p (s t k) -> p s t k", s=2, t=NT)
        PT2 = view(carve("l2", 2 * TOK), "p (s t q) -> p s t q", s=2, t=NT)
        c2T = view(carve("l2", H2 * TOK), "p (h n) -> p h n", h=H2)
        wo2 = view(carve("l2", H2 * D), "p (h d) -> p h d", h=H2)

        bank = [ctx.enter_context(nc.psum_tensor(f"bank{i}", [P, 512], f32)) for i in range(8)]
        RING = 6

        def col(name, k=0):
            return cols[:, COL[name] + k:COL[name] + k + 1]

        def row(name):
            return rows[:, ROWS.index(name), :]

        def const(name):
            a, w = CAT[name]
            return consts[:, a:a + w]

        def weight(name, k=KT):
            a, w = WAT[name]
            return view(wres[:, a:a + w], "p (k n) -> p k n", k=k)

        ident = const("ident")
        sel = view(const("sel"), "p (j c) -> p j c", j=S8)
        hmask = const("headmask")
        w1 = view(mlp_w[:, 0:KT * HF], "p (k n) -> p k n", k=KT)
        w2 = view(mlp_w[:, KT * HF:], "p (m n) -> p m n", m=MT)
        l1w = view(weight("L1_W", 1)[:, 0, :], "p (w k n) -> p w k n", w=8, k=KT)

        def sem(name):
            return ctx.enter_context(nc.semaphore(name))

        s_small, s_qkv, s_wl0, s_wl1, s_wl3, s_once, s_ctx0, s_chunk0 = map(
            sem, ("vectors_in", "w_qkv_in", "w_l0_in", "w_l1_in", "w_l3_in", "preset", "ctx0_in", "chunk0_in"))
        names = """next_in mlp_in wo_in w2_in0 w2_in1 w2_in2 out_done
            masks_ready slots_zero ctx_tp ctxT_ready
            dve_step pool_step act_step
            ln_mv ln_rstd ln_xn ln_tp ln_hT x_biased x_updated
            qk_mm qk_T kbd_dve kbd_pool v_mm v_bd att_scores att_scaled att_masked att_max att_sub att_exp
            att_tp att_PT att_pv att_out proj_mm
            mlp_up_mm mlp_act
            l1_sx l1_xm0 l1_z_mm l1_z l1_y_mm l1_y l1_xm l1_td_mm l1_td l1_dec_mm l1_dec l1_rkvg_mm l1_rkvg
            l1_rku l1_rku_mm l1_uv l1_vb l1_kv l1_slot l1_state l1_rs l1_rs_used l1_og l1_cent l1_sq l1_var l1_sd
            l1_gn l1_gn_tp l1_gn_T l1_gated l1_sx2 l1_x2 l1_ffk_mm l1_relu l1_kk l1_rr_mm l1_rr
            l2_dbv l2_q_mm l2_q l2_k_mm l2_k l2_kb l2_v_mm l2_v l2_scores l2_max l2_sub l2_exp l2_prob_a
            l2_prob_b l2_rden l2_tp l2_PT l2_pv l2_c""".split()
        loop_sems = [sem(n) for n in names]
        S = dict(zip(names, loop_sems))
        nums = [s.num for s in loop_sems]
        assert nums == list(range(nums[0], nums[0] + len(nums)))

        def flat(ap):
            return ap.rearrange("p a b -> p (a b)")

        def load_chunk(queue, c, first, rest):
            queue.dma_start(flat(ctx_tok), c(t_ctx)).then_inc(first, 16)
            queue.dma_start(flat(x_first), c(t_x)).then_inc(rest, 16)
            queue.dma_start(flat(m_cross), c(t_cross)).then_inc(rest, 16)
            for half in range(2):
                queue.dma_start(flat(m_key8[half * SEQ:(half + 1) * SEQ]),
                                c(t_bmask)[half, :].partition_broadcast(SEQ)).then_inc(rest, 16)
            queue.dma_start(s0.rearrange("p k b j -> p (k b j)"), c(t_state)).then_inc(rest, 16)

        def load_weights(queue, s, first, last):
            a, b = WAT[first][0], WAT[last][0] + WAT[last][1]
            queue.dma_start(wres[:, a:b], t_wres[:, a:b]).then_inc(s, 16)

        with nc.Block() as block:
            @block.sync
            def _(sp):
                sp.dma_start(consts[:, 0:P], t_consts[:, 0:P]).then_inc(s_small, 16)
                load_chunk(sp, lambda t: t[0], s_ctx0, s_chunk0)
                load_weights(sp, s_wl1, "L1_m1", "L1_W")

            @block.scalar
            def _(act):
                act.dma_start(cols, t_cols).then_inc(s_small, 16)
                load_weights(act, s_qkv, "L0_qkv", "L0_qkv")
                act.dma_start(m_self[0:SEQ, :], t_ltor).then_inc(s_small, 16)
                act.dma_start(m_self[SEQ:P, :], t_ltor).then_inc(s_small, 16)
                act.dma_start(consts[:, P:], t_consts[:, P:]).then_inc(s_small, 16)
                act.dma_start(rows.rearrange("p r d -> p (r d)"), t_rows.partition_broadcast(P)).then_inc(s_small, 16)
                load_weights(act, s_wl0, "L0_ao", "L0_co")
                load_weights(act, s_wl3, "L3_qkv", "L3_c")

            @block.gpsimd
            def _(pool):
                nc.gpsimd.memset(neghalf, -0.5).then_inc(s_once, 1)
                nc.gpsimd.memset(vbd, 0.0).then_inc(s_once, 1)
                nc.gpsimd.memset(pbd, 0.0).then_inc(s_once, 1)
        SMALL, ONCE = 6 * 16, 3
        CHUNK0 = 5 * 16

        with nc.Fori(0, CHUNKS) as chunk:
            with nc.Block() as block:

                ring = {"n": 0, "freed": [None] * RING, "at": {}}

                def take(pe, tag, stage, n):
                    i = ring["n"] % RING
                    ring["n"] += 1
                    if ring["freed"][i]:
                        pe.wait_ge(S[ring["freed"][i][0]], ring["freed"][i][1])
                    ring["freed"][i] = (stage, n)
                    ring["at"][tag] = i
                    return bank[i]

                def held(tag):
                    return bank[ring["at"][tag]]

                @block.tensor
                def _(pe):
                    mm = nc.tensor.matmul

                    def transposes():
                        b = [take(pe, ("ctx", k), "ctxT_ready", k + 1) for k in range(KT)]
                        for t in range(NT):
                            for k in range(KT):
                                last = nc.tensor.transpose(b[k][:, t * P:(t + 1) * P], ctx_tok[:, t, k * P:(k + 1) * P], ident)
                                if t == NT - 1:
                                    last.then_inc(S["ctx_tp"], 1)

                    def norm(L, before_last=None):
                        b = [take(pe, ("ln", L, half), "ln_hT", 2 * KT * L + KT * (half + 1)) for half in range(2)]
                        for t in range(NT):
                            if t == NT - 1 and before_last:
                                before_last()
                            pe.wait_ge(S["ln_xn"], NT * L + t + 1)
                            for k in range(KT):
                                o = k * TOK // 2 + t % 2 * P
                                last = nc.tensor.transpose(b[t // 2][:, o:o + P], xn[:, t, k * P:(k + 1) * P], ident)
                                if t % 2:
                                    last.then_inc(S["ln_tp"], 1)

                    def norm_and_linears(L, jobs):
                        banks = {}

                        def half(job, part):
                            tag, w, m0, signal, used_by, n = job
                            if part == 0:
                                banks[tag] = take(pe, tag, used_by, n)
                            h = slice(part * TOK // 2, (part + 1) * TOK // 2)
                            for k in range(KT):
                                last = mm(banks[tag][:, h], w[:, k, m0:m0 + P], hT[:, k, h], start=(k == 0), stop=(k == KT - 1))
                            if part:
                                last.then_inc(S[signal], 1)

                        early = len(jobs) // 2

                        def before_last():
                            pe.wait_ge(S["ln_hT"], 2 * KT * L + KT)
                            for job in jobs[:early]:
                                half(job, 0)

                        norm(L, before_last)
                        for job in jobs[early:]:
                            half(job, 0)
                        pe.wait_ge(S["ln_hT"], 2 * KT * (L + 1))
                        for job in jobs:
                            half(job, 1)

                    def linear(tag, w, src, m0, signal, used_by, n, rows_out=P):
                        b = take(pe, tag, used_by, n)
                        for k in range(w.shape[1]):
                            last = mm(b[0:rows_out, :], w[:, k, m0:m0 + rows_out], src[:, k, :],
                                      start=(k == 0), stop=(k == w.shape[1] - 1))
                        last.then_inc(S[signal], 1)

                    def out_proj(site, w, src, nk, before):
                        for t in range(NT):
                            before(t)
                            b = take(pe, ("proj", site, t), "x_updated", NT * site + t + 1)
                            for k in range(nk):
                                last = mm(b[:, 0:D], src[:, k, t * P:(t + 1) * P], w[:, k, :],
                                          start=(k == 0), stop=(k == nk - 1))
                            last.then_inc(S["proj_mm"], 1)

                    def values(a, wv, kv_src, g):
                        b = take(pe, ("v", a, g), "v_bd", 8 * a + 4 * (g + 1))
                        for i in range(2):
                            t = 2 * g + i
                            for k in range(KT):
                                last = mm(b[:, i * D:(i + 1) * D], kv_src[:, k, t * P:(t + 1) * P], wv[:, k, :],
                                          start=(k == 0), stop=(k == KT - 1))
                        last.then_inc(S["v_mm"], 1)

                    def attention(a, L, site, wq, wk, wv, kv_src, w_out):
                        def project(m, key, n):
                            w, src = (wk, kv_src) if key else (wq, hT)
                            linear(("qk", a, n), w, src, m * P, "qk_mm", "qk_T", 4 * a + n + 1)

                        own = kv_src is hT
                        if own:
                            norm_and_linears(L, [(("qk", a, n), wk if key else wq, m * P, "qk_mm", "qk_T", 4 * a + n + 1)
                                                 for n, (m, key) in enumerate(QK_OWN[:3])])
                        else:
                            project(0, True, 0)
                            project(1, True, 1)
                            norm(L, lambda: values(a, wv, kv_src, 0))
                            values(a, wv, kv_src, 1)
                            pe.wait_ge(S["ln_hT"], 2 * KT * (L + 1))
                            project(0, False, 2)
                        U = KT * NT
                        for s in range(U + LAG + 1):
                            if s < U:
                                g, t, n = s // NT, s % NT, U * a + s
                                if s == 0:
                                    pe.wait_ge(S["qk_T"], 4 * a + (2 if own else 3))
                                    pe.wait_ge(S["kbd_dve"], HG * (a + 1))
                                if s == NT:
                                    pe.wait_ge(S["qk_T"], 4 * a + 4)
                                    pe.wait_ge(S["kbd_pool"], HG * (a + 1))
                                if s == 2:
                                    project(1, False, 3)
                                    if own:
                                        for i in range(NT // 2):
                                            values(a, wv, kv_src, i)
                                b = take(pe, ("s", n), "att_scaled", n + 1)
                                for h in range(2):
                                    q0 = t * P + h * SEQ
                                    last = mm(b[h * SEQ:(h + 1) * SEQ, :], qT[:, g, q0:q0 + SEQ], kbd[:, g, :, q0:q0 + SEQ],
                                              start=True, stop=True)
                                last.then_inc(S["att_scores"], 1)
                            if LAG <= s < U + LAG:
                                n = U * a + s - LAG
                                pe.wait_ge(S["att_exp"], n + 1)
                                b = take(pe, ("tp", n), "att_PT", n + 1)
                                for h in range(4):
                                    last = nc.tensor.transpose(b[:, h * P:(h + 1) * P],
                                                               T[:, n % TR, 2 * h:2 * h + 2, :].rearrange("p h k -> p (h k)"), ident)
                                last.then_inc(S["att_tp"], 1)
                            if s >= LAG + 1:
                                u = s - LAG - 1
                                g, t, n = u // NT, u % NT, U * a + u
                                pe.wait_ge(S["att_PT"], n + 1)
                                if u == 0:
                                    pe.wait_ge(S["v_bd"], 8 * (a + 1))
                                b = take(pe, ("pv", n), "att_out", n + 1)
                                for h in range(4):
                                    o = slice(32 * h, 32 * h + 32)
                                    for half in range(2):
                                        mm(b[o, half * SEQ:(half + 1) * SEQ], vbd[:, 2 * t + half, 4 * g + h, :],
                                           PTs[:, n % 2, h, half * SEQ:(half + 1) * SEQ], start=True, stop=True,
                                           tile_position=(0, 32 * h))
                                    last = mm(b[o, P:2 * P], const("ones2"), PTs[:, n % 2, h, :], start=True, stop=True,
                                              tile_position=(0, 32 * h))
                                last.then_inc(S["att_pv"], 1)
                        if a == 0:
                            pe.wait_ge(s_wl0, 16)
                        out_proj(site, w_out, aT, KT, lambda t: pe.wait_ge(S["att_out"], U * a + NT + t + 1))

                    def mlp(m, L, site):
                        pe.wait_ge(S["mlp_in"], 16 * (m + 1))
                        norm_and_linears(L, [(("mlp", m, i), w1, i * P, "mlp_up_mm", "mlp_act", MT * m + i + 1)
                                             for i in range(4)])
                        for i in range(4, MT):
                            linear(("mlp", m, i), w1, hT, i * P, "mlp_up_mm", "mlp_act", MT * m + i + 1)
                        pe.wait_ge(S["mlp_act"], MT * (m + 1))
                        out_proj(site, w2, gT, MT, lambda t: None)

                    pe.wait_ge(s_small, SMALL)
                    pe.wait_ge(s_ctx0, 16)
                    transposes()
                    pe.wait_ge(s_qkv, 16)
                    pe.wait_ge(s_once, ONCE)
                    qkv = weight("L0_qkv")
                    attention(0, 0, 0, qkv[:, :, 0:D], qkv[:, :, D:2 * D], qkv[:, :, 2 * D:3 * D], hT, weight("L0_ao"))
                    pe.wait_ge(S["ctxT_ready"], KT)
                    pe.wait_ge(s_wl0, 16)
                    kv = weight("L0_kv")
                    attention(1, 1, 1, weight("L0_q"), kv[:, :, 0:D], kv[:, :, D:2 * D], ctxT, weight("L0_co"))
                    mlp(0, 2, 2)
                    norm(3)
                    pe.wait_ge(s_wl1, 16)
                    m1 = weight("L1_m1")
                    pe.wait_ge(S["l1_xm0"], KT)
                    linear("z0", m1, xm[:, 1], 0, "l1_z_mm", "l1_z", 1)
                    linear("z1", m1, xm[:, 1], P, "l1_z_mm", "l1_z", 2, rows_out=32)
                    pe.wait_ge(S["l1_z"], 2)

                    def l1_y(f):
                        i = FS.index(f)
                        for c in range(KT):
                            b = take(pe, ("y", i, c), "l1_y", KT * i + c + 1)
                            if f < 4:
                                w, z = weight("L1_m2a", 1)[32 * f:32 * f + 32, 0], zA[32 * f:32 * f + 32, :]
                            else:
                                w, z = weight("L1_m2b", 1)[0:32, 0], zB[0:32, :]
                            mm(b[:, :], w[:, c * P:(c + 1) * P], z, start=True, stop=True,
                               tile_position=(32 * (f % 4), 0)).then_inc(S["l1_y_mm"], 1)

                    def l1_use(i):
                        f, x = FS[i], xm[:, i % 2]
                        pe.wait_ge(S["l1_xm"], KT * (i + 1))
                        if f == 1:
                            linear("td", weight("L1_td1"), x, 0, "l1_td_mm", "l1_td", 1, rows_out=64)
                        else:
                            for c in range(KT):
                                n = KT * (i - 1) + c
                                linear(("rkvg", n), l1w[:, {3: 0, 0: 1, 2: 2, 4: 3}[f]], x, c * P, "l1_rkvg_mm", "l1_rkvg", n + 1)

                    l1_y(FS[0])
                    for i in range(5):
                        if i < 4:
                            l1_y(FS[i + 1])
                        l1_use(i)
                        if i == 1:
                            pe.wait_ge(S["l1_td"], 1)
                            for c in range(KT):
                                b = take(pe, ("dec", c), "l1_dec", 2 * c + 1)
                                mm(b[:, :], weight("L1_td2", 1)[0:64, 0, c * P:(c + 1) * P], tw[0:64, :],
                                   start=True, stop=True).then_inc(S["l1_dec_mm"], 1)
                    for c in range(KT):
                        pe.wait_ge(S["l1_rku"], c + 1)
                        b = take(pe, ("rku", c), "l1_uv", c + 1)
                        mm(b[:, :], const("block8"), rku[:, c, :], start=True, stop=True).then_inc(S["l1_rku_mm"], 1)

                    def l1_sum(n):
                        c, j = n // S8, n % S8
                        pe.wait_ge(S["l1_rs"], n + 1)
                        for t in range(NT):
                            last = mm(bank[6 + c][:, t * P + j:(t + 1) * P:S8], rsZ[:, n % 3, t * P:(t + 1) * P],
                                      const("heads8"), start=False, stop=(j == S8 - 1 and t == NT - 1), skip_group_check=True)
                        last.then_inc(S["l1_rs_used"], 1)

                    for n in range(KT * S8 + SUMLAG):
                        if n < KT * S8:
                            c, j = n // S8, n % S8
                            if n == 0:
                                pe.wait_ge(S["l1_rkvg"], 2 * KT)
                            b = take(pe, ("vb", n), "l1_kv", n + 1)
                            mm(b[:, :], sel[:, j, :], vT[:, c, :], start=True, stop=True).then_inc(S["l1_vb"], 1)
                        if n == 2:
                            pe.wait_ge(S["l1_uv"], KT)
                            for c in range(KT):
                                for t in range(NT):
                                    mm(bank[6 + c][:, t * P:(t + 1) * P], rku[:, c, t * P:(t + 1) * P], ident,
                                       start=(t == 0), stop=False, skip_group_check=True)
                        if n >= SUMLAG:
                            l1_sum(n - SUMLAG)
                    for c in range(KT):
                        pe.wait_ge(S["l1_gn"], c + 1)
                        b = take(pe, ("gn", c), "l1_gn_T", c + 1)
                        for t in range(NT):
                            last = nc.tensor.transpose(b[:, t * P:(t + 1) * P], gn[:, c, t * P:(t + 1) * P], ident)
                        last.then_inc(S["l1_gn_tp"], 1)
                    pe.wait_ge(S["l1_gated"], KT)
                    out_proj(3, l1w[:, 4], aT, KT, lambda t: None)
                    norm(4)
                    pe.wait_ge(S["l1_x2"], KT)
                    for c in range(KT):
                        linear(("ffk", c), l1w[:, 5], xm[:, 0], c * P, "l1_ffk_mm", "l1_relu", c + 1)
                    pe.wait_ge(S["l1_x2"], 2 * KT)
                    for t in range(NT):
                        b = take(pe, ("rr", t), "l1_rr", t + 1)
                        for k in range(KT):
                            last = mm(b[:, 0:D], xm[:, 1, k, t * P:(t + 1) * P], l1w[:, 6, k, :], start=(k == 0), stop=(k == KT - 1))
                        last.then_inc(S["l1_rr_mm"], 1)
                    pe.wait_ge(S["l1_kk"], KT)
                    out_proj(4, l1w[:, 7], aT, KT, lambda t: None)

                    def cross2(z, L, site):
                        def head_w(n):
                            return w2ring[:, n % 3, :].rearrange("p (w k d) -> p w k d", w=3, k=KT)

                        def query(h):
                            n = H2 * z + h
                            pe.wait_ge(S[f"w2_in{n % 3}"], 32 * (n // 3 + 1))
                            linear(("q2", n), head_w(n)[:, 0], hT, 0, "l2_q_mm", "l2_q", n + 1)

                        def keys_values(h):
                            n = H2 * z + h
                            w = head_w(n)
                            pe.wait_ge(S[f"w2_in{n % 3}"], 32 * (n // 3 + 1))
                            linear(("k2", n), w[:, 1], ctxT, 0, "l2_k_mm", "l2_k", n + 1)
                            b = take(pe, ("v2", n), "l2_v", n + 1)
                            for t in range(NT):
                                for k in range(KT):
                                    last = mm(b[:, t * P:(t + 1) * P], ctxT[:, k, t * P:(t + 1) * P], w[:, 2, k, :],
                                              start=(k == 0), stop=(k == KT - 1))
                            last.then_inc(S["l2_v_mm"], 1)

                        def scores(h):
                            n = H2 * z + h
                            pe.wait_ge(S["l2_q"], n + 1)
                            pe.wait_ge(S["l2_k"], n + 1)
                            pe.wait_ge(S["l2_kb"], n + 1)
                            b = take(pe, ("s2", n), "l2_sub", n + 1)
                            for t in range(NT):
                                for half in range(2):
                                    q0 = t * P + half * SEQ
                                    last = mm(b[half * SEQ:(half + 1) * SEQ, t * KX:(t + 1) * KX], q2[:, n % 2, q0:q0 + SEQ],
                                              k2[:, n % 2, 2 * t + half, :], start=True, stop=True)
                            last.then_inc(S["l2_scores"], 1)

                        def turn(h):
                            n = H2 * z + h
                            pe.wait_ge(S["l2_prob_a"], n + 1)
                            pe.wait_ge(S["l2_prob_b"], n + 1)
                            b = take(pe, ("tp2", n), "l2_PT", n + 1)
                            for t in range(NT):
                                last = nc.tensor.transpose(b[:, t * P:(t + 1) * P], pbd[:, n % 2, t, :], ident)
                            last.then_inc(S["l2_tp"], 1)

                        def weigh(h):
                            n = H2 * z + h
                            pe.wait_ge(S["l2_PT"], n + 1)
                            pe.wait_ge(S["l2_v"], n + 1)
                            b = take(pe, ("pv2", n), "l2_c", n + 1)
                            for t in range(NT):
                                last = mm(b[:, t * P:(t + 1) * P], v2[:, n % 2, t, :], PT2[:, n % 2, t, :], start=True, stop=True)
                            last.then_inc(S["l2_pv"], 1)

                        def project(t, heads):
                            if heads[0] == 0:
                                take(pe, ("proj", site, t), "x_updated", NT * site + t + 1)
                            b = held(("proj", site, t))
                            for h in heads:
                                last = mm(b[:, 0:D], c2T[:, h, t * P:(t + 1) * P], wo2[:, h, :],
                                          start=(h == 0), stop=(h == H2 - 1), skip_group_check=True)
                            if heads[-1] == H2 - 1:
                                last.then_inc(S["proj_mm"], 1)

                        keys_values(0)
                        pe.wait_ge(S[f"w2_in{(H2 * z + 1) % 3}"], 32 * ((H2 * z + 1) // 3 + 1))
                        norm_and_linears(L, [(("q2", H2 * z + h), head_w(H2 * z + h)[:, 0], 0, "l2_q_mm", "l2_q", H2 * z + h + 1)
                                             for h in range(2)])
                        for h in range(H2 - 1):
                            scores(h)
                            if h >= 1:
                                query(h + 1)
                            keys_values(h + 1)
                            if h >= 1:
                                weigh(h - 1)
                            turn(h)
                        early, late = range(H2 - 2), range(H2 - 2, H2)
                        scores(H2 - 1)
                        weigh(H2 - 2)
                        pe.wait_ge(S["wo_in"], 16 * (z + 1))
                        pe.wait_ge(S["l2_c"], H2 * z + len(early))
                        project(0, early)
                        turn(H2 - 1)
                        project(1, early)
                        weigh(H2 - 1)
                        project(2, early)
                        pe.wait_ge(S["l2_c"], H2 * (z + 1))
                        for t in range(NT - 1):
                            project(t, late)
                        project(NT - 1, range(H2))

                    cross2(0, 5, 5)
                    cross2(1, 6, 6)
                    mlp(1, 7, 7)
                    pe.wait_ge(s_wl3, 16)
                    w3 = weight("L3_qkv", 1)[:, 0, :].rearrange("p (w k n) -> p w k n", w=3, k=KT)
                    attention(2, 8, 8, w3[:, 0], w3[:, 1], w3[:, 2], ctxT, weight("L3_c"))
                    mlp(2, 9, 9)

                @block.scalar
                def _(act):
                    A = nc.scalar.activation

                    def norm(L, s, b):
                        for half in range(2):
                            h = slice(half * TOK // 2, (half + 1) * TOK // 2)
                            for k in range(KT):
                                act.wait_ge(S["ln_tp"], 2 * KT * L + KT * (half + 1))
                                A(hT[:, k, h], held(("ln", L, half))[:, k * TOK // 2:(k + 1) * TOK // 2],
                                  ACT.Identity, bias=col(b, k), scale=col(s, k)).then_inc(S["ln_hT"], 1)

                    def attention(a, L, bq, bk, ln_s, ln_b):
                        own = a == 0
                        for n, (m, key) in enumerate(QK_OWN if own else QK_ENC):
                            if n == (0 if own else KT):
                                norm(L, ln_s, ln_b)
                            act.wait_ge(S["qk_mm"], 4 * a + n + 1)
                            out, b = (kT, bk) if key else (qT, bq)
                            A(out[:, m, :], held(("qk", a, n))[:, :], ACT.Identity, bias=col(b, m)).then_inc(S["qk_T"], 1)
                        U = KT * NT
                        for s in range(1, U + LAG):
                            if s >= LAG:
                                n = U * a + s - LAG
                                act.wait_ge(S["att_tp"], n + 1)
                                if s - LAG >= 2:
                                    act.wait_ge(S["att_pv"], n - 1)
                                A(PTs[:, n % 2].rearrange("p h q -> p (h q)"), held(("tp", n))[:, :], ACT.Copy).then_inc(S["att_PT"], 1)
                            if s - 1 < U:
                                n = U * a + s - 1
                                act.wait_ge(S["att_sub"], n + 1)
                                A(T[:, n % TR], T[:, n % TR], ACT.Exp).then_inc(S["att_exp"], 1)

                    def mlp(m, bias, func):
                        for i in range(MT):
                            act.wait_ge(S["mlp_up_mm"], MT * m + i + 1)
                            A(gT[:, i, :], held(("mlp", m, i))[:, :], func, bias=col(bias, i)).then_inc(S["mlp_act"], 1)

                    act.wait_ge(s_small, SMALL)
                    for k in range(KT):
                        act.wait_ge(S["ctx_tp"], k + 1)
                        A(ctxT[:, k, :], held(("ctx", k))[:, :], ACT.Copy).then_inc(S["ctxT_ready"], 1)
                    attention(0, 0, "L0_bq_s", "L0_bk_s", "L0_ln1_s", "L0_ln1_b")
                    attention(1, 1, "L0_b_q", "L0_bk_c", "L0_ln2_s", "L0_ln2_b")
                    norm(2, "L0_ln3_s", "L0_ln3_b")
                    mlp(0, "L0_b1", ACT.Gelu_apprx_tanh)
                    norm(3, "L1_ln1_w", "L1_ln1_b")
                    for i, z in enumerate((zA, zB)):
                        act.wait_ge(S["l1_z_mm"], i + 1)
                        r = P if i == 0 else 32
                        A(z[0:r, :], held(f"z{i}")[0:r, :], ACT.Tanh).then_inc(S["l1_z"], 1)
                    act.wait_ge(S["l1_td_mm"], 1)
                    A(tw[0:64, :], held("td")[0:64, :], ACT.Tanh).then_inc(S["l1_td"], 1)

                    def rkvg(i, out, func):
                        for c in range(KT):
                            n = KT * (i - 1) + c
                            act.wait_ge(S["l1_rkvg_mm"], n + 1)
                            A(out[:, c, :], held(("rkvg", n))[:, :], func).then_inc(S["l1_rkvg"], 1)

                    rkvg(1, kT, ACT.Copy)
                    for c in range(KT):
                        act.wait_ge(S["l1_dec_mm"], c + 1)
                        A(dtmp[:, c, :], held(("dec", c))[:, :], ACT.Exp, bias=col("L1_time_decay", c)).then_inc(S["l1_dec"], 1)
                        act.wait_ge(S["l1_dec"], 2 * c + 1)
                        A(wdec[:, c, :].rearrange("p (b s) -> p b s", s=SLOT)[:, :, 1:SLOT],
                          dtmp[:, c, :].rearrange("p (b s) -> p b s", s=SEQ), ACT.Exp, scale=-1.0).then_inc(S["l1_dec"], 1)
                    rkvg(2, vT, ACT.Copy)
                    rkvg(3, qT, ACT.Copy)
                    rkvg(4, gateT, ACT.Silu)
                    act.wait_ge(s_chunk0, CHUNK0)
                    def gn_roots(c):
                        act.wait_ge(S["l1_cent"], c + 1)
                        A(gnsq, gn[:, c, :], ACT.Square).then_inc(S["l1_sq"], 1)
                        act.wait_ge(S["l1_var"], c + 1)
                        A(gn_sd, gn_var, ACT.Sqrt).then_inc(S["l1_sd"], 1)

                    for n in range(KT * S8):
                        if n >= 3:
                            act.wait_ge(S["l1_state"], n - 2)
                        A(kvA[:, n % 3, :].rearrange("p (b s) -> p b s", s=SLOT)[:, :, 0], s0[:, n // S8, :, n % S8], ACT.Copy)\
                            .then_inc(S["l1_slot"], 1)
                        if n == GN_AT:
                            gn_roots(0)
                    gn_roots(1)
                    for c in range(KT):
                        act.wait_ge(S["l1_gn_tp"], c + 1)
                        A(dtmp[:, c, :], held(("gn", c))[:, :], ACT.Identity, bias=col("L1_gn_b", c), scale=col("L1_gn_w", c)).then_inc(S["l1_gn_T"], 1)
                    norm(4, "L1_ln2_w", "L1_ln2_b")
                    for c in range(KT):
                        act.wait_ge(S["l1_ffk_mm"], c + 1)
                        A(dtmp[:, c, :], held(("ffk", c))[:, :], ACT.Relu).then_inc(S["l1_relu"], 1)
                    for t in range(NT):
                        act.wait_ge(S["l1_rr_mm"], t + 1)
                        A(gateT[:, t // 2, (t % 2) * D:(t % 2 + 1) * D], held(("rr", t))[:, 0:D], ACT.Sigmoid).then_inc(S["l1_rr"], 1)

                    def cross2(z, L, bq, bk, ln_s, ln_b):
                        def query(h):
                            n = H2 * z + h
                            act.wait_ge(S["l2_q_mm"], n + 1)
                            if n >= 2:
                                act.wait_ge(S["l2_scores"], n - 1)
                            A(q2[:, n % 2, :], held(("q2", n))[:, :], ACT.Identity, bias=col(bq, h)).then_inc(S["l2_q"], 1)

                        def keys(h):
                            n = H2 * z + h
                            act.wait_ge(S["l2_k_mm"], n + 1)
                            if n == 0:
                                act.wait_ge(S["x_updated"], 5 * NT)
                            if n >= 2:
                                act.wait_ge(S["l2_scores"], n - 1)
                            A(k2[:, n % 2, :, 0:SEQ], held(("k2", n))[:, :].rearrange("p (b k) -> p b k", b=NB), ACT.Identity,
                              bias=col(bk, h)).then_inc(S["l2_k"], 1)

                        keys(0)
                        norm(L, ln_s, ln_b)
                        query(0)
                        query(1)
                        for h in range(H2):
                            n = H2 * z + h
                            act.wait_ge(S["l2_sub"], n + 1)
                            A(E2[:, n % 2], E2[:, n % 2], ACT.Exp, scale=float(P) ** -0.5).then_inc(S["l2_exp"], 1)
                            if h + 1 < H2:
                                if h >= 1:
                                    query(h + 1)
                                keys(h + 1)
                            act.wait_ge(S["l2_tp"], n + 1)
                            if n >= 2:
                                act.wait_ge(S["l2_pv"], n - 1)
                            A(PT2[:, n % 2].rearrange("p t q -> p (t q)"), held(("tp2", n))[:, :], ACT.Copy).then_inc(S["l2_PT"], 1)

                    cross2(0, 5, "L2_bq1", "L2_bk1", "L2_ln1_s", "L2_ln1_b")
                    cross2(1, 6, "L2_bq2", "L2_bk2", "L2_ln2_s", "L2_ln2_b")
                    norm(7, "L2_lnm_s", "L2_lnm_b")
                    mlp(1, "L2_bf1", ACT.Gelu)
                    attention(2, 8, "L3_q_b", "L3_k_b", "L3_ln1_w", "L3_ln1_b")
                    norm(9, "L3_ln2_w", "L3_ln2_b")
                    mlp(2, "L3_fcb", ACT.Gelu_apprx_tanh)

                @block.vector
                def _(dve):
                    V = nc.vector
                    steps = [0]

                    def settle(ins):
                        steps[0] += 1
                        ins.then_inc(S["dve_step"], 1)
                        dve.wait_ge(S["dve_step"], steps[0])

                    def renew(site, biased, L, gate=False):
                        src = x_first if site is None else X
                        for s in range(NT + 2):
                            if s < NT and site is not None:
                                t = s
                                dve.wait_ge(S["proj_mm"], NT * site + t + 1)
                                y = held(("proj", site, t))[:, 0:D]
                                if gate:
                                    dve.wait_ge(S["l1_rr"], t + 1)
                                    tmp = rsZ[:, t // 2, (t % 2) * D:(t % 2 + 1) * D]
                                    settle(V.tensor_tensor(tmp, y, gateT[:, t // 2, (t % 2) * D:(t % 2 + 1) * D], ALU.mult))
                                    y = tmp
                                if biased is not None:
                                    dve.wait_ge(S["x_biased"], biased + 1)
                                V.tensor_tensor(X[:, t, :], X[:, t, :], y, ALU.add).then_inc(S["x_updated"], 1)
                            if 1 <= s <= NT and L is not None:
                                t = s - 1
                                if site is not None:
                                    dve.wait_ge(S["x_updated"], NT * site + t + 1)
                                settle(V.bn_stats(bst[:, t, :], src[:, t, :]))
                                V.bn_aggr(mv[:, t, :], bst[:, t, :]).then_inc(S["ln_mv"], 1)
                            if s >= 2 and L is not None:
                                t = s - 2
                                dve.wait_ge(S["ln_mv"], NT * L + t + 1)
                                dve.wait_ge(S["ln_rstd"], NT * L + t + 1)
                                V.tensor_scalar(xn[:, t, :], src[:, t, :], mv[:, t, 0:1], rstd[:, t:t + 1], ALU.subtract, ALU.mult)\
                                    .then_inc(S["ln_xn"], 1)

                    def attention(a, bv, mult):
                        dve.wait_ge(S["qk_T"], 4 * a + 1)
                        for h in range(HG):
                            V.tensor_scalar(kbd[:, 0, h, :], kT[:, 0, :], hmask[:, h:h + 1], None, ALU.mult).then_inc(S["kbd_dve"], 1)
                        def values():
                            for g in range(NT // 2):
                                dve.wait_ge(S["v_mm"], 2 * a + g + 1)
                                for half in range(2):
                                    for par in range(2):
                                        src = held(("v", a, g))[half * SEQ:(half + 1) * SEQ, :].rearrange(
                                            "p (t h r d) -> p t h r d", t=2, h=8, r=2)[:, :, :, par, :]
                                        brow = row(bv)[half * SEQ:(half + 1) * SEQ, :].rearrange(
                                            "p (h r d) -> p h r d", h=8, r=2)[:, :, par, :].unsqueeze(1).to_broadcast([SEQ, 2, 8, 16])
                                        dst = vbd[par * SEQ:(par + 1) * SEQ, 4 * g + half:4 * g + half + 3:2, :, par * 16:(par + 1) * 16]
                                        V.tensor_tensor(dst, src, brow, ALU.add).then_inc(S["v_bd"], 1)

                        if a > 0:
                            values()
                        U = KT * NT
                        for s in range(U + LAG + 1):
                            if s < U:
                                n, t = U * a + s, s % NT
                                dve.wait_ge(S["att_scores"], n + 1)
                                if n >= TR:
                                    dve.wait_ge(S["att_tp"], n - TR + 1)
                                if s == 0:
                                    dve.wait_ge(S["masks_ready"], 3)
                                m = mult(t).unsqueeze(1).to_broadcast([P, HG, SEQ])
                                V.scalar_tensor_tensor(T[:, n % TR], held(("s", n))[:, :].rearrange("p (h k) -> p h k", h=HG),
                                                       (D // H0) ** -0.5, m, ALU.mult, ALU.mult).then_inc(S["att_scaled"], 1)
                            if 1 <= s <= U:
                                n = U * a + s - 1
                                dve.wait_ge(S["att_masked"], n + 1)
                                V.tensor_reduce(nmax[:, n % TR, :], T[:, n % TR], AX, ALU.max, negate=True).then_inc(S["att_max"], 1)
                            if s == 2 and a == 0:
                                values()
                            if s >= LAG + 1:
                                u = s - LAG - 1
                                n, g, t = U * a + u, u // NT, u % NT
                                dve.wait_ge(S["att_pv"], n + 1)
                                b = held(("pv", n))
                                settle(V.reciprocal(rden[:, n % 2, :], b[:, P:2 * P]))
                                V.tensor_tensor(aT[:, g, t * P:(t + 1) * P], b[:, 0:P], rden[:, n % 2, :], ALU.mult).then_inc(S["att_out"], 1)

                    dve.wait_ge(s_small, SMALL)
                    dve.wait_ge(s_once, ONCE)
                    dve.wait_ge(s_chunk0, CHUNK0)
                    renew(None, None, 0)
                    attention(0, "L0_bv_s", lambda t: m_self)
                    renew(0, 0, 1)
                    attention(1, "L0_bv_c", lambda t: m_cross[:, t, :])
                    renew(1, 1, 2)
                    renew(2, 2, 3)
                    def shift(L, state_row):
                        dve.wait_ge(S["ln_hT"], 2 * KT * L + KT + 1)
                        h = hT[:, 0, :].rearrange("p (b s) -> p b s", s=SEQ)
                        o = sxT[:, 0, :].rearrange("p (b s) -> p b s", s=SEQ)
                        st = ctxT[:, 0, :].rearrange("p (b s) -> p b s", s=SEQ)[:, :, state_row:state_row + 1]
                        V.tensor_tensor(o[:, :, 1:SEQ], h[:, :, 0:SEQ - 1], h[:, :, 1:SEQ], ALU.subtract)
                        settle(V.tensor_tensor(o[:, :, 0:1], st, h[:, :, 0:1], ALU.subtract))

                    dve.wait_ge(S["ctxT_ready"], KT)
                    shift(3, 1)
                    for c in range(KT):
                        if c:
                            dve.wait_ge(S["l1_sx"], 2)
                        dve.wait_ge(S["ln_hT"], 7 * KT + c + 1)
                        V.scalar_tensor_tensor(xm[:, 1, c, :], sxT[:, c, :], col("L1_maa_x", c), hT[:, c, :], ALU.mult, ALU.add)\
                            .then_inc(S["l1_xm0"], 1)
                    for i, f in enumerate(FS):
                        for c in range(KT):
                            dve.wait_ge(S["l1_y_mm"], KT * i + c + 1)
                            if i == 1:
                                dve.wait_ge(S["l1_z_mm"], 2)
                            if i == 2:
                                dve.wait_ge(S["l1_td_mm"], 1)
                            if i > 2:
                                dve.wait_ge(S["l1_rkvg_mm"], KT * (i - 2))
                            V.scalar_tensor_tensor(xm[:, i % 2, c, :], held(("y", i, c))[:, :], col(f"L1_st{f}", c), sxT[:, c, :],
                                                   ALU.add, ALU.mult).then_inc(S["l1_y"], 1)
                    dve.wait_ge(S["l1_rkvg"], 3 * KT)
                    for c in range(KT):
                        V.scalar_tensor_tensor(rku[:, c, :], kT[:, c, :], col("L1_u", c), qT[:, c, :], ALU.mult, ALU.mult)\
                            .then_inc(S["l1_rku"], 1)
                    for c in range(KT):
                        dve.wait_ge(S["l1_rku_mm"], c + 1)
                        V.tensor_tensor(rku[:, c, :], held(("rku", c))[:, :], vT[:, c, :], ALU.mult).then_inc(S["l1_uv"], 1)
                    def group_norm(c):
                        og = bank[6 + c][:, :].rearrange("p (h j) -> p h j", j=S8)
                        xg = gn[:, c, :].rearrange("p (h j) -> p h j", j=S8)
                        dve.wait_ge(S["l1_rs_used"], S8 * (c + 1))
                        settle(V.tensor_reduce(small[:, 0:64], og, AX, ALU.add))
                        V.scalar_tensor_tensor(xg, small[:, 0:64].unsqueeze(2).to_broadcast([P, 64, S8]), -1.0 / S8,
                                               og, ALU.mult, ALU.add).then_inc(S["l1_cent"], 1)
                        dve.wait_ge(S["l1_sq"], c + 1)
                        settle(V.tensor_reduce(gn_var, gnsq.rearrange("p (h j) -> p h j", j=S8), AX, ALU.add))
                        V.tensor_scalar(gn_var, gn_var, 1.0 / S8, EPS, ALU.mult, ALU.add).then_inc(S["l1_var"], 1)
                        dve.wait_ge(S["l1_sd"], c + 1)
                        settle(V.reciprocal(gn_r, gn_sd))
                        settle(V.tensor_tensor(gn_sd, gn_r, gn_r, ALU.mult))
                        settle(V.tensor_tensor(gn_sd, gn_sd, gn_var, ALU.mult))
                        settle(V.tensor_scalar(gn_sd, gn_sd, -0.5, 1.5, ALU.mult, ALU.add))
                        settle(V.tensor_tensor(gn_r, gn_r, gn_sd, ALU.mult))
                        V.tensor_tensor(xg, xg, gn_r.unsqueeze(2).to_broadcast([P, 64, S8]), ALU.mult).then_inc(S["l1_gn"], 1)

                    for n in range(KT * S8 + 1):
                        if n == GN_AT:
                            group_norm(0)
                        if n < KT * S8:
                            c = n // S8
                            dve.wait_ge(S["l1_vb"], n + 1)
                            if n >= 3:
                                dve.wait_ge(S["l1_state"], n - 2)
                            V.tensor_tensor(kvA[:, n % 3, :].rearrange("p (b s) -> p b s", s=SLOT)[:, :, 1:SLOT],
                                            held(("vb", n))[:, :].rearrange("p (b s) -> p b s", s=SEQ),
                                            kT[:, c, :].rearrange("p (b s) -> p b s", s=SEQ), ALU.mult).then_inc(S["l1_kv"], 1)
                        if n >= 1:
                            m = n - 1
                            dve.wait_ge(S["l1_slot"], m + 1)
                            dve.wait_ge(S["l1_kv"], m + 1)
                            dve.wait_ge(S["l1_dec"], 4)
                            dve.wait_ge(S["slots_zero"], 1)
                            if m >= 3:
                                dve.wait_ge(S["l1_rs"], m - 2)
                            V.tensor_tensor_scan(stS[:, m % 3, :], wdec[:, m // S8, :], kvA[:, m % 3, :], 0.0, ALU.mult, ALU.add)\
                                .then_inc(S["l1_state"], 1)
                    group_norm(1)
                    for c in range(KT):
                        dve.wait_ge(S["l1_gn_T"], c + 1)
                        dve.wait_ge(S["l1_rkvg"], 4 * KT)
                        V.tensor_tensor(aT[:, c, :], dtmp[:, c, :], gateT[:, c, :], ALU.mult).then_inc(S["l1_gated"], 1)
                    renew(3, None, 4)
                    shift(4, 0)
                    for k, name in enumerate(("L1_fmk", "L1_fmr")):
                        for c in range(KT):
                            if c:
                                dve.wait_ge(S["l1_sx2"], 2)
                            dve.wait_ge(S["ln_hT"], 9 * KT + c + 1)
                            V.scalar_tensor_tensor(xm[:, k, c, :], sxT[:, c, :], col(name, c), hT[:, c, :], ALU.mult, ALU.add)\
                                .then_inc(S["l1_x2"], 1)
                    for c in range(KT):
                        dve.wait_ge(S["l1_relu"], c + 1)
                        V.tensor_tensor(aT[:, c, :], dtmp[:, c, :], dtmp[:, c, :], ALU.mult).then_inc(S["l1_kk"], 1)
                    renew(4, None, 5, gate=True)

                    def cross2(z, biv):
                        def value(h):
                            n = H2 * z + h
                            dve.wait_ge(S["l2_v_mm"], n + 1)
                            dve.wait_ge(S["l2_dbv"], n + 1)
                            if n >= 2:
                                dve.wait_ge(S["l2_pv"], n - 1)
                            V.tensor_tensor(v2[:, n % 2], held(("v2", n))[:, :].rearrange("p (t d) -> p t d", t=NT),
                                            dbv[:, n % 2, :].unsqueeze(1).to_broadcast([P, NT, P]), ALU.add).then_inc(S["l2_v"], 1)

                        def context(h):
                            n = H2 * z + h
                            dve.wait_ge(S["l2_pv"], n + 1)
                            V.tensor_scalar(c2T[:, h, :], held(("pv2", n))[:, :], col(biv, h), None, ALU.add).then_inc(S["l2_c"], 1)

                        value(0)
                        for h in range(H2):
                            n = H2 * z + h
                            dve.wait_ge(S["l2_scores"], n + 1)
                            s = held(("s2", n))[:, 0:NT * KX].rearrange("p (t k) -> p t k", t=NT)
                            V.tensor_reduce(nmax[:, n % 2, 0:NT], s, AX, ALU.max, negate=True).then_inc(S["l2_max"], 1)
                            dve.wait_ge(S["l2_max"], n + 1)
                            if n >= 2:
                                dve.wait_ge(S["l2_prob_a"], n - 1)
                                dve.wait_ge(S["l2_prob_b"], n - 1)
                            V.tensor_tensor(E2[:, n % 2], s, nmax[:, n % 2, 0:NT].unsqueeze(2).to_broadcast([P, NT, KX]), ALU.add)\
                                .then_inc(S["l2_sub"], 1)
                            dve.wait_ge(S["l2_exp"], n + 1)
                            den = small[:, 8 * (n % 2):8 * (n % 2) + 4]
                            rec = small[:, 8 * (n % 2) + 4:8 * (n % 2) + 8]
                            settle(V.tensor_reduce(den, E2[:, n % 2], AX, ALU.add))
                            V.reciprocal(rec, den).then_inc(S["l2_rden"], 1)
                            dve.wait_ge(S["l2_rden"], n + 1)
                            if n >= 2:
                                dve.wait_ge(S["l2_tp"], n - 1)
                            V.tensor_tensor(pbd[0:SEQ, n % 2, :, 0:SEQ], E2[0:SEQ, n % 2, :, 0:SEQ],
                                            rec[0:SEQ, :].unsqueeze(2).to_broadcast([SEQ, NT, SEQ]), ALU.mult).then_inc(S["l2_prob_a"], 1)
                            if h + 1 < H2:
                                value(h + 1)
                            if h >= 1:
                                context(h - 1)
                        context(H2 - 1)

                    cross2(0, "L2_biv1")
                    renew(5, 3, 6)
                    cross2(1, "L2_biv2")
                    renew(6, 4, 7)
                    renew(7, 5, 8)
                    attention(2, "L3_v_b", lambda t: m_key[:, t, :])
                    renew(8, 6, 9)
                    renew(9, 7, None)

                @block.gpsimd
                def _(pool):
                    G = nc.gpsimd
                    steps = [0]

                    def settle(ins):
                        steps[0] += 1
                        ins.then_inc(S["pool_step"], 1)
                        pool.wait_ge(S["pool_step"], steps[0])

                    def power(out, var, n, signal):
                        settle(G.tensor_scalar(out, var, 1.0, EPS, ALU.mult, ALU.add))
                        G.tensor_tensor(out, out, neghalf.to_broadcast([P, n]), ALU.pow).then_inc(S[signal], 1)

                    def norm(L):
                        for t in range(NT):
                            pool.wait_ge(S["ln_mv"], NT * L + t + 1)
                            if L:
                                pool.wait_ge(S["ln_xn"], NT * (L - 1) + t + 1)
                            power(rstd[:, t:t + 1], mv[:, t, 1:2], 1, "ln_rstd")

                    def bias(L, name):
                        pool.wait_ge(S["ln_xn"], NT * (L + 1))
                        G.tensor_tensor(X, x_first if L == 0 else X, row(name).unsqueeze(1).to_broadcast([P, NT, D]), ALU.add).then_inc(S["x_biased"], 1)

                    def attention(a, add):
                        if a == 2:
                            pool.wait_ge(S["x_updated"], 8 * NT)
                        pool.wait_ge(S["qk_T"], 4 * a + (3 if a == 0 else 2))
                        for h in range(HG):
                            G.tensor_scalar(kbd[:, 1, h, :], kT[:, 1, :], hmask[:, h:h + 1], 1.0, ALU.mult, ALU.mult).then_inc(S["kbd_pool"], 1)
                        U = KT * NT
                        for s in range(U + 1):
                            if s < U:
                                n = U * a + s
                                pool.wait_ge(S["att_scaled"], n + 1)
                                G.tensor_tensor(T[:, n % TR], T[:, n % TR], add(s % NT).unsqueeze(1).to_broadcast([P, HG, SEQ]), ALU.add)\
                                    .then_inc(S["att_masked"], 1)
                            if s >= 1:
                                n = U * a + s - 1
                                pool.wait_ge(S["att_max"], n + 1)
                                G.tensor_tensor(T[:, n % TR], T[:, n % TR], nmax[:, n % TR, :].unsqueeze(2).to_broadcast([P, HG, SEQ]), ALU.add)\
                                    .then_inc(S["att_sub"], 1)

                    pool.wait_ge(s_small, SMALL)
                    pool.wait_ge(s_once, ONCE)
                    norm(0)
                    bias(0, "L0_b_ao")
                    pool.wait_ge(s_chunk0, CHUNK0)
                    G.tensor_scalar(a_self, m_self, 10000.0, -10000.0, ALU.mult, ALU.add).then_inc(S["masks_ready"], 1)
                    G.tensor_scalar(a_cross, m_cross, 10000.0, -10000.0, ALU.mult, ALU.add).then_inc(S["masks_ready"], 1)
                    settle(G.tensor_copy(m_key, m_key8))
                    G.tensor_scalar(a_key, m_key, -1.0, NEG_BIG, ALU.add, ALU.mult).then_inc(S["masks_ready"], 1)
                    pool.wait_ge(S["masks_ready"], 3)
                    attention(0, lambda t: a_self)
                    norm(1)
                    bias(1, "L0_b_co")
                    attention(1, lambda t: a_cross[:, t, :])
                    norm(2)
                    bias(2, "L0_b2")
                    norm(3)

                    def shift(L, state_row, signal):
                        for c in range(1, KT):
                            pool.wait_ge(S["ln_hT"], 2 * KT * L + KT + c + 1)
                            h = hT[:, c, :].rearrange("p (b s) -> p b s", s=SEQ)
                            o = sxT[:, c, :].rearrange("p (b s) -> p b s", s=SEQ)
                            st = ctxT[:, c, :].rearrange("p (b s) -> p b s", s=SEQ)[:, :, state_row:state_row + 1]
                            G.tensor_tensor(o[:, :, 1:SEQ], h[:, :, 0:SEQ - 1], h[:, :, 1:SEQ], ALU.subtract).then_inc(S[signal], 1)
                            G.tensor_tensor(o[:, :, 0:1], st, h[:, :, 0:1], ALU.subtract).then_inc(S[signal], 1)

                    pool.wait_ge(S["ctxT_ready"], KT)
                    pool.wait_ge(S["x_updated"], 3 * NT)
                    G.memset(wdec.rearrange("p k (b s) -> p (k b) s", s=SLOT)[:, :, 0:1], 0.0).then_inc(S["slots_zero"], 1)
                    shift(3, 1, "l1_sx")
                    for i in range(5):
                        for c in range(KT):
                            pool.wait_ge(S["l1_y"], KT * i + c + 1)
                            G.tensor_tensor(xm[:, i % 2, c, :], xm[:, i % 2, c, :], hT[:, c, :], ALU.add).then_inc(S["l1_xm"], 1)
                    for m in range(KT * S8):
                            pool.wait_ge(S["l1_state"], m + 1)
                            if m == 0:
                                pool.wait_ge(S["l1_rkvg"], 3 * KT)
                            if m >= 3:
                                pool.wait_ge(S["l1_rs_used"], m - 2)
                            G.tensor_tensor(rsZ[:, m % 3, :].rearrange("p (b s) -> p b s", s=SEQ),
                                            stS[:, m % 3, :].rearrange("p (b s) -> p b s", s=SLOT)[:, :, 0:SEQ],
                                            qT[:, m // S8, :].rearrange("p (b s) -> p b s", s=SEQ), ALU.mult).then_inc(S["l1_rs"], 1)
                    norm(4)
                    shift(4, 0, "l1_sx2")
                    def cross2(z, L, bik, out_bias):
                        def head(h):
                            n = H2 * z + h
                            pool.wait_ge(S[f"w2_in{n % 3}"], 32 * (n // 3 + 1))
                            if n == 0:
                                pool.wait_ge(S["x_updated"], 5 * NT)
                            if n >= 2:
                                pool.wait_ge(S["l2_v"], n - 1)
                                pool.wait_ge(S["l2_scores"], n - 1)
                            G.tensor_tensor(dbv[:, n % 2, :], b2ring[:, n % 3, 0, :], b2ring[:, n % 3, 1, :], ALU.subtract).then_inc(S["l2_dbv"], 1)
                            G.tensor_copy(k2[:, n % 2, :, SEQ], col(bik, h).to_broadcast([P, NB])).then_inc(S["l2_kb"], 1)

                        norm(L)
                        head(0)
                        bias(L, out_bias)
                        for h in range(H2):
                            if h + 1 < H2:
                                head(h + 1)
                            n = H2 * z + h
                            pool.wait_ge(S["l2_rden"], n + 1)
                            pool.wait_ge(S["l2_exp"], n + 1)
                            pool.wait_ge(S["l2_kb"], min(n + 2, H2 * (z + 1)))
                            if n >= 2:
                                pool.wait_ge(S["l2_tp"], n - 1)
                            rec = small[SEQ:P, 8 * (n % 2) + 4:8 * (n % 2) + 8]
                            G.tensor_tensor(pbd[SEQ:P, n % 2, :, SEQ:P], E2[SEQ:P, n % 2, :, 0:SEQ],
                                            rec.unsqueeze(2).to_broadcast([SEQ, NT, SEQ]), ALU.mult).then_inc(S["l2_prob_b"], 1)
                            pool.wait_ge(S["l2_prob_b"], n + 1)

                    cross2(0, 5, "L2_bik1", "L2_bo1")
                    cross2(1, 6, "L2_bik2", "L2_bo2")
                    norm(7)
                    bias(7, "L2_bf2")
                    norm(8)
                    bias(8, "L3_cb")
                    attention(2, lambda t: a_key[:, t, :])
                    norm(9)
                    bias(9, "L3_pb")

                @block.sync
                def _(sp):
                    sp.dma_start(mlp_w, t_mlp[0]).then_inc(S["mlp_in"], 16)

                    def head_weights(n):
                        if n >= 3:
                            sp.wait_ge(S["l2_q_mm"], n - 2)
                            sp.wait_ge(S["l2_v_mm"], n - 2)
                            sp.wait_ge(S["l2_dbv"], n - 2)
                        sp.dma_start(w2ring[:, n % 3, :], t_w2[n]).then_inc(S[f"w2_in{n % 3}"], 16)
                        sp.dma_start(b2ring[:, n % 3].rearrange("p w d -> p (w d)"), t_b2[n].partition_broadcast(P))\
                            .then_inc(S[f"w2_in{n % 3}"], 16)

                    for n in range(3):
                        head_weights(n)
                    sp.wait_ge(S["x_updated"], 3 * NT)
                    sp.dma_start(mlp_w, t_mlp[1]).then_inc(S["mlp_in"], 16)
                    sp.wait_ge(S["x_updated"], 5 * NT)
                    sp.dma_start(flat(wo2), t_wo2[0]).then_inc(S["wo_in"], 16)
                    for n in range(3, 2 * H2):
                        if n == H2 + 3:
                            sp.wait_ge(S["x_updated"], 6 * NT)
                            sp.dma_start(flat(wo2), t_wo2[1]).then_inc(S["wo_in"], 16)
                        head_weights(n)
                    sp.wait_ge(S["x_updated"], 8 * NT)
                    sp.dma_start(mlp_w, t_mlp[2]).then_inc(S["mlp_in"], 16)
                    load_chunk(sp, lambda t: t[1:CHUNKS + 1][chunk], S["next_in"], S["next_in"])
                    sp.wait_ge(S["next_in"], 16 + CHUNK0)
                    for t in range(NT):
                        sp.wait_ge(S["x_updated"], 9 * NT + t + 1)
                        sp.dma_start(t_out[chunk][:, t * D:(t + 1) * D], X[:, t, :]).then_inc(S["out_done"], 16)
                    sp.wait_ge(S["out_done"], 16 * NT)
            nc.gpsimd.sem_clear(range(nums[0], nums[0] + len(nums)))
            nc.all_engine_barrier()


def shape_constants():
    p = np.arange(P)
    sel = np.zeros((P, S8, P), np.float32)
    for j in range(S8):
        sel[:, j, :] = (p[:, None] // S8 == p[None, :] // S8) & (p[:, None] % S8 == j)
    parts = {
        "ident": np.eye(P),
        "sel": sel.reshape(P, -1),
        "headmask": p[:, None] // 16 == np.arange(HG)[None, :],
        "ones2": p[:, None] // SEQ == np.arange(32)[None, :] // 16,
        "heads8": p[:, None] // S8 == np.arange(HL1)[None, :],
        "block8": p[:, None] // S8 == p[None, :] // S8,
    }
    return np.concatenate([parts[n].astype(np.float32) for n, _ in CONSTS], axis=1)


def kernel(**inputs):
    import concourse.bacc as bacc
    from concourse.bass_utils import run_bass_kernel_spmd as run

    def g(name):
        return np.asarray(inputs[name])

    def L(i, name):
        return g(f"L{i}_xattn_{name}")

    def rows_on_partitions(w):
        k = w.shape[0] // P
        return w.reshape(k, P, w.shape[1]).transpose(1, 0, 2).reshape(P, -1)

    def pad_rows(w):
        out = np.zeros((P, w.shape[1]), w.dtype)
        out[:w.shape[0]] = w
        return out

    def tokens(a):
        n = a.shape[-1]
        return a.reshape(CHUNKS, NT, P, n).transpose(0, 2, 1, 3).reshape(CHUNKS, P, NT * n)

    x, enc = g("x"), g("ctx_2048")
    st = enc[:, 2:2 + S8, :].reshape(CHUNKS, NB, KT, P, S8).transpose(0, 3, 2, 1, 4).reshape(CHUNKS, P, -1)
    bqkv, bkv = L(0, "b_qkv"), L(0, "b_kv")
    stack = L(1, "maa_stack").reshape(5, D)
    vec = {
        "L0_ln1_s": L(0, "ln1_s"), "L0_ln1_b": L(0, "ln1_b"), "L0_bq_s": bqkv[:D], "L0_bk_s": bqkv[D:2 * D],
        "L0_ln2_s": L(0, "ln2_s"), "L0_ln2_b": L(0, "ln2_b"), "L0_b_q": L(0, "b_q"), "L0_bk_c": bkv[:D],
        "L0_ln3_s": L(0, "ln3_s"), "L0_ln3_b": L(0, "ln3_b"), "L1_ln1_w": L(1, "ln1_w"), "L1_ln1_b": L(1, "ln1_b"),
        "L1_ln2_w": L(1, "ln2_w"), "L1_ln2_b": L(1, "ln2_b"), "L1_maa_x": L(1, "maa_x"),
        "L1_time_decay": L(1, "time_decay"), "L1_u": L(1, "u"), "L1_gn_w": L(1, "gn_w"), "L1_gn_b": L(1, "gn_b"),
        "L1_fmk": L(1, "ffn_maa_k"), "L1_fmr": L(1, "ffn_maa_r"),
        "L2_ln1_s": L(2, "ln1_scale"), "L2_ln1_b": L(2, "ln1_offset"), "L2_ln2_s": L(2, "ln2_scale"),
        "L2_ln2_b": L(2, "ln2_offset"), "L2_lnm_s": L(2, "ln_mlp_scale"), "L2_lnm_b": L(2, "ln_mlp_offset"),
        "L3_ln1_w": L(3, "ln1_w"), "L3_ln1_b": L(3, "ln1_b"), "L3_q_b": L(3, "q_b"), "L3_k_b": L(3, "k_b"),
        "L3_ln2_w": L(3, "ln2_w"), "L3_ln2_b": L(3, "ln2_b"),
        "L0_b1": L(0, "b1"), "L2_bf1": L(2, "b_fc1"), "L3_fcb": L(3, "fc_b"),
        "L2_bq1": L(2, "bq1"), "L2_bk1": L(2, "bk1"), "L2_bik1": L(2, "bias_k1"), "L2_biv1": L(2, "bias_v1"),
        "L2_bq2": L(2, "bq2"), "L2_bk2": L(2, "bk2"), "L2_bik2": L(2, "bias_k2"), "L2_biv2": L(2, "bias_v2"),
        "L0_bv_s": bqkv[2 * D:], "L0_b_ao": L(0, "b_ao"), "L0_bv_c": bkv[D:], "L0_b_co": L(0, "b_co"), "L0_b2": L(0, "b2"),
        "L2_bo1": L(2, "bo1"), "L2_bo2": L(2, "bo2"), "L2_bf2": L(2, "b_fc2"),
        "L3_v_b": L(3, "v_b"), "L3_cb": L(3, "cproj_b"), "L3_pb": L(3, "proj_b"),
    }
    for i in range(5):
        vec[f"L1_st{i}"] = stack[i]
    cols = np.concatenate([vec[n].reshape(-1, P).T for n in COL2 + COL8 + COL16], axis=1)
    rows = np.concatenate([vec[n].reshape(-1) for n in ROWS])
    m2 = L(1, "maa_w2")
    wres = {
        "L0_qkv": rows_on_partitions(L(0, "w_qkv")), "L0_ao": rows_on_partitions(L(0, "w_ao")),
        "L0_q": rows_on_partitions(L(0, "w_q")), "L0_kv": rows_on_partitions(L(0, "w_kv")),
        "L0_co": rows_on_partitions(L(0, "w_co")),
        "L1_m1": rows_on_partitions(L(1, "maa_w1")), "L1_m2a": m2[:4].reshape(P, D), "L1_m2b": pad_rows(m2[4]),
        "L1_td1": rows_on_partitions(L(1, "td_w1")), "L1_td2": pad_rows(L(1, "td_w2")),
        "L1_W": np.concatenate([rows_on_partitions(L(1, n).T) for n in ("Wr", "Wk", "Wv", "Wg", "Wo", "Wfk", "Wfr", "Wfv")], axis=1),
        "L3_qkv": np.concatenate([rows_on_partitions(L(3, n)) for n in ("q_w", "k_w", "v_w")], axis=1),
        "L3_c": rows_on_partitions(L(3, "cproj_w")),
    }
    wres = np.concatenate([wres[n] for n, _ in WRES], axis=1)
    mlp = np.stack([np.concatenate([rows_on_partitions(a), rows_on_partitions(b)], axis=1) for a, b in
                    ((L(0, "w1"), L(0, "w2")), (L(2, "w_fc1"), L(2, "w_fc2")), (L(3, "fc_w"), L(3, "proj_w")))])
    w2, b2, wo2 = [], [], []
    for z in (1, 2):
        w = np.stack([L(2, f"w{n}{z}").reshape(KT, P, H2, P) for n in "qkv"])
        w2.append(w.transpose(3, 2, 0, 1, 4).reshape(H2, P, -1))
        b2.append(np.stack([L(2, f"bv{z}").reshape(H2, P), L(2, f"bias_v{z}").reshape(H2, P)], axis=1).reshape(H2, 2 * P))
        wo2.append(L(2, f"wo{z}").reshape(H2, P, D).transpose(1, 0, 2).reshape(P, -1))
    arrays = {
        "x_in": tokens(x), "ctx_in": tokens(enc), "state": st,
        "ltor": g("mask_1x1xSxS2_fc1").reshape(SEQ, SEQ), "cross": tokens(g("mask_Bx1xSxS2_ff1").reshape(NSEQ, SEQ, SEQ)),
        "bmask": g("mask_BxS2_bf1").view(np.uint8).reshape(CHUNKS, NT, 2, SEQ).transpose(0, 2, 1, 3).reshape(CHUNKS, 2, NT * SEQ),
        "cols": cols, "rows": rows, "consts": shape_constants(), "wres": wres, "mlp": mlp,
        "w2": np.concatenate(w2), "b2": np.concatenate(b2), "wo2": np.stack(wo2),
    }
    for k in ("x_in", "ctx_in", "state", "cross", "bmask"):
        arrays[k] = np.concatenate([arrays[k], arrays[k][:1]])
    arrays = {k: np.ascontiguousarray(v) for k, v in arrays.items()}
    nc = bacc.Bacc("TRN2", target_bir_lowering=False, num_devices=1)
    args = [nc.dram_tensor(f"in_{k}", v.shape, mybir.dt.from_np(v.dtype), kind="ExternalInput").ap() for k, v in arrays.items()]
    out = nc.dram_tensor("out_0", (CHUNKS, P, NT * D), mybir.dt.float32, kind="ExternalOutput").ap()
    build(nc, *args, out)
    r = run(nc, [{f"in_{k}": v for k, v in arrays.items()}], core_ids=[0]).results[0]["out_0"]
    return r.reshape(CHUNKS, P, NT, D).transpose(0, 2, 1, 3).reshape(NSEQ, SEQ, D)
```

```python
import numpy as np
import concourse.bass as bass
from concourse import mybir
from contextlib import ExitStack

P = 128
D = 256
KT = D // P
NSEQ, SEQ = 32, 64
CHUNKS = 4
NB = NSEQ // CHUNKS
TOK = NB * SEQ
NT = TOK // P
HF = 4 * D
MT = HF // P
EPS = 1e-5
H0 = 16
HG = 8
H2 = 16
KX = SEQ + 1
SLOT = SEQ + 1
S8 = 8
HL1 = P // S8
FS = [1, 0, 2, 3, 4]
LAG = 3
TR = LAG + 3
QK_OWN = [(0, True), (0, False), (1, True), (1, False)]
QK_ENC = [(0, True), (1, True), (0, False), (1, False)]
CR = 4
WR = 4
SUMLAG = 5
NEG_BIG = float(np.finfo(np.float32).max)

COL2 = ["L0_ln1_s", "L0_ln1_b", "L0_bq_s", "L0_bk_s", "L0_ln2_s", "L0_ln2_b", "L0_b_q", "L0_bk_c",
        "L0_ln3_s", "L0_ln3_b", "L1_ln1_w", "L1_ln1_b", "L1_ln2_w", "L1_ln2_b", "L1_maa_x",
        "L1_st0", "L1_st1", "L1_st2", "L1_st3", "L1_st4", "L1_time_decay", "L1_u", "L1_gn_w",
        "L1_gn_b", "L1_fmk", "L1_fmr", "L2_ln1_s", "L2_ln1_b", "L2_ln2_s", "L2_ln2_b",
        "L2_lnm_s", "L2_lnm_b", "L3_ln1_w", "L3_ln1_b", "L3_q_b", "L3_k_b", "L3_ln2_w", "L3_ln2_b"]
COL8 = ["L0_b1", "L2_bf1", "L3_fcb"]
COL16 = ["L2_bq1", "L2_bk1", "L2_bik1", "L2_biv1", "L2_bq2", "L2_bk2", "L2_bik2", "L2_biv2"]
COL = {}
_at = 0
for _names, _w in ((COL2, KT), (COL8, MT), (COL16, H2)):
    for _n in _names:
        COL[_n] = _at
        _at += _w
NCOL = _at
ROWS = ["L0_bv_s", "L0_b_ao", "L0_bv_c", "L0_b_co", "L0_b2", "L2_bo1", "L2_bo2", "L2_bf2",
        "L3_v_b", "L3_cb", "L3_pb"]
CONSTS = [("ident", P), ("sel", S8 * P), ("headmask", HG), ("ones2", 32), ("heads8", HL1), ("block8", P)]
CAT = {}
_at = 0
for _n, _w in CONSTS:
    CAT[_n] = (_at, _w)
    _at += _w
NCONST = _at
WRES = [("L0_qkv", KT * 3 * D), ("L0_ao", KT * D), ("L0_q", KT * D), ("L0_kv", KT * 2 * D), ("L0_co", KT * D),
        ("L1_m1", KT * 160), ("L1_m2a", D), ("L1_m2b", D), ("L1_td1", KT * 64), ("L1_td2", D),
        ("L1_W", 8 * KT * D), ("L3_qkv", 3 * KT * D), ("L3_c", KT * D)]
WAT = {}
_at = 0
for _n, _w in WRES:
    WAT[_n] = (_at, _w)
    _at += _w
NWRES = _at


def build(nc, t_x, t_ctx, t_state, t_ltor, t_cross, t_bmask, t_cols, t_rows, t_consts, t_wres, t_mlp,
          t_w2, t_b2, t_wo2, t_out):
    f32 = mybir.dt.float32
    f32r = mybir.dt.float32r
    ALU = mybir.AluOpType
    ACT = mybir.ActivationFunctionType
    AX = mybir.AxisListType.X
    ctx = ExitStack()
    with ctx:
        def sb(name, cols, dt=f32):
            return ctx.enter_context(nc.sbuf_tensor(name, [P, cols], dt))[:, :]

        def view(ap, pat, **kw):
            return ap.rearrange(pat, **kw)

        cols = sb("cols", NCOL)
        rows = view(sb("rows", len(ROWS) * D), "p (r d) -> p r d", d=D)
        consts = sb("consts", NCONST)
        wres = sb("wres", NWRES)
        mlp_w = sb("mlp_w", KT * HF + MT * D)
        X = view(sb("X", NT * D), "p (t d) -> p t d", d=D)
        xn = view(sb("xn", NT * D), "p (t d) -> p t d", d=D)
        gn = xn.rearrange("p t d -> p (t d)").rearrange("p (c n) -> p c n", c=KT)
        ctxT = view(sb("ctxT", KT * TOK), "p (k n) -> p k n", k=KT)
        hT = view(sb("hT", KT * TOK), "p (k n) -> p k n", k=KT)
        qT = view(sb("qT", KT * TOK), "p (k n) -> p k n", k=KT)
        kT = view(sb("kT", KT * TOK), "p (k n) -> p k n", k=KT)
        aT = view(sb("aT", KT * TOK), "p (k n) -> p k n", k=KT)
        vbd = view(sb("vbd", NB * 8 * 32), "p (b h c) -> p b h c", b=NB, h=8)
        pbd = view(sb("pbd", 2 * NT * P), "p (s t k) -> p s t k", s=2, t=NT)
        w2ring = view(sb("w2ring", 3 * 3 * KT * P), "p (s w) -> p s w", s=3)
        b2ring = view(sb("b2ring", 3 * 2 * P), "p (s w d) -> p s w d", s=3, w=2)
        dbv = view(sb("dbv", 2 * P), "p (s d) -> p s d", s=2)
        m_self = sb("m_self", SEQ)
        m_cross = view(sb("m_cross", NT * SEQ), "p (t k) -> p t k", t=NT)
        m_key8 = view(sb("m_key8", NT * SEQ, mybir.dt.uint8), "p (t k) -> p t k", t=NT)
        m_key = view(sb("m_key", NT * SEQ), "p (t k) -> p t k", t=NT)
        a_self = sb("a_self", SEQ)
        a_cross = view(sb("a_cross", NT * SEQ), "p (t k) -> p t k", t=NT)
        a_key = view(sb("a_key", NT * SEQ), "p (t k) -> p t k", t=NT)
        s0 = view(sb("s0", KT * NB * S8), "p (k b j) -> p k b j", k=KT, b=NB)
        bst = view(sb("bst", NT * 6), "p (t s) -> p t s", t=NT)
        mv = view(sb("mv", NT * 2), "p (t s) -> p t s", t=NT)
        rstd = sb("rstd", NT)
        neghalf = sb("neghalf", 1)
        nmax = view(sb("nmax", TR * HG), "p (s h) -> p s h", s=TR)
        small = sb("small", 2 * 64)
        gn_var = sb("gn_var", 64)
        gn_sd = sb("gn_sd", 64)
        gn_r = sb("gn_r", 64)
        ARENA = 16920
        with nc.sbuf_tensor("arena", [P, ARENA], f32) as arena_t:
            arena = arena_t[:, :]
        used = {}

        def carve(layer, n):
            at = used.get(layer, 0)
            used[layer] = at + n
            assert used[layer] <= ARENA, (layer, used[layer])
            return arena[:, at:at + n]

        kbd = view(carve("att", KT * HG * TOK), "p (g h n) -> p g h n", g=KT, h=HG)
        T = view(carve("att", TR * TOK), "p (s h k) -> p s h k", s=TR, h=HG)
        PTs = view(carve("att", 2 * TOK), "p (s h q) -> p s h q", s=2, h=4)
        rden = view(carve("att", 2 * P), "p (s q) -> p s q", s=2)
        inputs_at = used["att"]
        ctx_tok = view(carve("att", NT * D), "p (t d) -> p t d", t=NT)
        x_first = view(carve("att", NT * D), "p (t d) -> p t d", t=NT)
        sxT = view(carve("l1", KT * TOK), "p (k n) -> p k n", k=KT)
        xm = view(carve("l1", 2 * KT * TOK), "p (s k n) -> p s k n", s=2, k=KT)
        zA = carve("l1", TOK)
        zB = carve("l1", TOK)
        tw = carve("l1", TOK)
        dtmp = view(carve("l1", KT * TOK), "p (k n) -> p k n", k=KT)
        wdec = view(carve("l1", KT * NB * SLOT), "p (k n) -> p k n", k=KT)
        vT = view(carve("l1", KT * TOK), "p (k n) -> p k n", k=KT)
        gateT = view(carve("l1", KT * TOK), "p (k n) -> p k n", k=KT)
        rku = view(carve("l1", KT * TOK), "p (k n) -> p k n", k=KT)
        rsZ = view(carve("l1", 3 * TOK), "p (s n) -> p s n", s=3)
        scan_at = used["l1"]
        kvA = view(carve("l1", 3 * NB * SLOT), "p (s n) -> p s n", s=3)
        stS = view(carve("l1", 3 * NB * SLOT), "p (s n) -> p s n", s=3)
        gnsq = dtmp[:, 1, :]
        q2 = view(carve("l2", 2 * TOK), "p (s n) -> p s n", s=2)
        k2 = view(carve("l2", 2 * NB * KX), "p (s b k) -> p s b k", s=2, b=NB)
        v2 = view(carve("l2", 2 * TOK), "p (s t d) -> p s t d", s=2, t=NT)
        E2 = view(carve("l2", 2 * NT * KX), "p (s t k) -> p s t k", s=2, t=NT)
        PT2 = view(carve("l2", 2 * TOK), "p (s t q) -> p s t q", s=2, t=NT)
        wo_ring = view(carve("l2", WR * D), "p (s d) -> p s d", s=WR)
        g_full = qT
        with ExitStack() as over:
            g_hi, g_lo = (view(over.enter_context(nc.sbuf_tensor(n, [P, MT * TOK], f32r))[:, :], "p (m n) -> p m n", m=MT)
                          for n in ("g_hi", "g_lo"))
            wd_hi, wd_lo = (view(over.enter_context(nc.sbuf_tensor(n, [P, MT * D], f32r))[:, :], "p (m d) -> p m d", m=MT)
                            for n in ("wd_hi", "wd_lo"))
        assert 2 * MT * (TOK + D) <= inputs_at
        sb("arena_below", used["l2"])
        c_hi, c_lo = (view(sb(n, CR * TOK, f32r), "p (s n) -> p s n", s=CR) for n in ("c_hi", "c_lo"))
        wo_hi, wo_lo = (view(sb(n, 2 * D, f32r), "p (s d) -> p s d", s=2) for n in ("wo_hi", "wo_lo"))
        l2_end = used["l2"] + 2 * CR * TOK + 4 * D
        hT_hi, hT_lo = (view(sb(n, KT * TOK, f32r), "p (k n) -> p k n", k=KT) for n in ("hT_hi", "hT_lo"))
        w2_hi, w2_lo = (view(sb(n, 2 * 2 * KT * P, f32r), "p (s w) -> p s w", s=2) for n in ("w2_hi", "w2_lo"))
        assert l2_end + 2 * KT * TOK + 8 * KT * P >= max(used["l1"], used["att"])
        assert l2_end + 2 * KT * TOK >= scan_at
        ctx_hi, ctx_lo = (view(sb(n, KT * TOK, f32r), "p (k n) -> p k n", k=KT) for n in ("ctx_hi", "ctx_lo"))

        bank = [ctx.enter_context(nc.psum_tensor(f"bank{i}", [P, 512], f32)) for i in range(8)]
        RING = 6

        def col(name, k=0):
            return cols[:, COL[name] + k:COL[name] + k + 1]

        def row(name):
            return rows[:, ROWS.index(name), :]

        def const(name):
            a, w = CAT[name]
            return consts[:, a:a + w]

        def weight(name, k=KT):
            a, w = WAT[name]
            return view(wres[:, a:a + w], "p (k n) -> p k n", k=k)

        ident = const("ident")
        sel = view(const("sel"), "p (j c) -> p j c", j=S8)
        hmask = const("headmask")
        w1 = view(mlp_w[:, 0:KT * HF], "p (k n) -> p k n", k=KT)
        w2 = view(mlp_w[:, KT * HF:], "p (m n) -> p m n", m=MT)
        l1w = view(weight("L1_W", 1)[:, 0, :], "p (w k n) -> p w k n", w=8, k=KT)

        def sem(name):
            return ctx.enter_context(nc.semaphore(name))

        s_small, s_qkv, s_wl0, s_wl1, s_wl3, s_once, s_ctx0, s_chunk0 = map(
            sem, ("vectors_in", "w_qkv_in", "w_l0_in", "w_l1_in", "w_l3_in", "preset", "ctx0_in", "chunk0_in"))
        names = """next_in mlp_in wo_in0 wo_in1 wo_in2 wo_in3 w2_in0 w2_in1 w2_in2 out_done
            masks_ready slots_zero ctx_tp ctxT_ready
            dve_step pool_step act_step
            ln_mv ln_rstd ln_xn ln_tp ln_hT x_biased x_updated
            qk_mm qk_T kbd_dve kbd_pool v_mm v_bd att_scores att_scaled att_masked att_max att_sub att_exp
            att_tp att_PT att_pv att_out proj_mm
            mlp_up_mm mlp_act mlp_ghi mlp_g mlp_whi mlp_wlo
            l1_sx l1_xm0 l1_z_mm l1_z l1_y_mm l1_y l1_xm l1_td_mm l1_td l1_dec_mm l1_dec l1_rkvg_mm l1_rkvg
            l1_rku l1_rku_mm l1_uv l1_vb l1_kv l1_slot l1_state l1_rs l1_rs_used l1_og l1_cent l1_sq l1_var l1_sd
            l1_gn l1_gn_tp l1_gn_T l1_gated l1_sx2 l1_x2 l1_ffk_mm l1_relu l1_kk l1_rr_mm l1_rr
            ctx_hi ctx_lo l2_hhi l2_hlo l2_whi l2_wlo l2_dbv l2_q_mm l2_q l2_k_mm l2_k l2_kb l2_v_mm l2_v l2_scores l2_max l2_sub l2_exp l2_prob_a
            l2_prob_b l2_rden l2_tp l2_PT l2_pv l2_chi l2_c l2_c_used l2_wohi l2_wolo""".split()
        loop_sems = [sem(n) for n in names]
        S = dict(zip(names, loop_sems))
        nums = [s.num for s in loop_sems]
        assert nums == list(range(nums[0], nums[0] + len(nums)))

        def flat(ap):
            return ap.rearrange("p a b -> p (a b)")

        def load_chunk(queue, c, first, rest):
            queue.dma_start(flat(ctx_tok), c(t_ctx)).then_inc(first, 16)
            queue.dma_start(flat(x_first), c(t_x)).then_inc(rest, 16)
            queue.dma_start(flat(m_cross), c(t_cross)).then_inc(rest, 16)
            for half in range(2):
                queue.dma_start(flat(m_key8[half * SEQ:(half + 1) * SEQ]),
                                c(t_bmask)[half, :].partition_broadcast(SEQ)).then_inc(rest, 16)
            queue.dma_start(s0.rearrange("p k b j -> p (k b j)"), c(t_state)).then_inc(rest, 16)

        def load_weights(queue, s, first, last):
            a, b = WAT[first][0], WAT[last][0] + WAT[last][1]
            queue.dma_start(wres[:, a:b], t_wres[:, a:b]).then_inc(s, 16)

        with nc.Block() as block:
            @block.sync
            def _(sp):
                sp.dma_start(consts[:, 0:P], t_consts[:, 0:P]).then_inc(s_small, 16)
                load_chunk(sp, lambda t: t[0], s_ctx0, s_chunk0)
                load_weights(sp, s_wl1, "L1_m1", "L1_W")

            @block.scalar
            def _(act):
                act.dma_start(cols, t_cols).then_inc(s_small, 16)
                load_weights(act, s_qkv, "L0_qkv", "L0_qkv")
                act.dma_start(m_self[0:SEQ, :], t_ltor).then_inc(s_small, 16)
                act.dma_start(m_self[SEQ:P, :], t_ltor).then_inc(s_small, 16)
                act.dma_start(consts[:, P:], t_consts[:, P:]).then_inc(s_small, 16)
                act.dma_start(rows.rearrange("p r d -> p (r d)"), t_rows.partition_broadcast(P)).then_inc(s_small, 16)
                load_weights(act, s_wl0, "L0_ao", "L0_co")
                load_weights(act, s_wl3, "L3_qkv", "L3_c")

            @block.gpsimd
            def _(pool):
                nc.gpsimd.memset(neghalf, -0.5).then_inc(s_once, 1)
                nc.gpsimd.memset(vbd, 0.0).then_inc(s_once, 1)
                nc.gpsimd.memset(pbd, 0.0).then_inc(s_once, 1)
        SMALL, ONCE = 6 * 16, 3
        CHUNK0 = 5 * 16

        with nc.Fori(0, CHUNKS) as chunk:
            with nc.Block() as block:

                ring = {"n": 0, "freed": [None] * RING, "at": {}}

                def take(pe, tag, stage, n):
                    i = ring["n"] % RING
                    ring["n"] += 1
                    if ring["freed"][i]:
                        pe.wait_ge(S[ring["freed"][i][0]], ring["freed"][i][1])
                    ring["freed"][i] = (stage, n)
                    ring["at"][tag] = i
                    return bank[i]

                def held(tag):
                    return bank[ring["at"][tag]]

                @block.tensor
                def _(pe):
                    mm = nc.tensor.matmul

                    def transposes():
                        b = [take(pe, ("ctx", k), "ctxT_ready", k + 1) for k in range(KT)]
                        for t in range(NT):
                            for k in range(KT):
                                last = nc.tensor.transpose(b[k][:, t * P:(t + 1) * P], ctx_tok[:, t, k * P:(k + 1) * P], ident)
                                if t == NT - 1:
                                    last.then_inc(S["ctx_tp"], 1)

                    def norm(L, before_last=None):
                        b = [take(pe, ("ln", L, half), "ln_hT", 2 * KT * L + KT * (half + 1)) for half in range(2)]
                        for t in range(NT):
                            if t == NT - 1 and before_last:
                                before_last()
                            pe.wait_ge(S["ln_xn"], NT * L + t + 1)
                            for k in range(KT):
                                o = k * TOK // 2 + t % 2 * P
                                last = nc.tensor.transpose(b[t // 2][:, o:o + P], xn[:, t, k * P:(k + 1) * P], ident)
                                if t % 2:
                                    last.then_inc(S["ln_tp"], 1)

                    def norm_and_linears(L, jobs):
                        banks = {}

                        def half(job, part):
                            tag, w, m0, signal, used_by, n = job
                            if part == 0:
                                banks[tag] = take(pe, tag, used_by, n)
                            h = slice(part * TOK // 2, (part + 1) * TOK // 2)
                            for k in range(KT):
                                last = mm(banks[tag][:, h], w[:, k, m0:m0 + P], hT[:, k, h], start=(k == 0), stop=(k == KT - 1))
                            if part:
                                last.then_inc(S[signal], 1)

                        early = len(jobs) // 2

                        def before_last():
                            pe.wait_ge(S["ln_hT"], 2 * KT * L + KT)
                            for job in jobs[:early]:
                                half(job, 0)

                        norm(L, before_last)
                        for job in jobs[early:]:
                            half(job, 0)
                        pe.wait_ge(S["ln_hT"], 2 * KT * (L + 1))
                        for job in jobs:
                            half(job, 1)

                    def linear(tag, w, src, m0, signal, used_by, n, rows_out=P):
                        b = take(pe, tag, used_by, n)
                        for k in range(w.shape[1]):
                            last = mm(b[0:rows_out, :], w[:, k, m0:m0 + rows_out], src[:, k, :],
                                      start=(k == 0), stop=(k == w.shape[1] - 1))
                        last.then_inc(S[signal], 1)

                    def out_proj(site, w, src, nk, before):
                        for t in range(NT):
                            b = take(pe, ("proj", site, t), "x_updated", NT * site + t + 1)
                            for k in range(nk):
                                before(t, k)
                                last = mm(b[:, 0:D], src[:, k, t * P:(t + 1) * P], w[:, k, :],
                                          start=(k == 0), stop=(k == nk - 1))
                            last.then_inc(S["proj_mm"], 1)

                    def values(a, wv, kv_src, g):
                        b = take(pe, ("v", a, g), "v_bd", 8 * a + 4 * (g + 1))
                        for i in range(2):
                            t = 2 * g + i
                            for k in range(KT):
                                last = mm(b[:, i * D:(i + 1) * D], kv_src[:, k, t * P:(t + 1) * P], wv[:, k, :],
                                          start=(k == 0), stop=(k == KT - 1))
                        last.then_inc(S["v_mm"], 1)

                    def attention(a, L, site, wq, wk, wv, kv_src, w_out):
                        def project(m, key, n):
                            w, src = (wk, kv_src) if key else (wq, hT)
                            linear(("qk", a, n), w, src, m * P, "qk_mm", "qk_T", 4 * a + n + 1)

                        own = kv_src is hT
                        if own:
                            norm_and_linears(L, [(("qk", a, n), wk if key else wq, m * P, "qk_mm", "qk_T", 4 * a + n + 1)
                                                 for n, (m, key) in enumerate(QK_OWN[:3])])
                        else:
                            project(0, True, 0)
                            project(1, True, 1)
                            norm(L, lambda: values(a, wv, kv_src, 0))
                            values(a, wv, kv_src, 1)
                            pe.wait_ge(S["ln_hT"], 2 * KT * (L + 1))
                            project(0, False, 2)
                        U = KT * NT
                        for s in range(U + LAG + 1):
                            if s < U:
                                g, t, n = s // NT, s % NT, U * a + s
                                if s == 0:
                                    pe.wait_ge(S["qk_T"], 4 * a + (2 if own else 3))
                                    pe.wait_ge(S["kbd_dve"], HG * (a + 1))
                                if s == NT:
                                    pe.wait_ge(S["qk_T"], 4 * a + 4)
                                    pe.wait_ge(S["kbd_pool"], HG * (a + 1))
                                if s == 2:
                                    project(1, False, 3)
                                    if own:
                                        for i in range(NT // 2):
                                            values(a, wv, kv_src, i)
                                b = take(pe, ("s", n), "att_scaled", n + 1)
                                for h in range(2):
                                    q0 = t * P + h * SEQ
                                    last = mm(b[h * SEQ:(h + 1) * SEQ, :], qT[:, g, q0:q0 + SEQ], kbd[:, g, :, q0:q0 + SEQ],
                                              start=True, stop=True)
                                last.then_inc(S["att_scores"], 1)
                            if LAG <= s < U + LAG:
                                n = U * a + s - LAG
                                pe.wait_ge(S["att_exp"], n + 1)
                                b = take(pe, ("tp", n), "att_PT", n + 1)
                                for h in range(4):
                                    last = nc.tensor.transpose(b[:, h * P:(h + 1) * P],
                                                               T[:, n % TR, 2 * h:2 * h + 2, :].rearrange("p h k -> p (h k)"), ident)
                                last.then_inc(S["att_tp"], 1)
                            if s >= LAG + 1:
                                u = s - LAG - 1
                                g, t, n = u // NT, u % NT, U * a + u
                                pe.wait_ge(S["att_PT"], n + 1)
                                if u == 0:
                                    pe.wait_ge(S["v_bd"], 8 * (a + 1))
                                b = take(pe, ("pv", n), "att_out", n + 1)
                                for h in range(4):
                                    o = slice(32 * h, 32 * h + 32)
                                    for half in range(2):
                                        mm(b[o, half * SEQ:(half + 1) * SEQ], vbd[:, 2 * t + half, 4 * g + h, :],
                                           PTs[:, n % 2, h, half * SEQ:(half + 1) * SEQ], start=True, stop=True,
                                           tile_position=(0, 32 * h))
                                    last = mm(b[o, P:2 * P], const("ones2"), PTs[:, n % 2, h, :], start=True, stop=True,
                                              tile_position=(0, 32 * h))
                                last.then_inc(S["att_pv"], 1)
                        if a == 0:
                            pe.wait_ge(s_wl0, 16)
                        out_proj(site, w_out, aT, KT, lambda t, k: pe.wait_ge(S["att_out"], U * a + NT * k + t + 1))

                    def mlp(m, L, site):
                        pe.wait_ge(S["mlp_in"], 16 * (m + 1))
                        norm_and_linears(L, [(("mlp", m, i), w1, i * P, "mlp_up_mm", "mlp_act", MT * m + i + 1)
                                             for i in range(4)])
                        for i in range(4, MT):
                            linear(("mlp", m, i), w1, hT, i * P, "mlp_up_mm", "mlp_act", MT * m + i + 1)
                        for t in range(NT):
                            b = take(pe, ("proj", site, t), "x_updated", NT * site + t + 1)
                            for k in range(MT):
                                if t == 0:
                                    pe.wait_ge(S["mlp_g"], MT * m + k + 1)
                                    pe.wait_ge(S["mlp_wlo"], MT * m + k + 1)
                                for i, j in ((0, 0), (0, 1), (1, 0)):
                                    last = mm(b[:, 0:D], (g_hi, g_lo)[i][:, k, t * P:(t + 1) * P], (wd_hi, wd_lo)[j][:, k, :],
                                              start=(k == 0 and i + j == 0), stop=(k == MT - 1 and i == 1))
                            last.then_inc(S["proj_mm"], 1)

                    pe.wait_ge(s_small, SMALL)
                    pe.wait_ge(s_ctx0, 16)
                    transposes()
                    pe.wait_ge(s_qkv, 16)
                    pe.wait_ge(s_once, ONCE)
                    qkv = weight("L0_qkv")
                    attention(0, 0, 0, qkv[:, :, 0:D], qkv[:, :, D:2 * D], qkv[:, :, 2 * D:3 * D], hT, weight("L0_ao"))
                    pe.wait_ge(S["ctxT_ready"], KT)
                    pe.wait_ge(s_wl0, 16)
                    kv = weight("L0_kv")
                    attention(1, 1, 1, weight("L0_q"), kv[:, :, 0:D], kv[:, :, D:2 * D], ctxT, weight("L0_co"))
                    mlp(0, 2, 2)
                    def by_halves(jobs, src, ready, signal):
                        banks = [take(pe, tag, used_by, n) for tag, _, _, _, used_by, n in jobs]
                        for half in range(2):
                            toks = slice(half * TOK // 2, (half + 1) * TOK // 2)
                            pe.wait_ge(S[ready], KT * (half + 1))
                            for b, (_, w, m0, n_out, _, _) in zip(banks, jobs):
                                for k in range(KT):
                                    last = mm(b[0:n_out, toks], w[:, k, m0:m0 + n_out], src[:, k, toks], start=(k == 0), stop=(k == KT - 1))
                                if half:
                                    last.then_inc(S[signal], 1)

                    norm(3)
                    pe.wait_ge(s_wl1, 16)
                    m1 = weight("L1_m1")
                    by_halves([("z0", m1, 0, P, "l1_z", 1), ("z1", m1, P, 32, "l1_z", 2)], xm[:, 1], "l1_xm0", "l1_z_mm")
                    pe.wait_ge(S["l1_z"], 2)

                    def l1_y(f):
                        i = FS.index(f)
                        for c in range(KT):
                            b = take(pe, ("y", i, c), "l1_y", KT * i + c + 1)
                            if f < 4:
                                w, z = weight("L1_m2a", 1)[32 * f:32 * f + 32, 0], zA[32 * f:32 * f + 32, :]
                            else:
                                w, z = weight("L1_m2b", 1)[0:32, 0], zB[0:32, :]
                            mm(b[:, :], w[:, c * P:(c + 1) * P], z, start=True, stop=True,
                               tile_position=(32 * (f % 4), 0)).then_inc(S["l1_y_mm"], 1)

                    def l1_use(i):
                        f, x = FS[i], xm[:, i % 2]
                        pe.wait_ge(S["l1_xm"], KT * (i + 1))
                        if f == 1:
                            linear("td", weight("L1_td1"), x, 0, "l1_td_mm", "l1_td", 1, rows_out=64)
                        else:
                            for c in range(KT):
                                n = KT * (i - 1) + c
                                linear(("rkvg", n), l1w[:, {3: 0, 0: 1, 2: 2, 4: 3}[f]], x, c * P, "l1_rkvg_mm", "l1_rkvg", n + 1)

                    l1_y(FS[0])
                    for i in range(5):
                        if i < 4:
                            l1_y(FS[i + 1])
                        l1_use(i)
                        if i == 1:
                            pe.wait_ge(S["l1_td"], 1)
                            for c in range(KT):
                                b = take(pe, ("dec", c), "l1_dec", 2 * c + 1)
                                mm(b[:, :], weight("L1_td2", 1)[0:64, 0, c * P:(c + 1) * P], tw[0:64, :],
                                   start=True, stop=True).then_inc(S["l1_dec_mm"], 1)
                    for c in range(KT):
                        pe.wait_ge(S["l1_rku"], c + 1)
                        b = take(pe, ("rku", c), "l1_uv", c + 1)
                        mm(b[:, :], const("block8"), rku[:, c, :], start=True, stop=True).then_inc(S["l1_rku_mm"], 1)

                    def l1_sum(n):
                        c, j = n // S8, n % S8
                        pe.wait_ge(S["l1_rs"], n + 1)
                        for t in range(NT):
                            last = mm(bank[6 + c][:, t * P + j:(t + 1) * P:S8], rsZ[:, n % 3, t * P:(t + 1) * P],
                                      const("heads8"), start=False, stop=(j == S8 - 1 and t == NT - 1), skip_group_check=True)
                        last.then_inc(S["l1_rs_used"], 1)

                    for n in range(KT * S8 + SUMLAG):
                        if n < KT * S8:
                            c, j = n // S8, n % S8
                            if n == 0:
                                pe.wait_ge(S["l1_rkvg"], 2 * KT)
                            b = take(pe, ("vb", n), "l1_kv", n + 1)
                            mm(b[:, :], sel[:, j, :], vT[:, c, :], start=True, stop=True).then_inc(S["l1_vb"], 1)
                        if n == 2:
                            pe.wait_ge(S["l1_uv"], KT)
                            for c in range(KT):
                                for t in range(NT):
                                    mm(bank[6 + c][:, t * P:(t + 1) * P], rku[:, c, t * P:(t + 1) * P], ident,
                                       start=(t == 0), stop=False, skip_group_check=True)
                        if n >= SUMLAG:
                            l1_sum(n - SUMLAG)
                    for c in range(KT):
                        pe.wait_ge(S["l1_gn"], c + 1)
                        b = take(pe, ("gn", c), "l1_gn_T", c + 1)
                        for t in range(NT):
                            last = nc.tensor.transpose(b[:, t * P:(t + 1) * P], gn[:, c, t * P:(t + 1) * P], ident)
                        last.then_inc(S["l1_gn_tp"], 1)
                    pe.wait_ge(S["l1_gated"], KT)
                    out_proj(3, l1w[:, 4], aT, KT, lambda t, k: None)
                    norm(4)
                    by_halves([(("ffk", c), l1w[:, 5], c * P, P, "l1_relu", c + 1) for c in range(KT)], xm[:, 0], "l1_x2", "l1_ffk_mm")
                    pe.wait_ge(S["l1_x2"], 3 * KT)
                    for t in range(NT):
                        b = take(pe, ("rr", t), "l1_rr", t + 1)
                        for k in range(KT):
                            last = mm(b[:, 0:D], xm[:, 1, k, t * P:(t + 1) * P], l1w[:, 6, k, :], start=(k == 0), stop=(k == KT - 1))
                        last.then_inc(S["l1_rr_mm"], 1)
                    pe.wait_ge(S["l1_kk"], KT)
                    out_proj(4, l1w[:, 7], aT, KT, lambda t, k: None)

                    def cross2(z, L, site):
                        def head_w(n):
                            return w2ring[:, n % 3, :].rearrange("p (w k d) -> p w k d", w=3, k=KT)

                        def parts(n, w):
                            return [x[:, n % 2, :].rearrange("p (w k d) -> p w k d", w=2, k=KT)[:, w] for x in (w2_hi, w2_lo)]

                        def split_mm(b, w, src, toks):
                            pairs = [(i, j, k) for i, j in ((0, 0), (0, 1), (1, 0)) for k in range(KT)]
                            for i, j, k in pairs:
                                last = mm(b[:, toks], w[i][:, k, :], src[j][:, k, toks],
                                          start=(i, j, k) == pairs[0], stop=(i, j, k) == pairs[-1])
                            return last

                        def query(h):
                            n = H2 * z + h
                            pe.wait_ge(S["l2_wlo"], n + 1)
                            b = take(pe, ("q2", n), "l2_q", n + 1)
                            split_mm(b, parts(n, 0), (hT_hi, hT_lo), slice(0, TOK)).then_inc(S["l2_q_mm"], 1)

                        def keys_values(h):
                            n = H2 * z + h
                            w = head_w(n)
                            pe.wait_ge(S[f"w2_in{n % 3}"], 32 * (n // 3 + 1))
                            pe.wait_ge(S["l2_wlo"], n + 1)
                            if n == 0:
                                pe.wait_ge(S["ctx_lo"], KT)
                            b = take(pe, ("k2", n), "l2_k", n + 1)
                            split_mm(b, parts(n, 1), (ctx_hi, ctx_lo), slice(0, TOK)).then_inc(S["l2_k_mm"], 1)
                            b = take(pe, ("v2", n), "l2_v", n + 1)
                            for t in range(NT):
                                for k in range(KT):
                                    last = mm(b[:, t * P:(t + 1) * P], ctxT[:, k, t * P:(t + 1) * P], w[:, 2, k, :],
                                              start=(k == 0), stop=(k == KT - 1))
                            last.then_inc(S["l2_v_mm"], 1)

                        def scores(h):
                            n = H2 * z + h
                            pe.wait_ge(S["l2_q"], n + 1)
                            pe.wait_ge(S["l2_k"], n + 1)
                            pe.wait_ge(S["l2_kb"], n + 1)
                            b = take(pe, ("s2", n), "l2_sub", n + 1)
                            for t in range(NT):
                                for half in range(2):
                                    q0 = t * P + half * SEQ
                                    last = mm(b[half * SEQ:(half + 1) * SEQ, t * KX:(t + 1) * KX], q2[:, n % 2, q0:q0 + SEQ],
                                              k2[:, n % 2, 2 * t + half, :], start=True, stop=True)
                            last.then_inc(S["l2_scores"], 1)

                        def turn(h):
                            n = H2 * z + h
                            pe.wait_ge(S["l2_prob_a"], n + 1)
                            pe.wait_ge(S["l2_prob_b"], n + 1)
                            b = take(pe, ("tp2", n), "l2_PT", n + 1)
                            for t in range(NT):
                                last = nc.tensor.transpose(b[:, t * P:(t + 1) * P], pbd[:, n % 2, t, :], ident)
                            last.then_inc(S["l2_tp"], 1)

                        def weigh(h):
                            n = H2 * z + h
                            pe.wait_ge(S["l2_PT"], n + 1)
                            pe.wait_ge(S["l2_v"], n + 1)
                            b = take(pe, ("pv2", n), "l2_c", n + 1)
                            for t in range(NT):
                                last = mm(b[:, t * P:(t + 1) * P], v2[:, n % 2, t, :], PT2[:, n % 2, t, :], start=True, stop=True)
                            last.then_inc(S["l2_pv"], 1)

                        def project(heads, banks):
                            for h in heads:
                                n = H2 * z + h
                                for g in banks:
                                    pe.wait_ge(S["l2_wolo"], n + 1)
                                    pe.wait_ge(S["l2_c"], n + 1)
                                    if h == 0:
                                        pe.wait_ge(S["x_updated"], NT * site)
                                    for t in (2 * g, 2 * g + 1):
                                        for i, j in ((0, 0), (0, 1), (1, 0)):
                                            last = mm(bank[6 + g][:, t % 2 * D:(t % 2 + 1) * D],
                                                      (c_hi, c_lo)[i][:, h % CR, t * P:(t + 1) * P], (wo_hi, wo_lo)[j][:, n % 2, :],
                                                      start=(h == 0 and t % 2 == 0 and i + j == 0),
                                                      stop=(h == H2 - 1 and t % 2 == 1 and i == 1), skip_group_check=True)
                                    if h == H2 - 1:
                                        last.then_inc(S["proj_mm"], 2)
                                    elif g == 1:
                                        last.then_inc(S["l2_c_used"], 1)

                        keys_values(0)
                        norm(L)
                        q = [take(pe, ("q2", H2 * z + h), "l2_q", H2 * z + h + 1) for h in range(2)]
                        for half in range(2):
                            pe.wait_ge(S["l2_hlo"], 2 * KT * z + KT * (half + 1))
                            for h in range(2):
                                pe.wait_ge(S["l2_wlo"], H2 * z + h + 1)
                                last = split_mm(q[h], parts(H2 * z + h, 0), (hT_hi, hT_lo), slice(half * TOK // 2, (half + 1) * TOK // 2))
                                if half:
                                    last.then_inc(S["l2_q_mm"], 1)
                        for h in range(H2 - 1):
                            scores(h)
                            if h >= 1:
                                query(h + 1)
                            keys_values(h + 1)
                            if h >= 1:
                                weigh(h - 1)
                            if 2 <= h < H2 - 2:
                                project([h - 2], range(2))
                            turn(h)
                        scores(H2 - 1)
                        weigh(H2 - 2)
                        project([H2 - 4], range(2))
                        project([H2 - 3], [0])
                        turn(H2 - 1)
                        project([H2 - 3], [1])
                        project([H2 - 2], [0])
                        weigh(H2 - 1)
                        project([H2 - 2], [1])
                        project([H2 - 1], range(2))

                    cross2(0, 5, 5)
                    cross2(1, 6, 6)
                    mlp(1, 7, 7)
                    pe.wait_ge(s_wl3, 16)
                    w3 = weight("L3_qkv", 1)[:, 0, :].rearrange("p (w k n) -> p w k n", w=3, k=KT)
                    attention(2, 8, 8, w3[:, 0], w3[:, 1], w3[:, 2], ctxT, weight("L3_c"))
                    mlp(2, 9, 9)

                @block.scalar
                def _(act):
                    A = nc.scalar.activation

                    def norm(L, s, b):
                        for half in range(2):
                            h = slice(half * TOK // 2, (half + 1) * TOK // 2)
                            for k in range(KT):
                                act.wait_ge(S["ln_tp"], 2 * KT * L + KT * (half + 1))
                                A(hT[:, k, h], held(("ln", L, half))[:, k * TOK // 2:(k + 1) * TOK // 2],
                                  ACT.Identity, bias=col(b, k), scale=col(s, k)).then_inc(S["ln_hT"], 1)

                    def attention(a, L, bq, bk, ln_s, ln_b):
                        own = a == 0
                        for n, (m, key) in enumerate(QK_OWN if own else QK_ENC):
                            if n == (0 if own else KT):
                                norm(L, ln_s, ln_b)
                            act.wait_ge(S["qk_mm"], 4 * a + n + 1)
                            out, b = (kT, bk) if key else (qT, bq)
                            A(out[:, m, :], held(("qk", a, n))[:, :], ACT.Identity, bias=col(b, m)).then_inc(S["qk_T"], 1)
                        U = KT * NT
                        for s in range(1, U + LAG):
                            if s >= LAG:
                                n = U * a + s - LAG
                                act.wait_ge(S["att_tp"], n + 1)
                                if s - LAG >= 2:
                                    act.wait_ge(S["att_pv"], n - 1)
                                A(PTs[:, n % 2].rearrange("p h q -> p (h q)"), held(("tp", n))[:, :], ACT.Copy).then_inc(S["att_PT"], 1)
                            if s - 1 < U:
                                n = U * a + s - 1
                                act.wait_ge(S["att_sub"], n + 1)
                                A(T[:, n % TR], T[:, n % TR], ACT.Exp).then_inc(S["att_exp"], 1)

                    def mlp(m, site, bias, func):
                        act.wait_ge(S["mlp_in"], 16 * (m + 1))
                        act.wait_ge(S["x_updated"], NT * site)
                        for i in range(MT):
                            A(wd_hi[:, i, :], w2[:, i, :], ACT.Copy).then_inc(S["mlp_whi"], 1)
                            act.wait_ge(S["mlp_up_mm"], MT * m + i + 1)
                            if i >= 2:
                                act.wait_ge(S["mlp_g"], MT * m + i - 1)
                            A(g_full[:, i % 2, :], held(("mlp", m, i))[:, :], func, bias=col(bias, i)).then_inc(S["mlp_act"], 1)

                    act.wait_ge(s_small, SMALL)
                    for k in range(KT):
                        act.wait_ge(S["ctx_tp"], k + 1)
                        A(ctxT[:, k, :], held(("ctx", k))[:, :], ACT.Copy).then_inc(S["ctxT_ready"], 1)
                    attention(0, 0, "L0_bq_s", "L0_bk_s", "L0_ln1_s", "L0_ln1_b")
                    attention(1, 1, "L0_b_q", "L0_bk_c", "L0_ln2_s", "L0_ln2_b")
                    norm(2, "L0_ln3_s", "L0_ln3_b")
                    mlp(0, 2, "L0_b1", ACT.Gelu_apprx_tanh)
                    norm(3, "L1_ln1_w", "L1_ln1_b")
                    for i, z in enumerate((zA, zB)):
                        act.wait_ge(S["l1_z_mm"], i + 1)
                        r = P if i == 0 else 32
                        A(z[0:r, :], held(f"z{i}")[0:r, :], ACT.Tanh).then_inc(S["l1_z"], 1)
                    act.wait_ge(S["l1_td_mm"], 1)
                    A(tw[0:64, :], held("td")[0:64, :], ACT.Tanh).then_inc(S["l1_td"], 1)

                    def rkvg(i, out, func):
                        for c in range(KT):
                            n = KT * (i - 1) + c
                            act.wait_ge(S["l1_rkvg_mm"], n + 1)
                            A(out[:, c, :], held(("rkvg", n))[:, :], func).then_inc(S["l1_rkvg"], 1)

                    rkvg(1, kT, ACT.Copy)
                    for c in range(KT):
                        act.wait_ge(S["l1_dec_mm"], c + 1)
                        A(dtmp[:, c, :], held(("dec", c))[:, :], ACT.Exp, bias=col("L1_time_decay", c)).then_inc(S["l1_dec"], 1)
                        act.wait_ge(S["l1_dec"], 2 * c + 1)
                        A(wdec[:, c, :].rearrange("p (b s) -> p b s", s=SLOT)[:, :, 1:SLOT],
                          dtmp[:, c, :].rearrange("p (b s) -> p b s", s=SEQ), ACT.Exp, scale=-1.0).then_inc(S["l1_dec"], 1)
                    rkvg(2, vT, ACT.Copy)
                    rkvg(3, qT, ACT.Copy)
                    rkvg(4, gateT, ACT.Silu)
                    act.wait_ge(s_chunk0, CHUNK0)
                    for k in range(KT):
                        A(ctx_hi[:, k, :], ctxT[:, k, :], ACT.Copy).then_inc(S["ctx_hi"], 1)

                    def weights_hi(n):
                        act.wait_ge(S[f"w2_in{n % 3}"], 32 * (n // 3 + 1))
                        if n < 2:
                            act.wait_ge(S["l1_rs"], KT * S8)
                        else:
                            act.wait_ge(S["l2_q_mm"], n - 1)
                            act.wait_ge(S["l2_k_mm"], n - 1)
                        A(w2_hi[:, n % 2, :], w2ring[:, n % 3, 0:2 * KT * P], ACT.Copy).then_inc(S["l2_whi"], 1)

                    def gn_roots(c):
                        act.wait_ge(S["l1_cent"], c + 1)
                        A(gnsq, gn[:, c, :], ACT.Square).then_inc(S["l1_sq"], 1)
                        act.wait_ge(S["l1_var"], c + 1)
                        A(gn_sd, gn_var, ACT.Sqrt).then_inc(S["l1_sd"], 1)

                    for n in range(KT * S8):
                        if n >= 3:
                            act.wait_ge(S["l1_state"], n - 2)
                        A(kvA[:, n % 3, :].rearrange("p (b s) -> p b s", s=SLOT)[:, :, 0], s0[:, n // S8, :, n % S8], ACT.Copy)\
                            .then_inc(S["l1_slot"], 1)
                    gn_roots(0)
                    gn_roots(1)
                    weights_hi(0)
                    weights_hi(1)
                    for c in range(KT):
                        act.wait_ge(S["l1_gn_tp"], c + 1)
                        A(dtmp[:, c, :], held(("gn", c))[:, :], ACT.Identity, bias=col("L1_gn_b", c), scale=col("L1_gn_w", c)).then_inc(S["l1_gn_T"], 1)
                    norm(4, "L1_ln2_w", "L1_ln2_b")
                    for c in range(KT):
                        act.wait_ge(S["l1_ffk_mm"], c + 1)
                        A(dtmp[:, c, :], held(("ffk", c))[:, :], ACT.Relu).then_inc(S["l1_relu"], 1)
                    for t in range(NT):
                        act.wait_ge(S["l1_rr_mm"], t + 1)
                        A(gateT[:, t // 2, (t % 2) * D:(t % 2 + 1) * D], held(("rr", t))[:, 0:D], ACT.Sigmoid).then_inc(S["l1_rr"], 1)

                    def cross2(z, L, bq, bk, biv, ln_s, ln_b):
                        def context_hi(h):
                            n = H2 * z + h
                            act.wait_ge(S["l2_pv"], n + 1)
                            if h >= CR:
                                act.wait_ge(S["l2_c_used"], (H2 - 1) * z + h - CR + 1)
                            elif z:
                                act.wait_ge(S["proj_mm"], 6 * NT)
                            A(c_hi[:, h % CR, :], held(("pv2", n))[:, :], ACT.Identity, bias=col(biv, h)).then_inc(S["l2_chi"], 1)

                        def out_weights_hi(h):
                            n = H2 * z + h
                            act.wait_ge(S[f"wo_in{n % WR}"], 16 * (n // WR + 1))
                            if h >= 2:
                                act.wait_ge(S["l2_c_used"], (H2 - 1) * z + h - 1)
                            elif z:
                                act.wait_ge(S["proj_mm"], 6 * NT)
                            A(wo_hi[:, n % 2, :], wo_ring[:, n % WR, :], ACT.Copy).then_inc(S["l2_wohi"], 1)

                        def query(h):
                            n = H2 * z + h
                            act.wait_ge(S["l2_q_mm"], n + 1)
                            if n >= 2:
                                act.wait_ge(S["l2_scores"], n - 1)
                            A(q2[:, n % 2, :], held(("q2", n))[:, :], ACT.Identity, bias=col(bq, h)).then_inc(S["l2_q"], 1)

                        def keys(h):
                            n = H2 * z + h
                            act.wait_ge(S["l2_k_mm"], n + 1)
                            if n == 0:
                                act.wait_ge(S["x_updated"], 5 * NT)
                            if n >= 2:
                                act.wait_ge(S["l2_scores"], n - 1)
                            A(k2[:, n % 2, :, 0:SEQ], held(("k2", n))[:, :].rearrange("p (b k) -> p b k", b=NB), ACT.Identity,
                              bias=col(bk, h)).then_inc(S["l2_k"], 1)

                        keys(0)
                        norm(L, ln_s, ln_b)
                        query(0)
                        query(1)
                        for h in range(H2):
                            n = H2 * z + h
                            if n + 2 < 2 * H2:
                                weights_hi(n + 2)
                            act.wait_ge(S["l2_sub"], n + 1)
                            A(E2[:, n % 2], E2[:, n % 2], ACT.Exp, scale=float(P) ** -0.5).then_inc(S["l2_exp"], 1)
                            if h + 1 < H2:
                                if h >= 1:
                                    query(h + 1)
                                keys(h + 1)
                            if h >= 1:
                                context_hi(h - 1)
                                out_weights_hi(h - 1)
                            act.wait_ge(S["l2_tp"], n + 1)
                            if n >= 2:
                                act.wait_ge(S["l2_pv"], n - 1)
                            A(PT2[:, n % 2].rearrange("p t q -> p (t q)"), held(("tp2", n))[:, :], ACT.Copy).then_inc(S["l2_PT"], 1)
                        out_weights_hi(H2 - 1)
                        context_hi(H2 - 1)

                    cross2(0, 5, "L2_bq1", "L2_bk1", "L2_biv1", "L2_ln1_s", "L2_ln1_b")
                    cross2(1, 6, "L2_bq2", "L2_bk2", "L2_biv2", "L2_ln2_s", "L2_ln2_b")
                    norm(7, "L2_lnm_s", "L2_lnm_b")
                    mlp(1, 7, "L2_bf1", ACT.Gelu)
                    attention(2, 8, "L3_q_b", "L3_k_b", "L3_ln1_w", "L3_ln1_b")
                    norm(9, "L3_ln2_w", "L3_ln2_b")
                    mlp(2, 9, "L3_fcb", ACT.Gelu_apprx_tanh)

                @block.vector
                def _(dve):
                    V = nc.vector
                    steps = [0]

                    def settle(ins):
                        steps[0] += 1
                        ins.then_inc(S["dve_step"], 1)
                        dve.wait_ge(S["dve_step"], steps[0])

                    def renew(site, biased, L, gate=False):
                        src = x_first if site is None else X
                        for s in range(NT + 2):
                            if s < NT and site is not None:
                                t = s
                                dve.wait_ge(S["proj_mm"], NT * site + t + 1)
                                y = bank[6 + t // 2][:, t % 2 * D:(t % 2 + 1) * D] if site in (5, 6) else held(("proj", site, t))[:, 0:D]
                                if gate:
                                    dve.wait_ge(S["l1_rr"], t + 1)
                                    tmp = rsZ[:, t // 2, (t % 2) * D:(t % 2 + 1) * D]
                                    settle(V.tensor_tensor(tmp, y, gateT[:, t // 2, (t % 2) * D:(t % 2 + 1) * D], ALU.mult))
                                    y = tmp
                                if biased is not None:
                                    dve.wait_ge(S["x_biased"], biased + 1)
                                V.tensor_tensor(X[:, t, :], X[:, t, :], y, ALU.add).then_inc(S["x_updated"], 1)
                            if 1 <= s <= NT and L is not None:
                                t = s - 1
                                if site is not None:
                                    dve.wait_ge(S["x_updated"], NT * site + t + 1)
                                settle(V.bn_stats(bst[:, t, :], src[:, t, :]))
                                V.bn_aggr(mv[:, t, :], bst[:, t, :]).then_inc(S["ln_mv"], 1)
                            if s >= 2 and L is not None:
                                t = s - 2
                                dve.wait_ge(S["ln_mv"], NT * L + t + 1)
                                dve.wait_ge(S["ln_rstd"], NT * L + t + 1)
                                V.tensor_scalar(xn[:, t, :], src[:, t, :], mv[:, t, 0:1], rstd[:, t:t + 1], ALU.subtract, ALU.mult)\
                                    .then_inc(S["ln_xn"], 1)

                    def mlp(m):
                        for i in range(MT):
                            n = MT * m + i
                            dve.wait_ge(S["mlp_act"], n + 1)
                            V.tensor_copy(g_hi[:, i, :], g_full[:, i % 2, :]).then_inc(S["mlp_ghi"], 1)
                            dve.wait_ge(S["mlp_ghi"], n + 1)
                            V.tensor_tensor(g_lo[:, i, :], g_full[:, i % 2, :], g_hi[:, i, :].bitcast(f32), ALU.subtract)\
                                .then_inc(S["mlp_g"], 1)

                    def attention(a, bv, mult):
                        dve.wait_ge(S["qk_T"], 4 * a + 1)
                        for h in range(HG):
                            V.tensor_scalar(kbd[:, 0, h, :], kT[:, 0, :], hmask[:, h:h + 1], None, ALU.mult).then_inc(S["kbd_dve"], 1)
                        def values():
                            for g in range(NT // 2):
                                dve.wait_ge(S["v_mm"], 2 * a + g + 1)
                                for half in range(2):
                                    for par in range(2):
                                        src = held(("v", a, g))[half * SEQ:(half + 1) * SEQ, :].rearrange(
                                            "p (t h r d) -> p t h r d", t=2, h=8, r=2)[:, :, :, par, :]
                                        brow = row(bv)[half * SEQ:(half + 1) * SEQ, :].rearrange(
                                            "p (h r d) -> p h r d", h=8, r=2)[:, :, par, :].unsqueeze(1).to_broadcast([SEQ, 2, 8, 16])
                                        dst = vbd[par * SEQ:(par + 1) * SEQ, 4 * g + half:4 * g + half + 3:2, :, par * 16:(par + 1) * 16]
                                        V.tensor_tensor(dst, src, brow, ALU.add).then_inc(S["v_bd"], 1)

                        if a > 0:
                            values()
                        U = KT * NT
                        for s in range(U + LAG + 1):
                            if s < U:
                                n, t = U * a + s, s % NT
                                dve.wait_ge(S["att_scores"], n + 1)
                                if n >= TR:
                                    dve.wait_ge(S["att_tp"], n - TR + 1)
                                if s == 0:
                                    dve.wait_ge(S["masks_ready"], 3)
                                m = mult(t).unsqueeze(1).to_broadcast([P, HG, SEQ])
                                V.scalar_tensor_tensor(T[:, n % TR], held(("s", n))[:, :].rearrange("p (h k) -> p h k", h=HG),
                                                       (D // H0) ** -0.5, m, ALU.mult, ALU.mult).then_inc(S["att_scaled"], 1)
                            if 1 <= s <= U:
                                n = U * a + s - 1
                                dve.wait_ge(S["att_masked"], n + 1)
                                V.tensor_reduce(nmax[:, n % TR, :], T[:, n % TR], AX, ALU.max, negate=True).then_inc(S["att_max"], 1)
                            if s == 2 and a == 0:
                                values()
                            if s >= LAG + 1:
                                u = s - LAG - 1
                                n, g, t = U * a + u, u // NT, u % NT
                                dve.wait_ge(S["att_pv"], n + 1)
                                b = held(("pv", n))
                                settle(V.reciprocal(rden[:, n % 2, :], b[:, P:2 * P]))
                                V.tensor_tensor(aT[:, g, t * P:(t + 1) * P], b[:, 0:P], rden[:, n % 2, :], ALU.mult).then_inc(S["att_out"], 1)

                    dve.wait_ge(s_small, SMALL)
                    dve.wait_ge(s_once, ONCE)
                    dve.wait_ge(s_chunk0, CHUNK0)
                    renew(None, None, 0)
                    attention(0, "L0_bv_s", lambda t: m_self)
                    renew(0, 0, 1)
                    attention(1, "L0_bv_c", lambda t: m_cross[:, t, :])
                    renew(1, 1, 2)
                    mlp(0)
                    renew(2, 2, 3)
                    def shift(L, state_row, half):
                        toks, seqs = slice(half * TOK // 2, (half + 1) * TOK // 2), slice(half * NB // 2, (half + 1) * NB // 2)
                        dve.wait_ge(S["ln_hT"], 2 * KT * L + KT * half + 1)
                        h = hT[:, 0, toks].rearrange("p (b s) -> p b s", s=SEQ)
                        o = sxT[:, 0, toks].rearrange("p (b s) -> p b s", s=SEQ)
                        st = ctxT[:, 0, :].rearrange("p (b s) -> p b s", s=SEQ)[:, seqs, state_row:state_row + 1]
                        V.tensor_tensor(o[:, :, 1:SEQ], h[:, :, 0:SEQ - 1], h[:, :, 1:SEQ], ALU.subtract)
                        settle(V.tensor_tensor(o[:, :, 0:1], st, h[:, :, 0:1], ALU.subtract))

                    dve.wait_ge(S["ctxT_ready"], KT)
                    for half in range(2):
                        shift(3, 1, half)
                        toks = slice(half * TOK // 2, (half + 1) * TOK // 2)
                        for c in range(KT):
                            if c:
                                dve.wait_ge(S["l1_sx"], 2 * (half + 1))
                            dve.wait_ge(S["ln_hT"], 2 * KT * 3 + KT * half + c + 1)
                            V.scalar_tensor_tensor(xm[:, 1, c, toks], sxT[:, c, toks], col("L1_maa_x", c), hT[:, c, toks], ALU.mult, ALU.add)\
                                .then_inc(S["l1_xm0"], 1)
                    for i, f in enumerate(FS):
                        for c in range(KT):
                            dve.wait_ge(S["l1_y_mm"], KT * i + c + 1)
                            if i == 1:
                                dve.wait_ge(S["l1_z_mm"], 2)
                            if i == 2:
                                dve.wait_ge(S["l1_td_mm"], 1)
                            if i > 2:
                                dve.wait_ge(S["l1_rkvg_mm"], KT * (i - 2))
                            V.scalar_tensor_tensor(xm[:, i % 2, c, :], held(("y", i, c))[:, :], col(f"L1_st{f}", c), sxT[:, c, :],
                                                   ALU.add, ALU.mult).then_inc(S["l1_y"], 1)
                    dve.wait_ge(S["l1_rkvg"], 3 * KT)
                    for c in range(KT):
                        V.scalar_tensor_tensor(rku[:, c, :], kT[:, c, :], col("L1_u", c), qT[:, c, :], ALU.mult, ALU.mult)\
                            .then_inc(S["l1_rku"], 1)
                    for c in range(KT):
                        dve.wait_ge(S["l1_rku_mm"], c + 1)
                        V.tensor_tensor(rku[:, c, :], held(("rku", c))[:, :], vT[:, c, :], ALU.mult).then_inc(S["l1_uv"], 1)
                    def group_norm(c):
                        og = bank[6 + c][:, :].rearrange("p (h j) -> p h j", j=S8)
                        xg = gn[:, c, :].rearrange("p (h j) -> p h j", j=S8)
                        dve.wait_ge(S["l1_rs_used"], S8 * (c + 1))
                        settle(V.tensor_reduce(small[:, 0:64], og, AX, ALU.add))
                        V.scalar_tensor_tensor(xg, small[:, 0:64].unsqueeze(2).to_broadcast([P, 64, S8]), -1.0 / S8,
                                               og, ALU.mult, ALU.add).then_inc(S["l1_cent"], 1)
                        dve.wait_ge(S["l1_sq"], c + 1)
                        settle(V.tensor_reduce(gn_var, gnsq.rearrange("p (h j) -> p h j", j=S8), AX, ALU.add))
                        V.tensor_scalar(gn_var, gn_var, 1.0 / S8, EPS, ALU.mult, ALU.add).then_inc(S["l1_var"], 1)
                        dve.wait_ge(S["l1_sd"], c + 1)
                        settle(V.reciprocal(gn_r, gn_sd))
                        settle(V.tensor_tensor(gn_sd, gn_r, gn_r, ALU.mult))
                        settle(V.tensor_tensor(gn_sd, gn_sd, gn_var, ALU.mult))
                        settle(V.tensor_scalar(gn_sd, gn_sd, -0.5, 1.5, ALU.mult, ALU.add))
                        settle(V.tensor_tensor(gn_r, gn_r, gn_sd, ALU.mult))
                        V.tensor_tensor(xg, xg, gn_r.unsqueeze(2).to_broadcast([P, 64, S8]), ALU.mult).then_inc(S["l1_gn"], 1)

                    for n in range(KT * S8 + 1):
                        if n < KT * S8:
                            c = n // S8
                            dve.wait_ge(S["l1_vb"], n + 1)
                            if n >= 3:
                                dve.wait_ge(S["l1_state"], n - 2)
                            V.tensor_tensor(kvA[:, n % 3, :].rearrange("p (b s) -> p b s", s=SLOT)[:, :, 1:SLOT],
                                            held(("vb", n))[:, :].rearrange("p (b s) -> p b s", s=SEQ),
                                            kT[:, c, :].rearrange("p (b s) -> p b s", s=SEQ), ALU.mult).then_inc(S["l1_kv"], 1)
                        if n >= 1:
                            m = n - 1
                            dve.wait_ge(S["l1_slot"], m + 1)
                            dve.wait_ge(S["l1_kv"], m + 1)
                            dve.wait_ge(S["l1_dec"], 4)
                            dve.wait_ge(S["slots_zero"], 1)
                            if m >= 3:
                                dve.wait_ge(S["l1_rs"], m - 2)
                            V.tensor_tensor_scan(stS[:, m % 3, :], wdec[:, m // S8, :], kvA[:, m % 3, :], 0.0, ALU.mult, ALU.add)\
                                .then_inc(S["l1_state"], 1)
                    group_norm(0)
                    group_norm(1)
                    for c in range(KT):
                        dve.wait_ge(S["l1_gn_T"], c + 1)
                        dve.wait_ge(S["l1_rkvg"], 4 * KT)
                        V.tensor_tensor(aT[:, c, :], dtmp[:, c, :], gateT[:, c, :], ALU.mult).then_inc(S["l1_gated"], 1)
                    renew(3, None, 4)
                    for k, name, half in ((0, "L1_fmk", 0), (0, "L1_fmk", 1), (1, "L1_fmr", None)):
                        if half is None:
                            toks = slice(0, TOK)
                        else:
                            toks = slice(half * TOK // 2, (half + 1) * TOK // 2)
                            shift(4, 0, half)
                        for c in range(KT):
                            if c and half is not None:
                                dve.wait_ge(S["l1_sx2"], 2 * (half + 1))
                                dve.wait_ge(S["ln_hT"], 2 * KT * 4 + KT * half + c + 1)
                            V.scalar_tensor_tensor(xm[:, k, c, toks], sxT[:, c, toks], col(name, c), hT[:, c, toks], ALU.mult, ALU.add)\
                                .then_inc(S["l1_x2"], 1)
                    for c in range(KT):
                        dve.wait_ge(S["l1_relu"], c + 1)
                        V.tensor_tensor(aT[:, c, :], dtmp[:, c, :], dtmp[:, c, :], ALU.mult).then_inc(S["l1_kk"], 1)
                    renew(4, None, 5, gate=True)

                    def cross2(z, biv):
                        def value(h):
                            n = H2 * z + h
                            dve.wait_ge(S["l2_v_mm"], n + 1)
                            dve.wait_ge(S["l2_dbv"], n + 1)
                            if n >= 2:
                                dve.wait_ge(S["l2_pv"], n - 1)
                            V.tensor_tensor(v2[:, n % 2], held(("v2", n))[:, :].rearrange("p (t d) -> p t d", t=NT),
                                            dbv[:, n % 2, :].unsqueeze(1).to_broadcast([P, NT, P]), ALU.add).then_inc(S["l2_v"], 1)

                        def context(h):
                            n = H2 * z + h
                            dve.wait_ge(S["l2_chi"], n + 1)
                            V.scalar_tensor_tensor(c_lo[:, h % CR, :], held(("pv2", n))[:, :], col(biv, h), c_hi[:, h % CR, :].bitcast(f32),
                                                   ALU.add, ALU.subtract).then_inc(S["l2_c"], 1)

                        for i in range(2 * KT):
                            h = slice((i // KT) * TOK // 2, (i // KT + 1) * TOK // 2)
                            dve.wait_ge(S["ln_hT"], 2 * KT * (5 + z) + i + 1)
                            V.tensor_copy(hT_hi[:, i % KT, h], hT[:, i % KT, h]).then_inc(S["l2_hhi"], 1)
                            dve.wait_ge(S["l2_hhi"], 2 * KT * z + i + 1)
                            V.tensor_tensor(hT_lo[:, i % KT, h], hT[:, i % KT, h], hT_hi[:, i % KT, h].bitcast(f32), ALU.subtract)\
                                .then_inc(S["l2_hlo"], 1)
                        value(0)
                        for h in range(H2):
                            n = H2 * z + h
                            dve.wait_ge(S["l2_scores"], n + 1)
                            s = held(("s2", n))[:, 0:NT * KX].rearrange("p (t k) -> p t k", t=NT)
                            V.tensor_reduce(nmax[:, n % 2, 0:NT], s, AX, ALU.max, negate=True).then_inc(S["l2_max"], 1)
                            dve.wait_ge(S["l2_max"], n + 1)
                            if n >= 2:
                                dve.wait_ge(S["l2_prob_a"], n - 1)
                                dve.wait_ge(S["l2_prob_b"], n - 1)
                            V.tensor_tensor(E2[:, n % 2], s, nmax[:, n % 2, 0:NT].unsqueeze(2).to_broadcast([P, NT, KX]), ALU.add)\
                                .then_inc(S["l2_sub"], 1)
                            dve.wait_ge(S["l2_exp"], n + 1)
                            den = small[:, 8 * (n % 2):8 * (n % 2) + 4]
                            rec = small[:, 8 * (n % 2) + 4:8 * (n % 2) + 8]
                            settle(V.tensor_reduce(den, E2[:, n % 2], AX, ALU.add))
                            V.reciprocal(rec, den).then_inc(S["l2_rden"], 1)
                            dve.wait_ge(S["l2_rden"], n + 1)
                            if n >= 2:
                                dve.wait_ge(S["l2_tp"], n - 1)
                            V.tensor_tensor(pbd[0:SEQ, n % 2, :, 0:SEQ], E2[0:SEQ, n % 2, :, 0:SEQ],
                                            rec[0:SEQ, :].unsqueeze(2).to_broadcast([SEQ, NT, SEQ]), ALU.mult).then_inc(S["l2_prob_a"], 1)
                            if h + 1 < H2:
                                value(h + 1)
                            if h >= 1:
                                context(h - 1)
                        context(H2 - 1)

                    cross2(0, "L2_biv1")
                    renew(5, 3, 6)
                    cross2(1, "L2_biv2")
                    renew(6, 4, 7)
                    mlp(1)
                    renew(7, 5, 8)
                    attention(2, "L3_v_b", lambda t: m_key[:, t, :])
                    renew(8, 6, 9)
                    mlp(2)
                    renew(9, 7, None)

                @block.gpsimd
                def _(pool):
                    G = nc.gpsimd
                    steps = [0]

                    def settle(ins):
                        steps[0] += 1
                        ins.then_inc(S["pool_step"], 1)
                        pool.wait_ge(S["pool_step"], steps[0])

                    def power(out, var, n, signal):
                        settle(G.tensor_scalar(out, var, 1.0, EPS, ALU.mult, ALU.add))
                        G.tensor_tensor(out, out, neghalf.to_broadcast([P, n]), ALU.pow).then_inc(S[signal], 1)

                    def norm(L):
                        for t in range(NT):
                            pool.wait_ge(S["ln_mv"], NT * L + t + 1)
                            if L:
                                pool.wait_ge(S["ln_xn"], NT * (L - 1) + t + 1)
                            power(rstd[:, t:t + 1], mv[:, t, 1:2], 1, "ln_rstd")

                    def bias(L, name):
                        pool.wait_ge(S["ln_xn"], NT * (L + 1))
                        G.tensor_tensor(X, x_first if L == 0 else X, row(name).unsqueeze(1).to_broadcast([P, NT, D]), ALU.add).then_inc(S["x_biased"], 1)

                    def mlp(m):
                        for i in range(MT):
                            pool.wait_ge(S["mlp_whi"], MT * m + i + 1)
                            G.tensor_tensor(wd_lo[:, i, :], w2[:, i, :], wd_hi[:, i, :].bitcast(f32), ALU.subtract).then_inc(S["mlp_wlo"], 1)

                    def attention(a, add):
                        if a == 2:
                            pool.wait_ge(S["x_updated"], 8 * NT)
                        pool.wait_ge(S["qk_T"], 4 * a + (3 if a == 0 else 2))
                        for h in range(HG):
                            G.tensor_scalar(kbd[:, 1, h, :], kT[:, 1, :], hmask[:, h:h + 1], 1.0, ALU.mult, ALU.mult).then_inc(S["kbd_pool"], 1)
                        U = KT * NT
                        for s in range(U + 1):
                            if s < U:
                                n = U * a + s
                                pool.wait_ge(S["att_scaled"], n + 1)
                                G.tensor_tensor(T[:, n % TR], T[:, n % TR], add(s % NT).unsqueeze(1).to_broadcast([P, HG, SEQ]), ALU.add)\
                                    .then_inc(S["att_masked"], 1)
                            if s >= 1:
                                n = U * a + s - 1
                                pool.wait_ge(S["att_max"], n + 1)
                                G.tensor_tensor(T[:, n % TR], T[:, n % TR], nmax[:, n % TR, :].unsqueeze(2).to_broadcast([P, HG, SEQ]), ALU.add)\
                                    .then_inc(S["att_sub"], 1)

                    pool.wait_ge(s_small, SMALL)
                    pool.wait_ge(s_once, ONCE)
                    norm(0)
                    bias(0, "L0_b_ao")
                    pool.wait_ge(s_chunk0, CHUNK0)
                    G.tensor_scalar(a_self, m_self, 10000.0, -10000.0, ALU.mult, ALU.add).then_inc(S["masks_ready"], 1)
                    G.tensor_scalar(a_cross, m_cross, 10000.0, -10000.0, ALU.mult, ALU.add).then_inc(S["masks_ready"], 1)
                    settle(G.tensor_copy(m_key, m_key8))
                    G.tensor_scalar(a_key, m_key, -1.0, NEG_BIG, ALU.add, ALU.mult).then_inc(S["masks_ready"], 1)
                    pool.wait_ge(S["masks_ready"], 3)
                    attention(0, lambda t: a_self)
                    norm(1)
                    bias(1, "L0_b_co")
                    attention(1, lambda t: a_cross[:, t, :])
                    norm(2)
                    bias(2, "L0_b2")
                    mlp(0)
                    norm(3)

                    def shift(L, state_row, signal):
                        for half in range(2):
                            toks, seqs = slice(half * TOK // 2, (half + 1) * TOK // 2), slice(half * NB // 2, (half + 1) * NB // 2)
                            for c in range(1, KT):
                                pool.wait_ge(S["ln_hT"], 2 * KT * L + KT * half + c + 1)
                                h = hT[:, c, toks].rearrange("p (b s) -> p b s", s=SEQ)
                                o = sxT[:, c, toks].rearrange("p (b s) -> p b s", s=SEQ)
                                st = ctxT[:, c, :].rearrange("p (b s) -> p b s", s=SEQ)[:, seqs, state_row:state_row + 1]
                                G.tensor_tensor(o[:, :, 1:SEQ], h[:, :, 0:SEQ - 1], h[:, :, 1:SEQ], ALU.subtract).then_inc(S[signal], 1)
                                G.tensor_tensor(o[:, :, 0:1], st, h[:, :, 0:1], ALU.subtract).then_inc(S[signal], 1)

                    pool.wait_ge(S["ctxT_ready"], KT)
                    pool.wait_ge(S["x_updated"], 3 * NT)
                    G.memset(wdec.rearrange("p k (b s) -> p (k b) s", s=SLOT)[:, :, 0:1], 0.0).then_inc(S["slots_zero"], 1)
                    shift(3, 1, "l1_sx")
                    for i in range(5):
                        for c in range(KT):
                            pool.wait_ge(S["l1_y"], KT * i + c + 1)
                            G.tensor_tensor(xm[:, i % 2, c, :], xm[:, i % 2, c, :], hT[:, c, :], ALU.add).then_inc(S["l1_xm"], 1)
                    for k in range(KT):
                        pool.wait_ge(S["ctx_hi"], k + 1)
                        G.tensor_tensor(ctx_lo[:, k, :], ctxT[:, k, :], ctx_hi[:, k, :].bitcast(f32), ALU.subtract).then_inc(S["ctx_lo"], 1)
                    for m in range(KT * S8):
                            pool.wait_ge(S["l1_state"], m + 1)
                            if m == 0:
                                pool.wait_ge(S["l1_rkvg"], 3 * KT)
                            if m >= 3:
                                pool.wait_ge(S["l1_rs_used"], m - 2)
                            G.tensor_tensor(rsZ[:, m % 3, :].rearrange("p (b s) -> p b s", s=SEQ),
                                            stS[:, m % 3, :].rearrange("p (b s) -> p b s", s=SLOT)[:, :, 0:SEQ],
                                            qT[:, m // S8, :].rearrange("p (b s) -> p b s", s=SEQ), ALU.mult).then_inc(S["l1_rs"], 1)

                    def weights_lo(n):
                        pool.wait_ge(S["l2_whi"], n + 1)
                        G.tensor_tensor(w2_lo[:, n % 2, :], w2ring[:, n % 3, 0:2 * KT * P], w2_hi[:, n % 2, :].bitcast(f32),
                                        ALU.subtract).then_inc(S["l2_wlo"], 1)

                    weights_lo(0)
                    weights_lo(1)
                    norm(4)
                    shift(4, 0, "l1_sx2")
                    def cross2(z, L, bik, out_bias):
                        def out_weights_lo(h):
                            n = H2 * z + h
                            pool.wait_ge(S["l2_wohi"], n + 1)
                            G.tensor_tensor(wo_lo[:, n % 2, :], wo_ring[:, n % WR, :], wo_hi[:, n % 2, :].bitcast(f32),
                                            ALU.subtract).then_inc(S["l2_wolo"], 1)

                        def head(h):
                            n = H2 * z + h
                            pool.wait_ge(S[f"w2_in{n % 3}"], 32 * (n // 3 + 1))
                            if n == 0:
                                pool.wait_ge(S["x_updated"], 5 * NT)
                            if n >= 2:
                                pool.wait_ge(S["l2_v"], n - 1)
                                pool.wait_ge(S["l2_scores"], n - 1)
                            G.tensor_tensor(dbv[:, n % 2, :], b2ring[:, n % 3, 0, :], b2ring[:, n % 3, 1, :], ALU.subtract).then_inc(S["l2_dbv"], 1)
                            G.tensor_copy(k2[:, n % 2, :, SEQ], col(bik, h).to_broadcast([P, NB])).then_inc(S["l2_kb"], 1)

                        norm(L)
                        head(0)
                        bias(L, out_bias)
                        for h in range(H2):
                            if H2 * z + h + 2 < 2 * H2:
                                weights_lo(H2 * z + h + 2)
                            if h + 1 < H2:
                                head(h + 1)
                            n = H2 * z + h
                            pool.wait_ge(S["l2_rden"], n + 1)
                            pool.wait_ge(S["l2_exp"], n + 1)
                            pool.wait_ge(S["l2_wlo"], min(n + 3, 2 * H2))
                            if n >= 2:
                                pool.wait_ge(S["l2_wolo"], H2 * z + max(h - 1, 0))
                            pool.wait_ge(S["l2_kb"], min(n + 2, H2 * (z + 1)))
                            if n >= 2:
                                pool.wait_ge(S["l2_tp"], n - 1)
                            rec = small[SEQ:P, 8 * (n % 2) + 4:8 * (n % 2) + 8]
                            G.tensor_tensor(pbd[SEQ:P, n % 2, :, SEQ:P], E2[SEQ:P, n % 2, :, 0:SEQ],
                                            rec.unsqueeze(2).to_broadcast([SEQ, NT, SEQ]), ALU.mult).then_inc(S["l2_prob_b"], 1)
                            pool.wait_ge(S["l2_prob_b"], n + 1)
                            if h >= 1:
                                out_weights_lo(h - 1)
                        out_weights_lo(H2 - 1)

                    cross2(0, 5, "L2_bik1", "L2_bo1")
                    cross2(1, 6, "L2_bik2", "L2_bo2")
                    norm(7)
                    bias(7, "L2_bf2")
                    mlp(1)
                    norm(8)
                    bias(8, "L3_cb")
                    attention(2, lambda t: a_key[:, t, :])
                    norm(9)
                    bias(9, "L3_pb")
                    mlp(2)

                @block.sync
                def _(sp):
                    sp.dma_start(mlp_w, t_mlp[0]).then_inc(S["mlp_in"], 16)

                    def head_weights(n):
                        if n >= 3:
                            sp.wait_ge(S["l2_wlo"], n - 2)
                            sp.wait_ge(S["l2_v_mm"], n - 2)
                            sp.wait_ge(S["l2_dbv"], n - 2)
                        sp.dma_start(w2ring[:, n % 3, :], t_w2[n]).then_inc(S[f"w2_in{n % 3}"], 16)
                        sp.dma_start(b2ring[:, n % 3].rearrange("p w d -> p (w d)"), t_b2[n].partition_broadcast(P))\
                            .then_inc(S[f"w2_in{n % 3}"], 16)

                    for n in range(3):
                        head_weights(n)
                    sp.wait_ge(S["x_updated"], 3 * NT)
                    sp.dma_start(mlp_w, t_mlp[1]).then_inc(S["mlp_in"], 16)
                    sp.wait_ge(S["x_updated"], 5 * NT)
                    def out_weights(n):
                        if n >= WR:
                            sp.wait_ge(S["l2_wolo"], n - WR + 1)
                        sp.dma_start(wo_ring[:, n % WR, :], t_wo2[n // H2][:, n % H2 * D:(n % H2 + 1) * D]).then_inc(S[f"wo_in{n % WR}"], 16)

                    out_weights(0)
                    for n in range(3, 2 * H2):
                        head_weights(n)
                        out_weights(n - 2)
                    out_weights(2 * H2 - 2)
                    out_weights(2 * H2 - 1)
                    sp.wait_ge(S["x_updated"], 8 * NT)
                    sp.dma_start(mlp_w, t_mlp[2]).then_inc(S["mlp_in"], 16)
                    load_chunk(sp, lambda t: t[1:CHUNKS + 1][chunk], S["next_in"], S["next_in"])
                    sp.wait_ge(S["next_in"], 16 + CHUNK0)
                    for t in range(NT):
                        sp.wait_ge(S["x_updated"], 9 * NT + t + 1)
                        sp.dma_start(t_out[chunk][:, t * D:(t + 1) * D], X[:, t, :]).then_inc(S["out_done"], 16)
                    sp.wait_ge(S["out_done"], 16 * NT)
            nc.gpsimd.sem_clear(range(nums[0], nums[0] + len(nums)))
            nc.all_engine_barrier()


def shape_constants():
    p = np.arange(P)
    sel = np.zeros((P, S8, P), np.float32)
    for j in range(S8):
        sel[:, j, :] = (p[:, None] // S8 == p[None, :] // S8) & (p[:, None] % S8 == j)
    parts = {
        "ident": np.eye(P),
        "sel": sel.reshape(P, -1),
        "headmask": p[:, None] // 16 == np.arange(HG)[None, :],
        "ones2": p[:, None] // SEQ == np.arange(32)[None, :] // 16,
        "heads8": p[:, None] // S8 == np.arange(HL1)[None, :],
        "block8": p[:, None] // S8 == p[None, :] // S8,
    }
    return np.concatenate([parts[n].astype(np.float32) for n, _ in CONSTS], axis=1)


def kernel(**inputs):
    import concourse.bacc as bacc
    from concourse.bass_utils import run_bass_kernel_spmd as run

    def g(name):
        return np.asarray(inputs[name])

    def L(i, name):
        return g(f"L{i}_xattn_{name}")

    def rows_on_partitions(w):
        k = w.shape[0] // P
        return w.reshape(k, P, w.shape[1]).transpose(1, 0, 2).reshape(P, -1)

    def pad_rows(w):
        out = np.zeros((P, w.shape[1]), w.dtype)
        out[:w.shape[0]] = w
        return out

    def tokens(a):
        n = a.shape[-1]
        return a.reshape(CHUNKS, NT, P, n).transpose(0, 2, 1, 3).reshape(CHUNKS, P, NT * n)

    x, enc = g("x"), g("ctx_2048")
    st = enc[:, 2:2 + S8, :].reshape(CHUNKS, NB, KT, P, S8).transpose(0, 3, 2, 1, 4).reshape(CHUNKS, P, -1)
    bqkv, bkv = L(0, "b_qkv"), L(0, "b_kv")
    stack = L(1, "maa_stack").reshape(5, D)
    vec = {
        "L0_ln1_s": L(0, "ln1_s"), "L0_ln1_b": L(0, "ln1_b"), "L0_bq_s": bqkv[:D], "L0_bk_s": bqkv[D:2 * D],
        "L0_ln2_s": L(0, "ln2_s"), "L0_ln2_b": L(0, "ln2_b"), "L0_b_q": L(0, "b_q"), "L0_bk_c": bkv[:D],
        "L0_ln3_s": L(0, "ln3_s"), "L0_ln3_b": L(0, "ln3_b"), "L1_ln1_w": L(1, "ln1_w"), "L1_ln1_b": L(1, "ln1_b"),
        "L1_ln2_w": L(1, "ln2_w"), "L1_ln2_b": L(1, "ln2_b"), "L1_maa_x": L(1, "maa_x"),
        "L1_time_decay": L(1, "time_decay"), "L1_u": L(1, "u"), "L1_gn_w": L(1, "gn_w"), "L1_gn_b": L(1, "gn_b"),
        "L1_fmk": L(1, "ffn_maa_k"), "L1_fmr": L(1, "ffn_maa_r"),
        "L2_ln1_s": L(2, "ln1_scale"), "L2_ln1_b": L(2, "ln1_offset"), "L2_ln2_s": L(2, "ln2_scale"),
        "L2_ln2_b": L(2, "ln2_offset"), "L2_lnm_s": L(2, "ln_mlp_scale"), "L2_lnm_b": L(2, "ln_mlp_offset"),
        "L3_ln1_w": L(3, "ln1_w"), "L3_ln1_b": L(3, "ln1_b"), "L3_q_b": L(3, "q_b"), "L3_k_b": L(3, "k_b"),
        "L3_ln2_w": L(3, "ln2_w"), "L3_ln2_b": L(3, "ln2_b"),
        "L0_b1": L(0, "b1"), "L2_bf1": L(2, "b_fc1"), "L3_fcb": L(3, "fc_b"),
        "L2_bq1": L(2, "bq1"), "L2_bk1": L(2, "bk1"), "L2_bik1": L(2, "bias_k1"), "L2_biv1": L(2, "bias_v1"),
        "L2_bq2": L(2, "bq2"), "L2_bk2": L(2, "bk2"), "L2_bik2": L(2, "bias_k2"), "L2_biv2": L(2, "bias_v2"),
        "L0_bv_s": bqkv[2 * D:], "L0_b_ao": L(0, "b_ao"), "L0_bv_c": bkv[D:], "L0_b_co": L(0, "b_co"), "L0_b2": L(0, "b2"),
        "L2_bo1": L(2, "bo1"), "L2_bo2": L(2, "bo2"), "L2_bf2": L(2, "b_fc2"),
        "L3_v_b": L(3, "v_b"), "L3_cb": L(3, "cproj_b"), "L3_pb": L(3, "proj_b"),
    }
    for i in range(5):
        vec[f"L1_st{i}"] = stack[i]
    cols = np.concatenate([vec[n].reshape(-1, P).T for n in COL2 + COL8 + COL16], axis=1)
    rows = np.concatenate([vec[n].reshape(-1) for n in ROWS])
    m2 = L(1, "maa_w2")
    wres = {
        "L0_qkv": rows_on_partitions(L(0, "w_qkv")), "L0_ao": rows_on_partitions(L(0, "w_ao")),
        "L0_q": rows_on_partitions(L(0, "w_q")), "L0_kv": rows_on_partitions(L(0, "w_kv")),
        "L0_co": rows_on_partitions(L(0, "w_co")),
        "L1_m1": rows_on_partitions(L(1, "maa_w1")), "L1_m2a": m2[:4].reshape(P, D), "L1_m2b": pad_rows(m2[4]),
        "L1_td1": rows_on_partitions(L(1, "td_w1")), "L1_td2": pad_rows(L(1, "td_w2")),
        "L1_W": np.concatenate([rows_on_partitions(L(1, n).T) for n in ("Wr", "Wk", "Wv", "Wg", "Wo", "Wfk", "Wfr", "Wfv")], axis=1),
        "L3_qkv": np.concatenate([rows_on_partitions(L(3, n)) for n in ("q_w", "k_w", "v_w")], axis=1),
        "L3_c": rows_on_partitions(L(3, "cproj_w")),
    }
    wres = np.concatenate([wres[n] for n, _ in WRES], axis=1)
    mlp = np.stack([np.concatenate([rows_on_partitions(a), rows_on_partitions(b)], axis=1) for a, b in
                    ((L(0, "w1"), L(0, "w2")), (L(2, "w_fc1"), L(2, "w_fc2")), (L(3, "fc_w"), L(3, "proj_w")))])
    w2, b2, wo2 = [], [], []
    for z in (1, 2):
        w = np.stack([L(2, f"w{n}{z}").reshape(KT, P, H2, P) for n in "qkv"])
        w2.append(w.transpose(3, 2, 0, 1, 4).reshape(H2, P, -1))
        b2.append(np.stack([L(2, f"bv{z}").reshape(H2, P), L(2, f"bias_v{z}").reshape(H2, P)], axis=1).reshape(H2, 2 * P))
        wo2.append(L(2, f"wo{z}").reshape(H2, P, D).transpose(1, 0, 2).reshape(P, -1))
    arrays = {
        "x_in": tokens(x), "ctx_in": tokens(enc), "state": st,
        "ltor": g("mask_1x1xSxS2_fc1").reshape(SEQ, SEQ), "cross": tokens(g("mask_Bx1xSxS2_ff1").reshape(NSEQ, SEQ, SEQ)),
        "bmask": g("mask_BxS2_bf1").view(np.uint8).reshape(CHUNKS, NT, 2, SEQ).transpose(0, 2, 1, 3).reshape(CHUNKS, 2, NT * SEQ),
        "cols": cols, "rows": rows, "consts": shape_constants(), "wres": wres, "mlp": mlp,
        "w2": np.concatenate(w2), "b2": np.concatenate(b2), "wo2": np.stack(wo2),
    }
    for k in ("x_in", "ctx_in", "state", "cross", "bmask"):
        arrays[k] = np.concatenate([arrays[k], arrays[k][:1]])
    arrays = {k: np.ascontiguousarray(v) for k, v in arrays.items()}
    nc = bacc.Bacc("TRN2", target_bir_lowering=False, num_devices=1)
    args = [nc.dram_tensor(f"in_{k}", v.shape, mybir.dt.from_np(v.dtype), kind="ExternalInput").ap() for k, v in arrays.items()]
    out = nc.dram_tensor("out_0", (CHUNKS, P, NT * D), mybir.dt.float32, kind="ExternalOutput").ap()
    build(nc, *args, out)
    r = run(nc, [{f"in_{k}": v for k, v in arrays.items()}], core_ids=[0]).results[0]["out_0"]
    return r.reshape(CHUNKS, P, NT, D).transpose(0, 2, 1, 3).reshape(NSEQ, SEQ, D)
```
